# Optimizing a Trainium2 kernel written in Bass

```python
import numpy as np
import jax
import jax.numpy as jnp

def _softmax(x, axis=-1):
    return jax.nn.softmax(x, axis=axis)

def _gelu(x):
    return jax.nn.gelu(x, approximate=True)

def _silu(x):
    return jax.nn.silu(x)

def _sigmoid(x):
    return jax.nn.sigmoid(x)

def _layernorm(x, axis=-1, eps=1e-05):
    m = jnp.mean(x, axis=axis, keepdims=True)
    v = jnp.var(x, axis=axis, keepdims=True)
    return (x - m) / jnp.sqrt(v + eps)

def _scatter_add(tgt, idx, src, axis=0):
    return tgt.at[idx].add(src)

def _segment_sum(src, seg, n):
    return jax.ops.segment_sum(src, seg, n)
kernel_name = 'mk_lm_tower_d2_tok_ids256_r4_e459e1'

def setup_inputs(seed: int=0):
    np.random.seed(seed)
    _w = jnp.asarray

    def _rec_inputs():
        import jax
        import jax.numpy as jnp
        _rk = jax.random.key(seed)
        x = jax.random.randint(jax.random.fold_in(_rk, 1), (8, 1024), 0, 256, jnp.int32)
        return x
    x = _rec_inputs()

    def _L0_tok_setup():
        import jax, jax.numpy as jnp
        import numpy as np
        VOCAB, D_MODEL, EMBED = (256, 64, 64)
        EPS = 1e-05

        def _layernorm(x, gamma, beta):
            mu = jnp.mean(x, axis=-1, keepdims=True)
            var = jnp.mean(jnp.square(x - mu), axis=-1, keepdims=True)
            return (x - mu) * jax.lax.rsqrt(var + EPS) * gamma + beta
        key = jax.random.key(seed)
        ks = jax.random.split(key, 8)
        tokens = jax.random.randint(ks[0], (64, 512), 0, VOCAB, dtype=jnp.int64 if jax.config.jax_enable_x64 else jnp.int32)
        emb_table = jax.random.normal(ks[1], (VOCAB, EMBED), dtype=jnp.float32)
        emb_table = emb_table.at[0].set(0.0)
        s1 = 1.0 / np.sqrt(EMBED + D_MODEL)
        W1 = jax.random.uniform(ks[2], (D_MODEL, EMBED + D_MODEL), minval=-s1, maxval=s1, dtype=jnp.float32)
        b1 = jax.random.uniform(ks[3], (D_MODEL,), minval=-s1, maxval=s1, dtype=jnp.float32)
        s2 = 1.0 / np.sqrt(D_MODEL)
        W2 = jax.random.uniform(ks[4], (D_MODEL, D_MODEL), minval=-s2, maxval=s2, dtype=jnp.float32)
        b2 = jax.random.uniform(ks[5], (D_MODEL,), minval=-s2, maxval=s2, dtype=jnp.float32)
        gamma = jnp.ones((D_MODEL,), dtype=jnp.float32)
        beta = jnp.zeros((D_MODEL,), dtype=jnp.float32)
        return {'tokens': tokens, 'emb_table': emb_table, 'W1': W1, 'b1': b1, 'W2': W2, 'b2': b2, 'gamma': gamma, 'beta': beta}
    _L0_tok_all = _L0_tok_setup()
    _L0_tok_in = {k: v for k, v in _L0_tok_all.items() if k in ('emb_table', 'W1', 'b1', 'W2', 'b2', 'gamma', 'beta')}
    del _L0_tok_all

    def _L0_attn_setup():
        import jax, jax.numpy as jnp
        import numpy as np
        import math
        D_MODEL = 64
        N_HEAD = 8
        BATCH = 2
        NTOK = 256
        A2LEN = 255

        def _linm(w, x):
            return jnp.einsum('oi,bti->bto', w[:, :-1], x) + w[:, -1]
        key = jax.random.key(seed)
        ks = jax.random.split(key, 5)
        scl = 0.02 / math.sqrt(2 * 9)
        x = jax.random.normal(ks[0], (BATCH, NTOK, D_MODEL), jnp.float32)
        wq = (scl * jax.random.normal(ks[1], (N_HEAD * D_MODEL, D_MODEL + 1), jnp.float32)).at[:, -1].set(0.0)
        wv = (scl * jax.random.normal(ks[2], (N_HEAD * D_MODEL, D_MODEL + 1), jnp.float32)).at[:, -1].set(0.0)
        wk = 0.005 * jnp.ones((N_HEAD, D_MODEL), jnp.float32)
        fanout_w = (scl * jax.random.normal(ks[3], (D_MODEL, D_MODEL + 1), jnp.float32)).at[:, -1].set(0.0)
        a2a = jax.random.permutation(ks[4], NTOK)[:A2LEN].astype(jnp.int32)
        return {'x': x, 'wq': wq, 'wv': wv, 'wk': wk, 'fanout_w': fanout_w, 'a2a': a2a}
    _L0_attn_all = _L0_attn_setup()
    _L0_attn_in = {k: v for k, v in _L0_attn_all.items() if k in ('wq', 'wv', 'wk', 'fanout_w', 'a2a')}
    del _L0_attn_all

    def _L0_ffn_setup():
        import jax, jax.numpy as jnp
        import numpy as np
        B, N, D = (16, 1024, 64)
        NUM_EXPERTS, TOP_K, HEADS = (4, 2, 4)
        N_EDGES = 262144
        LN_EPS = 1e-05

        def _layernorm(x, g, b):
            mu = x.mean(-1, keepdims=True)
            var = ((x - mu) ** 2).mean(-1, keepdims=True)
            return (x - mu) * jax.lax.rsqrt(var + LN_EPS) * g + b

        def _forward(x, edge_index, W_gat, att_src, att_dst, b_gat, ln_gamma, ln_beta, W1, b1, W2, b2):
            Bc, Nc, Dc = x.shape
            M = Bc * Nc
            x_flat = x.reshape(M, Dc)
            h = (x_flat @ W_gat).reshape(M, HEADS, NUM_EXPERTS)
            loops = jnp.arange(M, dtype=edge_index.dtype)
            src = jnp.concatenate([edge_index[0], loops])
            dst = jnp.concatenate([edge_index[1], loops])
            a_src = (h * att_src).sum(-1)
            a_dst = (h * att_dst).sum(-1)
            e = jax.nn.leaky_relu(a_src[src] + a_dst[dst], negative_slope=0.2)
            e_max = jax.ops.segment_max(e, dst, num_segments=M)
            ee = jnp.exp(e - e_max[dst])
            denom = jax.ops.segment_sum(ee, dst, num_segments=M)
            alpha = ee / (denom[dst] + 1e-16)
            msg = h[src] * alpha[:, :, None]
            agg = jax.ops.segment_sum(msg, dst, num_segments=M).reshape(M, HEADS * NUM_EXPERTS) + b_gat
            scores = _layernorm(agg, ln_gamma, ln_beta).reshape(M, HEADS, NUM_EXPERTS).mean(1)
            scores = scores.reshape(Bc, Nc, NUM_EXPERTS)
            topk_s, topk_i = jax.lax.top_k(scores, TOP_K)
            w = jax.nn.softmax(topk_s, axis=-1)
            out = jnp.zeros_like(x)
            for ei in range(NUM_EXPERTS):
                g = jnp.where(topk_i == ei, w, 0.0).sum(-1)
                hh = jax.nn.gelu(x @ W1[ei] + b1[ei], approximate=False)
                out = out + g[..., None] * (hh @ W2[ei] + b2[ei])
            return out
        key = jax.random.key(seed)
        ks = jax.random.split(key, 8)
        s = 0.05
        return {'x': jax.random.normal(ks[0], (B, N, D), jnp.float32), 'W_gat': jax.random.normal(ks[1], (D, HEADS * NUM_EXPERTS), jnp.float32) * s, 'att_src': jax.random.normal(ks[2], (HEADS, NUM_EXPERTS), jnp.float32) * s, 'att_dst': jax.random.normal(ks[3], (HEADS, NUM_EXPERTS), jnp.float32) * s, 'b_gat': jnp.zeros((HEADS * NUM_EXPERTS,), jnp.float32), 'ln_gamma': jnp.ones((HEADS * NUM_EXPERTS,), jnp.float32), 'ln_beta': jnp.zeros((HEADS * NUM_EXPERTS,), jnp.float32), 'W1': jax.random.normal(ks[4], (NUM_EXPERTS, D, 2 * D), jnp.float32) * s, 'b1': jnp.zeros((NUM_EXPERTS, 2 * D), jnp.float32), 'W2': jax.random.normal(ks[5], (NUM_EXPERTS, 2 * D, D), jnp.float32) * s, 'b2': jnp.zeros((NUM_EXPERTS, D), jnp.float32), 'edge_index': jax.random.randint(ks[6], (2, N_EDGES), 0, B * N, jnp.int32)}
    _L0_ffn_all = _L0_ffn_setup()
    _L0_ffn_in = {k: v for k, v in _L0_ffn_all.items() if k in ('W_gat', 'att_src', 'att_dst', 'b_gat', 'ln_gamma', 'ln_beta', 'W1', 'b1', 'W2', 'b2', 'edge_index')}
    del _L0_ffn_all

    def _L1_attn_setup():
        import jax, jax.numpy as jnp
        import numpy as np
        import math
        B, N, D = (4, 1024, 64)
        key = jax.random.key(seed)
        k0, k1, k2, k3 = jax.random.split(key, 4)
        bound = math.sqrt(6.0 / D)
        return {'x': jax.random.normal(k0, (B, N, D), dtype=jnp.float32), 'Wq': jax.random.uniform(k1, (D, D), dtype=jnp.float32, minval=-bound, maxval=bound), 'Wk': jax.random.uniform(k2, (D, D), dtype=jnp.float32, minval=-bound, maxval=bound), 'Wv': jax.random.uniform(k3, (D, D), dtype=jnp.float32, minval=-bound, maxval=bound)}
    _L1_attn_all = _L1_attn_setup()
    _L1_attn_in = {k: v for k, v in _L1_attn_all.items() if k in ('Wq', 'Wk', 'Wv')}
    del _L1_attn_all

    def _L1_ffn_setup():
        import jax, jax.numpy as jnp
        import numpy as np
        NUM_EXPERTS = 8
        TOP_K = 2
        B, S, D = (8, 2048, 64)

        def _moe(tokens, router_w, w1, b1, w2, b2):
            N = tokens.shape[0]
            E = router_w.shape[0]
            logits = tokens.astype(jnp.float32) @ router_w.astype(jnp.float32).T
            probs = jax.nn.softmax(logits, axis=-1)
            rw, re = jax.lax.top_k(probs, TOP_K)
            if TOP_K > 1:
                rw = rw / jnp.maximum(rw.sum(-1, keepdims=True), 1e-12)
            rw = rw.astype(tokens.dtype)
            combine = jnp.zeros((N, E), tokens.dtype).at[jnp.arange(N)[:, None], re].set(rw)
            out = tokens
            for e in range(E):
                h = jax.nn.gelu(tokens @ w1[e] + b1[e], approximate=False)
                y = h @ w2[e] + b2[e]
                out = out + combine[:, e:e + 1] * y
            return out
        key = jax.random.key(seed)
        ks = jax.random.split(key, 4)
        scale = 1.0 / np.sqrt(D).astype(np.float32)
        return {'input_embeddings': jax.random.normal(ks[0], (B, S, D), jnp.float32), 'router_w': jax.random.normal(ks[1], (NUM_EXPERTS, D), jnp.float32) * scale, 'w1': jax.random.normal(ks[2], (NUM_EXPERTS, D, D), jnp.float32) * scale, 'b1': jnp.zeros((NUM_EXPERTS, D), jnp.float32), 'w2': jax.random.normal(ks[3], (NUM_EXPERTS, D, D), jnp.float32) * scale, 'b2': jnp.zeros((NUM_EXPERTS, D), jnp.float32)}
    _L1_ffn_all = _L1_ffn_setup()
    _L1_ffn_in = {k: v for k, v in _L1_ffn_all.items() if k in ('router_w', 'w1', 'b1', 'w2', 'b2')}
    del _L1_ffn_all
    return {'x': x, 'L0_tok_emb_table': _L0_tok_in['emb_table'], 'L0_tok_W1': _L0_tok_in['W1'], 'L0_tok_b1': _L0_tok_in['b1'], 'L0_tok_W2': _L0_tok_in['W2'], 'L0_tok_b2': _L0_tok_in['b2'], 'L0_tok_gamma': _L0_tok_in['gamma'], 'L0_tok_beta': _L0_tok_in['beta'], 'L0_attn_wq': _L0_attn_in['wq'], 'L0_attn_wv': _L0_attn_in['wv'], 'L0_attn_wk': _L0_attn_in['wk'], 'L0_attn_fanout_w': _L0_attn_in['fanout_w'], 'L0_attn_a2a': _L0_attn_in['a2a'], 'L0_ffn_W_gat': _L0_ffn_in['W_gat'], 'L0_ffn_att_src': _L0_ffn_in['att_src'], 'L0_ffn_att_dst': _L0_ffn_in['att_dst'], 'L0_ffn_b_gat': _L0_ffn_in['b_gat'], 'L0_ffn_ln_gamma': _L0_ffn_in['ln_gamma'], 'L0_ffn_ln_beta': _L0_ffn_in['ln_beta'], 'L0_ffn_W1': _L0_ffn_in['W1'], 'L0_ffn_b1': _L0_ffn_in['b1'], 'L0_ffn_W2': _L0_ffn_in['W2'], 'L0_ffn_b2': _L0_ffn_in['b2'], 'L0_ffn_edge_index': _L0_ffn_in['edge_index'], 'L1_attn_Wq': _L1_attn_in['Wq'], 'L1_attn_Wk': _L1_attn_in['Wk'], 'L1_attn_Wv': _L1_attn_in['Wv'], 'L1_ffn_router_w': _L1_ffn_in['router_w'], 'L1_ffn_w1': _L1_ffn_in['w1'], 'L1_ffn_b1': _L1_ffn_in['b1'], 'L1_ffn_w2': _L1_ffn_in['w2'], 'L1_ffn_b2': _L1_ffn_in['b2']}

def reference(x, L0_tok_emb_table, L0_tok_W1, L0_tok_b1, L0_tok_W2, L0_tok_b2, L0_tok_gamma, L0_tok_beta, L0_attn_wq, L0_attn_wv, L0_attn_wk, L0_attn_fanout_w, L0_attn_a2a, L0_ffn_W_gat, L0_ffn_att_src, L0_ffn_att_dst, L0_ffn_b_gat, L0_ffn_ln_gamma, L0_ffn_ln_beta, L0_ffn_W1, L0_ffn_b1, L0_ffn_W2, L0_ffn_b2, L0_ffn_edge_index, L1_attn_Wq, L1_attn_Wk, L1_attn_Wv, L1_ffn_router_w, L1_ffn_w1, L1_ffn_b1, L1_ffn_w2, L1_ffn_b2):
    import jax
    import jax.numpy as jnp

    def _L0_tok_ref(tokens, emb_table, W1, b1, W2, b2, gamma, beta):
        import jax, jax.numpy as jnp
        import numpy as np
        VOCAB, D_MODEL, EMBED = (256, 64, 64)
        EPS = 1e-05

        def _layernorm(x, gamma, beta):
            mu = jnp.mean(x, axis=-1, keepdims=True)
            var = jnp.mean(jnp.square(x - mu), axis=-1, keepdims=True)
            return (x - mu) * jax.lax.rsqrt(var + EPS) * gamma + beta
        emb = emb_table[tokens]
        W1_emb = W1[:, :EMBED]
        h = jax.nn.relu(jnp.einsum('bue,de->bud', emb, W1_emb) + b1)
        out = jnp.einsum('bud,od->buo', h, W2) + b2
        return _layernorm(out, gamma, beta)

    def _L0_attn_ref(x, wq, wv, wk, fanout_w, a2a):
        import jax, jax.numpy as jnp
        import numpy as np
        import math
        D_MODEL = 64
        N_HEAD = 8
        BATCH = 2
        NTOK = 256
        A2LEN = 255

        def _linm(w, x):
            return jnp.einsum('oi,bti->bto', w[:, :-1], x) + w[:, -1]
        b, ntok, d = x.shape
        h = N_HEAD
        q = _linm(wq, x).reshape(b, ntok, h, d)
        v = _linm(wv, x).reshape(b, ntok, h, d)
        k = x[:, :, None, :] * wk[None, None, :, :]
        a2len = A2LEN
        qg, kg, vg = (q[:, a2a], k[:, a2a], v[:, a2a])
        padded = (a2len + 15) // 16 * 16
        padn = padded - a2len
        qq = jnp.pad(qg, ((0, 0), (0, padn), (0, 0), (0, 0)))
        kk = jnp.pad(kg, ((0, 0), (0, padn), (0, 0), (0, 0)))
        scale = 1.0 / math.sqrt(d)
        attn = -scale * jnp.sum(jnp.abs(qq[:, None, :, :, :] - kk[:, :, None, :, :]), axis=-1)
        a = attn[:, :a2len + 1, :a2len, :]
        a = a.at[:, a2len, :, :].set(0.0)
        a = jax.nn.softmax(a, axis=1)
        a = a[:, :a2len]
        bb = jnp.einsum('bsdh,bshw->bdhw', a, vg)
        bout = jnp.zeros((b, ntok, h, d), x.dtype).at[:, a2a].set(bb)
        bsum = jnp.sum(bout, axis=2)
        y = bsum * jax.nn.sigmoid(1.702 * bsum)
        y = _linm(fanout_w, y)
        return x + y

    def _L0_ffn_ref(x, W_gat, att_src, att_dst, b_gat, ln_gamma, ln_beta, W1, b1, W2, b2, edge_index):
        import jax, jax.numpy as jnp
        import numpy as np
        B, N, D = (16, 1024, 64)
        NUM_EXPERTS, TOP_K, HEADS = (4, 2, 4)
        N_EDGES = 262144
        LN_EPS = 1e-05

        def _layernorm(x, g, b):
            mu = x.mean(-1, keepdims=True)
            var = ((x - mu) ** 2).mean(-1, keepdims=True)
            return (x - mu) * jax.lax.rsqrt(var + LN_EPS) * g + b

        def _forward(x, edge_index, W_gat, att_src, att_dst, b_gat, ln_gamma, ln_beta, W1, b1, W2, b2):
            Bc, Nc, Dc = x.shape
            M = Bc * Nc
            x_flat = x.reshape(M, Dc)
            h = (x_flat @ W_gat).reshape(M, HEADS, NUM_EXPERTS)
            loops = jnp.arange(M, dtype=edge_index.dtype)
            src = jnp.concatenate([edge_index[0], loops])
            dst = jnp.concatenate([edge_index[1], loops])
            a_src = (h * att_src).sum(-1)
            a_dst = (h * att_dst).sum(-1)
            e = jax.nn.leaky_relu(a_src[src] + a_dst[dst], negative_slope=0.2)
            e_max = jax.ops.segment_max(e, dst, num_segments=M)
            ee = jnp.exp(e - e_max[dst])
            denom = jax.ops.segment_sum(ee, dst, num_segments=M)
            alpha = ee / (denom[dst] + 1e-16)
            msg = h[src] * alpha[:, :, None]
            agg = jax.ops.segment_sum(msg, dst, num_segments=M).reshape(M, HEADS * NUM_EXPERTS) + b_gat
            scores = _layernorm(agg, ln_gamma, ln_beta).reshape(M, HEADS, NUM_EXPERTS).mean(1)
            scores = scores.reshape(Bc, Nc, NUM_EXPERTS)
            topk_s, topk_i = jax.lax.top_k(scores, TOP_K)
            w = jax.nn.softmax(topk_s, axis=-1)
            out = jnp.zeros_like(x)
            for ei in range(NUM_EXPERTS):
                g = jnp.where(topk_i == ei, w, 0.0).sum(-1)
                hh = jax.nn.gelu(x @ W1[ei] + b1[ei], approximate=False)
                out = out + g[..., None] * (hh @ W2[ei] + b2[ei])
            return out
        return _forward(x, edge_index, W_gat, att_src, att_dst, b_gat, ln_gamma, ln_beta, W1, b1, W2, b2)

    def _L1_attn_ref(x, Wq, Wk, Wv):
        import jax, jax.numpy as jnp
        import numpy as np
        import math
        B, N, D = (4, 1024, 64)
        q = x @ Wq.T
        k = x @ Wk.T
        v = x @ Wv.T
        n = x.shape[1]
        d_k = x.shape[2]
        mask = jnp.triu(jnp.ones((n, n), dtype=x.dtype), k=1)
        scale = jnp.asarray(1.0 / math.sqrt(d_k), dtype=x.dtype)
        s = (jnp.einsum('bnd,bmd->bnm', q, k) - (1.0 - mask) * 10000000000.0) * scale
        s = jax.nn.softmax(s, axis=1)
        return jnp.einsum('bnm,bmd->bnd', s, v)

    def _L1_ffn_ref(input_embeddings, router_w, w1, b1, w2, b2):
        import jax, jax.numpy as jnp
        import numpy as np
        NUM_EXPERTS = 8
        TOP_K = 2
        B, S, D = (8, 2048, 64)

        def _moe(tokens, router_w, w1, b1, w2, b2):
            N = tokens.shape[0]
            E = router_w.shape[0]
            logits = tokens.astype(jnp.float32) @ router_w.astype(jnp.float32).T
            probs = jax.nn.softmax(logits, axis=-1)
            rw, re = jax.lax.top_k(probs, TOP_K)
            if TOP_K > 1:
                rw = rw / jnp.maximum(rw.sum(-1, keepdims=True), 1e-12)
            rw = rw.astype(tokens.dtype)
            combine = jnp.zeros((N, E), tokens.dtype).at[jnp.arange(N)[:, None], re].set(rw)
            out = tokens
            for e in range(E):
                h = jax.nn.gelu(tokens @ w1[e] + b1[e], approximate=False)
                y = h @ w2[e] + b2[e]
                out = out + combine[:, e:e + 1] * y
            return out
        b, s, d = input_embeddings.shape
        tokens = input_embeddings.reshape(b * s, d)
        return _moe(tokens, router_w, w1, b1, w2, b2).reshape(b, s, d)
    h = _L0_tok_ref(x, L0_tok_emb_table, L0_tok_W1, L0_tok_b1, L0_tok_W2, L0_tok_b2, L0_tok_gamma, L0_tok_beta)
    h = h + _L0_attn_ref(_layernorm(h, axis=-1), L0_attn_wq, L0_attn_wv, L0_attn_wk, L0_attn_fanout_w, L0_attn_a2a)
    h = h + _L0_ffn_ref(_layernorm(h, axis=-1), L0_ffn_W_gat, L0_ffn_att_src, L0_ffn_att_dst, L0_ffn_b_gat, L0_ffn_ln_gamma, L0_ffn_ln_beta, L0_ffn_W1, L0_ffn_b1, L0_ffn_W2, L0_ffn_b2, L0_ffn_edge_index)
    h = h + _L1_attn_ref(_layernorm(h, axis=-1), L1_attn_Wq, L1_attn_Wk, L1_attn_Wv)
    h = h + _L1_ffn_ref(_layernorm(h, axis=-1), L1_ffn_router_w, L1_ffn_w1, L1_ffn_b1, L1_ffn_w2, L1_ffn_b2)
    return h

_drawn_inputs = setup_inputs


def setup_inputs(seed=0):
    import zlib

    import numpy as np

    out = dict(_drawn_inputs(seed))
    spreads = {'L0_tok_gamma': (1.0, 0.2),
     'L0_tok_beta': (0.0, 0.1),
     'L0_attn_wk': (0.004999999888241291, 0.6),
     'L0_ffn_b_gat': (0.0, 0.341),
     'L0_ffn_ln_gamma': (1.0, 0.6),
     'L0_ffn_ln_beta': (0.0, 0.57),
     'L0_ffn_b1': (0.0, 0.54),
     'L0_ffn_b2': (0.0, 0.1),
     'L1_ffn_b1': (0.0, 0.639),
     'L1_ffn_b2': (0.0, 0.401)}
    factors = {'L0_attn_wq': 200.0,
     'L0_attn_wv': 64.0,
     'L0_attn_fanout_w': 23.63,
     'L0_ffn_W_gat': 3.334,
     'L0_ffn_att_src': 8.0,
     'L0_ffn_att_dst': 200.0}
    for name, (base, spread) in spreads.items():
        noise = np.random.default_rng([zlib.crc32(name.encode()), seed]).standard_normal(out[name].shape)
        drawn = base * np.exp(spread * noise) if base else spread * noise
        out[name] = jnp.asarray(drawn.astype(out[name].dtype))
    for name, factor in factors.items():
        out[name] = (out[name] * factor).astype(out[name].dtype)
    return out
```

```python
import concourse.bass as bass
from concourse import mybir
from concourse.alu_op_type import AluOpType as ALU
from contextlib import ExitStack

F32 = mybir.dt.float32
BF16 = mybir.dt.bfloat16
I32 = mybir.dt.int32
ACT = mybir.ActivationFunctionType
AX = mybir.AxisListType

P = 128
BATCH, SEQ, D = 8, 1024, 64
NODES = BATCH * SEQ
TILES = NODES // P
EDGES = 262144
COLS = EDGES // P
GC = 8
GROUPS = COLS // GC
SLOTS = EDGES + NODES
SCOLS = SLOTS // P
DROPPED = 1 << 20


class Stage(ExitStack):

    def __init__(self, nc, c):
        super().__init__()
        self.nc = nc
        c.stages += 1
        self.tag = f"s{c.stages}_"
        self.used, self.whole = c.used, c.whole

    def sb(self, name, shape, dt=F32):
        return self.enter_context(self.nc.sbuf_tensor(self.tag + name, shape, dt))

    def ps(self, name, shape, dt=F32):
        return self.enter_context(self.nc.psum_tensor(self.tag + name, shape, dt))

    def sem(self, name):
        s = self.enter_context(self.nc.semaphore(self.tag + name))
        self.used.append(s)
        return s

    def pool_sem(self, name):
        return self.whole.enter_context(self.nc.semaphore(self.tag + name))


def clear_semaphores(nc, c):
    with nc.Block() as block:

        @block.sync
        def _(sp):
            for s in c.used:
                sp.sem_clear(s)
            c.used.clear()


class Done:

    def __init__(self, sem, base=0):
        self.sem, self.base, self.n = sem, base, 0

    def add(self, instruction, by=1):
        instruction.then_inc(self.sem, by)
        self.n += by
        return self.base + self.n

    def wait(self, engine):
        engine.wait_ge(self.sem, self.base + self.n)


def make_constants(nc, c):
    with Stage(nc, c) as ctx, nc.Block() as block:
        const_step = ctx.sem("const_step")

        @block.gpsimd
        def _(pool):
            done = Done(const_step)
            nc.gpsimd.memset(c.ident[:, :], 0.0)
            nc.gpsimd.memset(c.upper[:, :], 1.0)
            nc.gpsimd.memset(c.zeros[:, :], 0.0)
            nc.gpsimd.memset(c.ones[:, :], 1.0)
            nc.gpsimd.iota(c.iota_i[:, :], [[1, P]], base=0, channel_multiplier=0)
            done.add(nc.gpsimd.iota(c.part_i[:, :], [[P, 2]], base=0, channel_multiplier=1))
            done.wait(pool)
            nc.gpsimd.affine_select(out=c.ident[:, :], in_=c.ident[:, :], compare_op=ALU.not_equal, fill=1.0,
                                    base=0, pattern=[[-1, P]], channel_multiplier=1)
            done.add(nc.gpsimd.affine_select(out=c.upper[:, :], in_=c.upper[:, :], compare_op=ALU.is_gt, fill=0.0,
                                             base=0, pattern=[[1, P]], channel_multiplier=-1))

        @block.vector
        def _(dve):
            dve.wait_ge(const_step, 2)
            nc.vector.tensor_copy(c.ident_b[:, :], c.ident[:, :])
            nc.vector.tensor_copy(c.upper_b[:, :], c.upper[:, :])
            nc.vector.tensor_copy(c.iota_b[:, :], c.iota_i[:, :])
            nc.vector.tensor_copy(c.part_f[:, :], c.part_i[:, :])


def sort_edges(nc, c, edge_index, sorted_src, start_rows, start_i, end_i):
    with Stage(nc, c) as ctx:
        sb = ctx.sb
        ps = ctx.ps
        sem = ctx.sem

        dst = sb("dst", [P, COLS], I32)
        src = sb("src", [P, COLS], I32)
        key_i = sb("key_i", [P, COLS], I32)
        row_key = sb("row_key", [P, COLS + GC], BF16)
        col_key = sb("col_key", [P, COLS + GC], BF16)
        dropped = sb("dropped", [P, COLS], F32)
        row_hot = sb("row_hot", [P, 2, GC, P], BF16)
        col_hot = sb("col_hot", [P, 2, GC, TILES], BF16)
        row_hot_t = sb("row_hot_t", [P, 2, GC, P], F32)
        before = sb("before", [P, 2, GC, P], BF16)
        next_slot = sb("next_slot", [P, 2, GC, TILES], F32)
        picked = sb("picked", [P, GC, TILES], F32)
        slot_f = sb("slot_f", [P, GC], F32)
        slot_i = sb("slot_i", [P, 2, GC], I32)
        src_out = sb("src_out", [P, 2, GC], I32)
        counts = sb("counts", [P, TILES], F32)
        cum = sb("cum", [P, TILES], F32)
        first = sb("first", [P, TILES], F32)
        first1 = sb("first1", [P, TILES], F32)
        own = sb("own", [P, TILES], I32)
        zero_fill = sb("zero_fill", [P, 5 * SCOLS // 4], F32)

        loaded, filled = sem("loaded"), sem("filled")
        step, hot_ready, hot_free = sem("step"), sem("hot_ready"), sem("hot_free")

        count_psum = Stage(nc, c)
        count_ps, row_ps = count_psum.ps("count_ps", [P, TILES]), count_psum.ps("row_ps", [P, 1])
        counted, summed, prefixed = sem("counted"), sem("summed"), sem("prefixed")

        def build_hot(dve, half, col, build_row=True):
            r = row_key[:, bass.ds(col, GC)].unsqueeze(2).to_broadcast([P, GC, P])
            k = col_key[:, bass.ds(col, GC)].unsqueeze(2).to_broadcast([P, GC, TILES])
            nc.vector.tensor_tensor(row_hot[:, half], r, c.iota_b[:, :].unsqueeze(1).to_broadcast([P, GC, P]), ALU.is_equal)
            nc.vector.tensor_tensor(col_hot[:, half], k, c.iota_b[:, 0:TILES].unsqueeze(1).to_broadcast([P, GC, TILES]),
                                    ALU.is_equal).then_inc(hot_ready, 1)

        with count_psum, nc.Block() as block:

            @block.sync
            def _(sp):
                sp.dma_start(dst[:, :], edge_index[1].rearrange("(p c) -> p c", p=P)).then_inc(loaded, 16)
                sp.dma_start(src[:, :], edge_index[0].rearrange("(p c) -> p c", p=P)).then_inc(loaded, 16)
                sp.wait_ge(filled, 1)
                sp.dma_start(sorted_src.rearrange("(p c) o -> p (c o)", p=P), zero_fill[:, 0:SCOLS].bitcast(I32)).then_inc(filled, 16)
                for q in range(4):
                    n = 5 * SCOLS // 4
                    sp.dma_start(start_rows.rearrange("(p c) o -> p (c o)", p=P)[:, q * n:(q + 1) * n],
                                 zero_fill[:, 0:n]).then_inc(filled, 16)
                sp.wait_ge(filled, 1 + 16 * 5)

            @block.gpsimd
            def _(pool):
                nc.gpsimd.memset(zero_fill[:, :], 0.0).then_inc(filled, 1)
                nc.gpsimd.iota(own[:, :], [[1, TILES]], base=0, channel_multiplier=TILES)

            @block.vector
            def _(dve):
                done = Done(step)
                dve.wait_ge(loaded, 32)
                done.add(nc.vector.tensor_scalar(key_i[:, :], dst[:, :], 6, None, ALU.logical_shift_right))
                done.wait(dve)
                done.add(nc.vector.tensor_scalar(row_key[:, 0:COLS], key_i[:, :], 255.0, None, ALU.min))
                nc.vector.tensor_scalar(dropped[:, :], key_i[:, :], float(P), float(DROPPED), ALU.is_ge, ALU.mult)
                done.add(nc.vector.tensor_scalar(src[:, :], src[:, :], float(NODES - 1), None, ALU.min))
                done.add(nc.vector.tensor_scalar(dst[:, :], dst[:, :], TILES - 1, None, ALU.bitwise_and))
                nc.vector.memset(row_key[:, COLS:COLS + GC], 255.0)
                nc.vector.memset(col_key[:, COLS:COLS + GC], 0.0)
                done.wait(dve)
                done.add(nc.vector.tensor_copy(col_key[:, 0:COLS], dst[:, :]))
                done.wait(dve)
                with dve.Fori(0, GROUPS // 2) as i:
                    for half in range(2):
                        dve.wait_ge(hot_free, 2 * i + (half + 1))
                        build_hot(dve, half, i * (2 * GC) + half * GC)
                dve.wait_ge(counted, 1)
                done.add(nc.vector.tensor_copy(counts[:, :], count_ps[:, :]))
                done.wait(dve)
                done.add(nc.vector.tensor_scalar_add(first[:, :], counts[:, :], 1.0))
                done.wait(dve)
                nc.vector.tensor_tensor_scan(cum[:, :], c.zeros[:, 0:TILES], first[:, :], 0.0, ALU.add, ALU.add).then_inc(summed, 1)
                dve.wait_ge(prefixed, 1)
                dve.wait_ge(summed, 1)
                done.add(nc.vector.tensor_tensor(first[:, :], cum[:, :], first[:, :], ALU.subtract))
                done.wait(dve)
                done.add(nc.vector.tensor_scalar(first[:, :], first[:, :], row_ps[:, 0:1], None, ALU.add))
                done.wait(dve)
                nc.vector.tensor_copy(start_i[:, :], first[:, :])
                nc.vector.tensor_scalar_add(first1[:, :], first[:, :], 1.0)
                nc.vector.tensor_tensor(end_i[:, :], first[:, :], counts[:, :], ALU.add)

            @block.tensor
            def _(pe):
                pe.sem_inc(hot_free, 2)
                nc.tensor.matmul(count_ps[:, :], c.zeros[:, 0:P], c.zeros[:, 0:TILES], start=True, stop=True)
                with pe.Fori(0, GROUPS // 2) as i:
                    for half in range(2):
                        pe.wait_ge(hot_ready, 2 * i + (half + 1))
                        for k in range(GC):
                            last = nc.tensor.matmul(count_ps[:, :], row_hot[:, half, k], col_hot[:, half, k],
                                                    start=False, stop=True, skip_group_check=True)
                        last.then_inc(hot_free, 1)
                nc.tensor.matmul(count_ps[:, :], c.zeros[:, 0:P], c.zeros[:, 0:TILES], start=False, stop=True,
                                 skip_group_check=True).then_inc(counted, 1)
                pe.wait_ge(summed, 1)
                nc.tensor.matmul(row_ps[:, :], c.upper[:, :], cum[:, TILES - 1:TILES], start=True, stop=True).then_inc(prefixed, 1)

        hot_ready2, chunk_free = sem("hot_ready2"), sem("chunk_free")
        turned, turned_sb, same_ps_ready, before_ready = sem("turned"), sem("turned_sb"), sem("same_ready"), sem("before_ready")
        counted2, snapped, slots_ps_ready = sem("counted2"), sem("snapped"), sem("slots_ready")
        picked_step, issue_ready, issue_free = sem("picked_step"), sem("issue_ready"), [ctx.pool_sem("issue_free0"), ctx.pool_sem("issue_free1")]
        pool_wait = sem("pool_wait")
        OWN = 16 * TILES // 2
        turn_ps = [ps(f"turn_ps{j}", [P, GC, P], BF16) for j in range(2)]
        same_ps = ps("same_ps", [P, GC, P])
        run_ps = ps("run_ps", [P, TILES])
        slots_ps = [ps(f"slots_ps{j}", [P, GC, TILES]) for j in range(2)]

        with nc.Block() as block:

            @block.vector
            def _(dve):
                def build(half, col):
                    r = row_key[:, bass.ds(col, GC)].unsqueeze(2).to_broadcast([P, GC, P])
                    k = col_key[:, bass.ds(col, GC)].unsqueeze(2).to_broadcast([P, GC, TILES])
                    nc.vector.tensor_tensor(row_hot[:, half], r, c.iota_b[:, :].unsqueeze(1).to_broadcast([P, GC, P]), ALU.is_equal)
                    nc.vector.tensor_tensor(col_hot[:, half], k, c.iota_b[:, 0:TILES].unsqueeze(1).to_broadcast([P, GC, TILES]),
                                            ALU.is_equal).then_inc(hot_ready2, 1)

                build(0, 0)
                with dve.Fori(0, GROUPS // 2) as i:
                    for half in range(2):
                        g1 = 2 * i + (half + 1)
                        dve.wait_ge(same_ps_ready, g1)
                        nc.vector.tensor_tensor(before[:, half], same_ps[:, :, :],
                                                c.upper_b[:, :].unsqueeze(1).to_broadcast([P, GC, P]),
                                                ALU.mult).then_inc(before_ready, 1)
                        build(1 - half, i * (2 * GC) + (half + 1) * GC)
                        dve.wait_ge(slots_ps_ready, g1)
                        done = Done(picked_step, 4 * i + 2 * half)
                        done.add(nc.vector.tensor_tensor(picked[:, :, :], slots_ps[half][:, :, :], col_hot[:, half], ALU.mult))
                        done.wait(dve)
                        done.add(nc.vector.tensor_reduce(slot_f[:, :], picked[:, :, :], AX.X, ALU.add))
                        dve.wait_ge(issue_free[half], i * (16 * GC) + OWN)
                        nc.vector.tensor_copy(src_out[:, half], src[:, bass.ds(i * (2 * GC) + half * GC, GC)])
                        done.wait(dve)
                        nc.vector.tensor_tensor(slot_i[:, half], slot_f[:, :],
                                                dropped[:, bass.ds(i * (2 * GC) + half * GC, GC)],
                                                ALU.add).then_inc(issue_ready, 1)

            @block.tensor
            def _(pe):
                def turn(half, number):
                    pe.wait_ge(hot_ready2, number)
                    for k in range(GC):
                        last = nc.tensor.transpose(turn_ps[half][:, k], row_hot[:, half, k], c.ident_b[:, :])
                    last.then_inc(turned, 1)

                nc.tensor.matmul(run_ps[:, :], c.ident[:, :], first1[:, :], start=True, stop=True).then_inc(counted2, 1)
                turn(0, 1)
                with pe.Fori(0, GROUPS // 2) as i:
                    for half in range(2):
                        g1 = 2 * i + (half + 1)
                        pe.wait_ge(turned_sb, g1)
                        pe.wait_ge(before_ready, g1)
                        for k in range(GC):
                            last = nc.tensor.matmul(same_ps[:, k], row_hot_t[:, half, k], row_hot_t[:, half, k],
                                                    start=True, stop=True)
                        last.then_inc(same_ps_ready, 1)
                        pe.wait_ge(before_ready, g1 + 1)
                        for k in range(GC):
                            pe.wait_ge(snapped, i * (2 * GC) + (half * GC + k + 1))
                            nc.tensor.matmul(run_ps[:, :], row_hot[:, half, k], col_hot[:, half, k],
                                             start=False, stop=True, skip_group_check=True).then_inc(counted2, 1)
                            nc.tensor.matmul(slots_ps[half][:, k], row_hot_t[:, half, k], next_slot[:, half, k],
                                             start=True, stop=False)
                            last = nc.tensor.matmul(slots_ps[half][:, k], before[:, half, k], col_hot[:, half, k],
                                                    start=False, stop=True)
                        last.then_inc(slots_ps_ready, 1)
                        turn(1 - half, g1 + 1)

            @block.scalar
            def _(act):
                act.sem_inc(before_ready, 1)
                with act.Fori(0, GROUPS // 2) as i:
                    for half in range(2):
                        g1 = 2 * i + (half + 1)
                        act.wait_ge(turned, g1)
                        nc.scalar.copy(row_hot_t[:, half], turn_ps[half][:, :, :]).then_inc(turned_sb, 1)
                        for k in range(GC):
                            act.wait_ge(counted2, i * (2 * GC) + (half * GC + k + 1))
                            nc.scalar.copy(next_slot[:, half, k], run_ps[:, :]).then_inc(snapped, 1)

            @block.gpsimd
            def _(pool):
                def send(slots, rows):
                    return nc.gpsimd.indirect_dma_start(
                        sorted_src, bass.IndirectOffsetOnAxis(ap=slots, axis=0), rows, None,
                        bounds_check=SLOTS - 1, oob_is_err=False)

                for t in range(TILES):
                    send(start_i[:, t:t + 1], own[:, t:t + 1]).then_inc(issue_free[t % 2], 16)
                with pool.Fori(0, GROUPS // 2) as i:
                    for half in range(2):
                        pool.wait_ge(issue_ready, 2 * i + (half + 1))
                        pool.sem_inc(pool_wait, 1)
                        for k in range(GC):
                            send(slot_i[:, half, k:k + 1], src_out[:, half, k:k + 1]).then_inc(issue_free[half], 16)
                for half in range(2):
                    pool.wait_ge(issue_free[half], OWN + GROUPS // 2 * 16 * GC)


VOCAB, HEADS0, KEYS = 256, 8, 255
EPS = 1e-5


def load_all(engine, pairs, sem):
    for tile, array in pairs:
        engine.dma_start(tile, array).then_inc(sem, 16)


def on_every_partition(array, n):
    return array.rearrange("(o n) -> o n", o=1).to_broadcast([P, n])


class Norm:

    def __init__(self, nc, ctx, name, T, n):
        self.nc, self.T, self.n = nc, T, n
        self.mean = ctx.sb(name + "_mean", [P, T])
        self.var = ctx.sb(name + "_var", [P, T])
        self.std = ctx.sb(name + "_std", [P, T])
        self.inv = ctx.sb(name + "_inv", [P, T])
        self.var_ready = ctx.sem(name + "_var_ready")
        self.std_ready = ctx.sem(name + "_std_ready")

    def wide(self, stat):
        return stat[:, :].unsqueeze(2).to_broadcast([P, self.T, self.n])

    def centre(self, dve, done, x, centred, square):
        v = self.nc.vector
        done.add(v.tensor_reduce(self.mean[:, :], x, AX.X, ALU.add))
        done.wait(dve)
        done.add(v.tensor_scalar_mul(self.mean[:, :], self.mean[:, :], 1.0 / self.n))
        done.wait(dve)
        done.add(v.tensor_tensor(centred, x, self.wide(self.mean), ALU.subtract))
        done.wait(dve)
        done.add(v.tensor_tensor(square, centred, centred, ALU.mult))
        done.wait(dve)
        done.add(v.tensor_reduce(self.var[:, :], square, AX.X, ALU.add))
        done.wait(dve)
        v.tensor_scalar(self.var[:, :], self.var[:, :], 1.0 / self.n, EPS, ALU.mult, ALU.add).then_inc(self.var_ready, 1)
        dve.wait_ge(self.std_ready, 1)
        done.add(v.reciprocal(self.inv[:, :], self.std[:, :]))
        done.wait(dve)

    def root(self, act):
        act.wait_ge(self.var_ready, 1)
        self.nc.scalar.activation(self.std[:, :], self.var[:, :], ACT.Sqrt).then_inc(self.std_ready, 1)


def token_tables(nc, c, w, tab_h, tab_x, tab_xt):
    with Stage(nc, c) as ctx:
        sb = ctx.sb
        sem = ctx.sem

        emb_t, w1_t, b1 = sb("emb_t", [D, VOCAB]), sb("w1_t", [D, D]), sb("b1", [D, 1])
        w2_t, gamma, beta = sb("w2_t", [D + 1, D]), sb("gamma", [P, D]), sb("beta", [P, D])
        hid = sb("hid", [D + 1, VOCAB])
        centred, square = sb("centred", [P, 2, D]), sb("square", [P, 2, D])
        hid_ps = ctx.ps("hid_ps", [D, VOCAB])
        out_ps = ctx.ps("out_ps", [P, 2, D])
        xt_ps = ctx.ps("xt_ps", [D, VOCAB])
        loaded, hid_done, act_done, out_done, x_done, xt_done, step = map(
            sem, ("loaded", "hid_done", "act_done", "out_done", "x_done", "xt_done", "step"))
        n1, n2 = Norm(nc, ctx, "n1", 2, D), Norm(nc, ctx, "n2", 2, D)
        with nc.Block() as block:

            @block.sync
            def _(sp):
                load_all(sp, [(emb_t[:, :], w["emb_t"]), (w1_t[:, :], w["tok_w1_t"]), (b1[:, :], w["tok_b1"]),
                              (w2_t[:, :], w["tok_w2_t"]), (gamma[:, :], on_every_partition(w["tok_gamma"], D)),
                              (beta[:, :], on_every_partition(w["tok_beta"], D))], loaded)

            @block.tensor
            def _(pe):
                pe.wait_ge(loaded, 16 * 6)
                nc.tensor.matmul(hid_ps[:, :], w1_t[:, :], emb_t[:, :], start=True, stop=True).then_inc(hid_done, 1)
                pe.wait_ge(act_done, 2)
                for j in range(2):
                    last = nc.tensor.matmul(out_ps[:, j], hid[:, j * P:(j + 1) * P], w2_t[:, :], start=True, stop=True)
                last.then_inc(out_done, 1)
                pe.wait_ge(x_done, 1)
                for j in range(2):
                    last = nc.tensor.transpose(xt_ps[:, j * P:(j + 1) * P], tab_x[:, j], c.ident[:, :])
                last.then_inc(xt_done, 1)

            @block.scalar
            def _(act):
                act.wait_ge(loaded, 16 * 6)
                act.wait_ge(hid_done, 1)
                nc.scalar.activation(hid[0:D, :], hid_ps[:, :], ACT.Relu, bias=b1[:, 0:1]).then_inc(act_done, 1)
                n1.root(act)
                n2.root(act)

            @block.vector
            def _(dve):
                done = Done(step)
                nc.vector.memset(tab_xt[D:D + 1, :], 1.0)
                nc.vector.memset(hid[D:D + 1, :], 1.0).then_inc(act_done, 1)
                dve.wait_ge(loaded, 16 * 6)
                dve.wait_ge(out_done, 1)
                n1.centre(dve, done, out_ps[:, :, :], centred[:, :, :], square[:, :, :])
                done.add(nc.vector.tensor_tensor(centred[:, :, :], centred[:, :, :], n1.wide(n1.inv), ALU.mult))
                done.wait(dve)
                done.add(nc.vector.tensor_tensor(centred[:, :, :], centred[:, :, :],
                                                 gamma[:, :].unsqueeze(1).to_broadcast([P, 2, D]), ALU.mult))
                done.wait(dve)
                done.add(nc.vector.tensor_tensor(tab_h[:, :, :], centred[:, :, :],
                                                 beta[:, :].unsqueeze(1).to_broadcast([P, 2, D]), ALU.add))
                done.wait(dve)
                n2.centre(dve, done, tab_h[:, :, :], centred[:, :, :], square[:, :, :])
                nc.vector.tensor_tensor(tab_x[:, :, :], centred[:, :, :], n2.wide(n2.inv), ALU.mult).then_inc(x_done, 1)
                dve.wait_ge(xt_done, 1)
                nc.vector.tensor_copy(tab_xt[0:D, :], xt_ps[:, :])


def word_attention(nc, c, w, tab_h, tab_x, tab_xt, words, chosen, chosen_table, plain_table):
    HALF, BLOCKS, PAIRS = 64, VOCAB // 64, HEADS0 // 2
    with Stage(nc, c) as ctx:
        sb = ctx.sb
        ps = ctx.ps
        sem = ctx.sem

        wq_t, wv_t = sb("wq_t", [D + 1, PAIRS, 2, D]), sb("wv_t", [D + 1, PAIRS, 2, D])
        wk, fan_t, fan_b = sb("wk", [P, PAIRS]), sb("fan_t", [D + 1, D]), sb("fan_b", [P, D])
        query = sb("query", [P, PAIRS, VOCAB])
        key = sb("key", [P, PAIRS, VOCAB])
        value = sb("value", [P, BLOCKS, PAIRS, D])
        count = sb("count", [P, BLOCKS, BATCH])
        match, negkey = sb("match", [P, SEQ]), sb("negkey", [P, SEQ])
        block_word_i, block_word = sb("block_word_i", [P, BLOCKS], I32), sb("block_word", [P, BLOCKS])
        weighed = sb("weighed", [P, BLOCKS, PAIRS, BATCH, D])
        twice = sb("twice", [D, 2, D])
        pick = sb("pick", [P, 3 * HALF - 1])
        minus_half = sb("minus_half", [P, 2, HALF])
        key_sum = sb("key_sum", [P, PAIRS, BLOCKS])
        gap = sb("gap", [P, 8, VOCAB])
        e = sb("e", [P, BLOCKS, PAIRS, VOCAB])
        den, total = sb("den", [P, BATCH]), sb("total", [P, 2, BATCH, D])
        part = sb("part", [P, BATCH, D])
        gate = sb("gate", [P, 2, BATCH, D])
        mixed_t = sb("mixed_t", [D + 1, 2, BATCH, P])
        base = sb("base", [P, 2, D])
        q_ps, k_ps = [ps(f"q_ps{j}", [P, 2, VOCAB]) for j in range(2)], ps("k_ps", [P, VOCAB])
        v_ps = ps("v_ps", [P, PAIRS, D])
        dist_ps = [ps(f"dist_ps{j}", [P, VOCAB]) for j in range(2)]
        num_ps, den_ps = ps("num_ps", [P, BATCH, D]), ps("den_ps", [P, BATCH])
        loaded, consts, picked, q_done, q_read, k_done, v_done, v_read = map(
            sem, ("loaded", "consts", "picked", "q_done", "q_read", "k_done", "v_done", "v_read"))
        keys_ready, gap_v, gap_s, gap_free, dist_read = map(
            sem, ("keys_ready", "gap_v", "gap_s", "gap_free", "dist_read"))
        weighed_ready, num_done, num_read, gate_in, gate_out, turn_in, turn_out, step, astep = map(
            sem, ("weighed_ready", "num_done", "num_read", "gate_in", "gate_out", "turn_in", "turn_out", "step",
                  "astep"))

        with nc.Block() as block:

            @block.sync
            def _(sp):
                load_all(sp, [(wq_t[:, :, :, :], w["wq_t"].rearrange("i (a h o) -> i a h o", a=PAIRS, h=2)),
                              (wv_t[:, :, :, :], w["wv_t"].rearrange("i (a h o) -> i a h o", a=PAIRS, h=2)),
                              (wk[:, :], w["wk_pairs"]), (fan_t[:, :], w["fan_t"]),
                              (fan_b[:, :], w["fan_t"][D:D + 1, :].to_broadcast([P, D]))], loaded)

            @block.gpsimd
            def _(pool):
                nc.gpsimd.memset(pick[:, :], 0.0)
                nc.gpsimd.iota(block_word_i[:, :], [[HALF, BLOCKS]], base=0, channel_multiplier=1).then_inc(consts, 1)

            @block.tensor
            def _(pe):
                pe.wait_ge(loaded, 16 * 5)
                pe.wait_ge(picked, 1)
                for a in range(PAIRS):
                    if a >= 2:
                        pe.wait_ge(q_read, a - 1)
                    nc.tensor.matmul(q_ps[a % 2][:, 0], wq_t[:, a], tab_xt[:, :], start=True, stop=True).then_inc(q_done, 1)
                nc.tensor.matmul(k_ps[:, :], twice[:, :, :], tab_xt[0:D, :], start=True, stop=True).then_inc(k_done, 1)
                for b in range(BLOCKS):
                    if b:
                        pe.wait_ge(v_read, b)
                    for h in range(2):
                        last = nc.tensor.matmul(v_ps[h * HALF:(h + 1) * HALF], tab_xt[:, b * HALF:(b + 1) * HALF],
                                                wv_t[:, :, h], start=True, stop=True)
                    last.then_inc(v_done, 1)
                pe.wait_ge(keys_ready, 1)
                for a in range(PAIRS):
                    for b in range(BLOCKS):
                        for h in range(2):
                            r = slice(h * HALF, (h + 1) * HALF)
                            last = nc.tensor.matmul(k_ps[r, a * BLOCKS + b:a * BLOCKS + b + 1], key[r, a, b * HALF:(b + 1) * HALF],
                                                    c.ones[r, 0:1], start=True, stop=True)
                last.then_inc(k_done, 1)
                pe.sem_inc(gap_free, 8)
                with pe.Fori(0, PAIRS) as a, pe.Fori(0, BLOCKS // 2) as j:
                    i = a * 2 + j
                    for half in range(2):
                        pe.wait_ge(dist_read, 2 * i + (half + 1))
                        nc.tensor.matmul(dist_ps[half][:, :], minus_half[:, :, :], query[:, bass.ds(a, 1)].squeeze(1), start=True, stop=False)
                        for u in range(HALF):
                            if u % 8 < 5:
                                pe.wait_ge(gap_v, i * (2 * 40) + (half * 40 + u // 8 * 5 + u % 8 + 1))
                            else:
                                pe.wait_ge(gap_s, i * (2 * 24) + (half * 24 + u // 8 * 3 + u % 8 - 4))
                            last = nc.tensor.matmul(dist_ps[half][:, :], pick[:, HALF - 1 - u:3 * HALF - 1 - u], gap[:, u % 8],
                                                    start=False, stop=(u == HALF - 1))
                            last.then_inc(gap_free, 1)
                pe.wait_ge(weighed_ready, 1)
                pe.wait_ge(dist_read, 2 + BLOCKS * PAIRS)
                n = 0
                for dh in range(2):
                    for a in range(PAIRS):
                        for h in range(2):
                            if n:
                                pe.wait_ge(num_read, n)
                            r = slice(h * HALF, (h + 1) * HALF)
                            for b in range(BLOCKS):
                                nc.tensor.matmul(num_ps[:, :, :], e[r, b, a, dh * P:(dh + 1) * P], weighed[r, b, a],
                                                 start=(b == 0), stop=(b == BLOCKS - 1))
                            for b in range(BLOCKS):
                                last = nc.tensor.matmul(den_ps[:, :], e[r, b, a, dh * P:(dh + 1) * P], count[r, b],
                                                        start=(b == 0), stop=(b == BLOCKS - 1))
                            last.then_inc(num_done, 1)
                            n += 1
                pe.wait_ge(turn_in, 1)
                for n in range(2 * BATCH // 4):
                    if n >= 2:
                        pe.wait_ge(turn_out, n - 1)
                    for k in range(4):
                        m = 4 * n + k
                        last = nc.tensor.transpose(q_ps[n % 2][0:D, k // 2, (k % 2) * P:(k % 2 + 1) * P], gate[:, m // BATCH, m % BATCH], c.ident[:, :])
                    last.then_inc(q_done, 1)
                pe.wait_ge(turn_out, 2 * BATCH // 4)
                for dh in range(2):
                    pe.wait_ge(num_read, 2 * HEADS0 + dh)
                    for b in range(BATCH):
                        last = nc.tensor.matmul(num_ps[:, b], mixed_t[:, dh, b], fan_t[:, :], start=True, stop=True)
                    last.then_inc(num_done, 1)

            @block.vector
            def _(dve):
                done = Done(step)
                dve.wait_ge(loaded, 16 * 5)
                dve.wait_ge(consts, 1)
                done.add(nc.vector.tensor_copy(block_word[:, :], block_word_i[:, :]))
                nc.vector.memset(mixed_t[D:D + 1, :, :, :], 1.0)
                for h in range(2):
                    nc.vector.memset(minus_half[h * HALF:(h + 1) * HALF, h], -0.5)
                    nc.vector.memset(minus_half[h * HALF:(h + 1) * HALF, 1 - h], 0.0)
                    nc.vector.memset(pick[h * HALF:(h + 1) * HALF, (h + 1) * HALF - 1:(h + 1) * HALF], 1.0)
                    last = nc.vector.tensor_copy(twice[:, h], c.ident[0:D, 0:D])
                last.then_inc(picked, 1)
                done.wait(dve)
                done.add(nc.vector.tensor_scalar_add(block_word[HALF:P, :], block_word[HALF:P, :], float(-HALF)))
                for a in range(PAIRS):
                    dve.wait_ge(q_done, a + 1)
                    nc.vector.tensor_copy(query[:, a], q_ps[a % 2][:, 0]).then_inc(q_read, 1)
                dve.wait_ge(k_done, 1)
                for a in range(PAIRS):
                    last = nc.vector.tensor_scalar(key[:, a], k_ps[:, :], wk[:, a:a + 1], None, ALU.mult)
                last.then_inc(keys_ready, 1)
                for b in range(BLOCKS):
                    dve.wait_ge(v_done, b + 1)
                    nc.vector.tensor_copy(value[:, b], v_ps[:, :, :]).then_inc(v_read, 1)
                dve.wait_ge(keys_ready, 1)
                dve.wait_ge(k_done, 2)
                nc.vector.tensor_scalar_mul(key_sum[:, :, :], k_ps[:, 0:PAIRS * BLOCKS].rearrange("p (a b) -> p a b", a=PAIRS),
                                            -1.0 / D ** 0.5).then_inc(keys_ready, 1)
                with dve.Fori(0, PAIRS) as a, dve.Fori(0, BLOCKS // 2) as j:
                    i = a * 2 + j
                    for half in range(2):
                        for u in range(HALF):
                            if u % 8 < 5:
                                dve.wait_ge(gap_free, i * (2 * HALF) + (half * HALF + u + 1))
                                nc.vector.tensor_scalar(gap[:, u % 8], query[:, bass.ds(a, 1)].squeeze(1),
                                                        key[:, :, :].rearrange("p a u -> p (a u)")[:, bass.ds(i * (2 * HALF) + (half * HALF + u), 1)],
                                                        0.0, ALU.subtract, ALU.max).then_inc(gap_v, 1)
                for b in range(BLOCKS):
                    for s in range(BATCH):
                        done.wait(dve)
                        done.add(nc.vector.scalar_tensor_tensor(
                            match[:, :], words[:, s * SEQ:(s + 1) * SEQ], block_word[:, b:b + 1], chosen[:, :],
                            ALU.is_equal, ALU.mult, accum_out=count[:, b, s:s + 1]))
                done.wait(dve)
                for b in range(BLOCKS):
                    for a in range(PAIRS):
                        last = nc.vector.tensor_tensor(weighed[:, b, a], count[:, b].unsqueeze(2).to_broadcast([P, BATCH, D]),
                                                       value[:, b, a].unsqueeze(1).to_broadcast([P, BATCH, D]), ALU.mult)
                last.then_inc(weighed_ready, 1)
                n = 0
                for dh in range(2):
                    done.add(nc.vector.memset(total[:, dh], 0.0))
                    for a in range(HEADS0):
                        dve.wait_ge(num_done, n + 1)
                        done.add(nc.vector.tensor_scalar_add(den[:, :], den_ps[:, :], 1.0))
                        done.wait(dve)
                        done.add(nc.vector.reciprocal(den[:, :], den[:, :]))
                        done.wait(dve)
                        nc.vector.tensor_tensor(part[:, :, :], num_ps[:, :, :], den[:, :].unsqueeze(2).to_broadcast([P, BATCH, D]),
                                                ALU.mult).then_inc(num_read, 1)
                        dve.wait_ge(num_read, n + 1)
                        done.add(nc.vector.tensor_tensor(total[:, dh], total[:, dh], part[:, :, :], ALU.add))
                        done.wait(dve)
                        n += 1
                nc.vector.sem_inc(gate_in, 1)
                dve.wait_ge(gate_out, 1)
                done.add(nc.vector.tensor_scalar_add(gate[:, :, :, :], gate[:, :, :, :], 1.0))
                done.wait(dve)
                done.add(nc.vector.reciprocal(gate[:, :, :, :], gate[:, :, :, :]))
                done.wait(dve)
                nc.vector.tensor_tensor(gate[:, :, :, :], gate[:, :, :, :], total[:, :, :, :], ALU.mult).then_inc(turn_in, 1)
                for n in range(2 * BATCH // 4):
                    dve.wait_ge(q_done, PAIRS + n + 1)
                    nc.vector.tensor_copy(mixed_t[0:D, n // 2, (n % 2) * 4:(n % 2) * 4 + 4],
                                          q_ps[n % 2][0:D].rearrange("d a (k p) -> d (a k) p", k=2)).then_inc(turn_out, 1)
                done.add(nc.vector.tensor_tensor(base[:, :, :], tab_h[:, :, :], tab_x[:, :, :], ALU.add))
                done.wait(dve)
                nc.vector.tensor_tensor(plain_table[:, :, :], base[:, :, :], fan_b[:, :].unsqueeze(1).to_broadcast([P, 2, D]), ALU.add)
                for dh in range(2):
                    dve.wait_ge(num_done, 2 * HEADS0 + dh + 1)
                    nc.vector.tensor_tensor(chosen_table[:, dh], num_ps[:, :, :], base[:, dh].unsqueeze(1).to_broadcast([P, BATCH, D]),
                                            ALU.add).then_inc(num_read, 1)

            @block.scalar
            def _(act):
                act.wait_ge(keys_ready, 2)
                nc.scalar.mul(negkey[:, :], key[:, :, :].rearrange("p a u -> p (a u)"), -1.0).then_inc(astep, 1)
                act.wait_ge(astep, 1)
                act.sem_inc(dist_read, 2)
                with act.Fori(0, PAIRS) as a, act.Fori(0, BLOCKS // 2) as j:
                    i = a * 2 + j
                    for half in range(2):
                        for u in range(HALF):
                            if u % 8 >= 5:
                                act.wait_ge(gap_free, i * (2 * HALF) + (half * HALF + u + 1))
                                nc.scalar.activation(gap[:, u % 8], query[:, bass.ds(a, 1)].squeeze(1), ACT.Relu,
                                                     bias=negkey[:, bass.ds(i * (2 * HALF) + (half * HALF + u), 1)]).then_inc(gap_s, 1)
                        act.wait_ge(gap_free, i * (2 * HALF) + (8 + (half + 1) * HALF))
                        nc.scalar.activation(e[:, :, :, :].rearrange("p b a v -> p (b a) v")[:, bass.ds(j * (2 * PAIRS) + (a + half * PAIRS), 1)].squeeze(1),
                                             dist_ps[half][:, :], ACT.Exp, scale=-2.0 / D ** 0.5,
                                             bias=key_sum[:, :, :].rearrange("p a b -> p (a b)")[:, bass.ds(2 * i + half, 1)]).then_inc(dist_read, 1)
                act.wait_ge(gate_in, 1)
                nc.scalar.activation(gate[:, :, :, :], total[:, :, :, :], ACT.Exp, scale=-1.702).then_inc(gate_out, 1)


def load_words(nc, c, w, words, chosen):
    with Stage(nc, c) as ctx:
        sb = ctx.sb

        words_i = sb("words_i", [P, NODES], I32)
        named_i, named = sb("named_i", [P, 2], I32), sb("named", [P, 2])
        place_i, place = sb("place_i", [P, SEQ], I32), sb("place", [P, SEQ])
        names = sb("names", [P, 2, SEQ], BF16)
        ones_b = sb("ones_b", [P, P], BF16)
        count_ps = ctx.ps("named_ps", [P, 2, SEQ // 2])
        loaded, made, named_loaded, names_ready, counted, step = (
            ctx.sem(n) for n in ("loaded", "made", "named_loaded", "names_ready", "counted", "step"))
        with nc.Block() as block:

            @block.gpsimd
            def _(pool):
                nc.gpsimd.iota(place_i[:, :], [[1, SEQ]], base=0, channel_multiplier=0)
                nc.gpsimd.memset(named_i[:, :], -1).then_inc(made, 1)

            @block.sync
            def _(sp):
                sp.dma_start(words_i[:, :], on_every_partition(w["tokens"], NODES)).then_inc(loaded, 16)
                sp.wait_ge(made, 1)
                with nc.allow_non_contiguous_dma(reason="255 words"):
                    sp.dma_start(named_i[:, 0:1], w["a2a"][0:P].rearrange("(p o) -> p o", o=1)).then_inc(named_loaded, 16)
                    sp.dma_start(named_i[0:KEYS - P, 1:2], w["a2a"][P:KEYS].rearrange("(p o) -> p o", o=1)).then_inc(named_loaded, 16)

            @block.vector
            def _(dve):
                done = Done(step)
                nc.vector.memset(ones_b[:, :], 1.0)
                dve.wait_ge(named_loaded, 32)
                nc.vector.tensor_copy(named[:, :], named_i[:, :])
                done.add(nc.vector.tensor_copy(place[:, :], place_i[:, :]))
                done.wait(dve)
                for j in range(2):
                    last = nc.vector.tensor_scalar(names[:, j], place[:, :], named[:, j:j + 1], None, ALU.is_equal)
                last.then_inc(names_ready, 1)
                dve.wait_ge(counted, 1)
                nc.vector.tensor_copy(chosen[:, :].rearrange("p (a n) -> p a n", a=2), count_ps[:, :, :])
                dve.wait_ge(loaded, 16)
                nc.vector.tensor_copy(words[:, :], words_i[:, :])

            @block.tensor
            def _(pe):
                pe.wait_ge(names_ready, 1)
                for q in range(2):
                    for j in range(2):
                        last = nc.tensor.matmul(count_ps[:, q], ones_b[:, :], names[:, j, q * (SEQ // 2):(q + 1) * (SEQ // 2)],
                                                start=(j == 0), stop=(j == 1))
                last.then_inc(counted, 1)


def look_up(nc, c, words, chosen, chosen_table, plain_table, node_t):
    HALF = SEQ // 2
    with Stage(nc, c) as ctx:
        sb = ctx.sb

        is_named, not_named = sb("is_named", [P, SEQ]), sb("not_named", [P, SEQ])
        named_word, plain_word = sb("named_word", [P, SEQ]), sb("plain_word", [P, SEQ])
        hot = sb("hot", [P, 2, 2, 2, HALF])
        node_ps = [ctx.ps(f"node_ps{j}", [D, HALF]) for j in range(2)]
        step, hot_ready, hot_used, copied = (
            ctx.sem(n) for n in ("step", "hot_ready", "hot_used", "copied"))
        with nc.Block() as block:

            @block.vector
            def _(dve):
                done = Done(step)
                done.add(nc.vector.tensor_scalar(is_named[:, :], chosen[:, :], 1.0, None, ALU.min))
                done.wait(dve)
                done.add(nc.vector.tensor_scalar(not_named[:, :], is_named[:, :], -1.0, 1.0, ALU.mult, ALU.add))
                done.wait(dve)
                for s in range(BATCH):
                    x = words[:, s * SEQ:(s + 1) * SEQ]
                    if s:
                        dve.wait_ge(hot_ready, 2 * s)
                    for out, mask in ((named_word, is_named), (plain_word, not_named)):
                        done.add(nc.vector.scalar_tensor_tensor(out[:, :], x, 1.0, mask[:, :], ALU.add, ALU.mult))
                    done.wait(dve)
                    for out in (named_word, plain_word):
                        done.add(nc.vector.tensor_scalar_add(out[:, :], out[:, :], -1.0))
                    done.wait(dve)
                    for half in range(2):
                        if s:
                            dve.wait_ge(hot_used, 2 * (s - 1) + half + 1)
                        for kind, out in enumerate((named_word, plain_word)):
                            for j in range(2):
                                last = nc.vector.tensor_scalar(hot[:, half, kind, j], out[:, half * HALF:(half + 1) * HALF],
                                                               c.part_f[:, j:j + 1], None, ALU.is_equal)
                        last.then_inc(hot_ready, 1)

            @block.tensor
            def _(pe):
                for s in range(BATCH):
                    for half in range(2):
                        pe.wait_ge(hot_ready, 2 * s + half + 1)
                        if s:
                            pe.wait_ge(copied, 2 * (s - 1) + half + 1)
                        for j in range(2):
                            nc.tensor.matmul(node_ps[half][:, :], chosen_table[:, j, s], hot[:, half, 0, j], start=(j == 0), stop=False)
                        for j in range(2):
                            last = nc.tensor.matmul(node_ps[half][:, :], plain_table[:, j], hot[:, half, 1, j], start=False, stop=(j == 1))
                        last.then_inc(hot_used, 1)

            @block.scalar
            def _(act):
                for s in range(BATCH):
                    for half in range(2):
                        act.wait_ge(hot_used, 2 * s + half + 1)
                        nc.scalar.copy(node_t[:, s * SEQ + half * HALF:s * SEQ + (half + 1) * HALF], node_ps[half][:, :]).then_inc(copied, 1)


def to_nodes(nc, c, node_t, h, add):
    T4 = 4
    with Stage(nc, c) as ctx:
        stage = ctx.sb("stage", [D, 2, T4, P])
        turn_ps = [ctx.ps(f"turn_ps{j}", [P, T4, D]) for j in range(2)]
        staged, turned, read, go = (ctx.sem(n) for n in ("staged", "turned", "read", "go"))
        by_tile = node_t.rearrange("d (p t) -> d t p", t=TILES)
        with nc.Block() as block:

            @block.scalar
            def _(act):
                act.sem_inc(turned, 2)
                with act.Fori(0, TILES // T4 // 2) as i:
                    for half in range(2):
                        act.wait_ge(turned, 2 * i + (half + 1))
                        nc.scalar.copy(stage[:, half], by_tile[:, bass.ds(i * (2 * T4) + half * T4, T4)]).then_inc(staged, 1)

            @block.tensor
            def _(pe):
                with pe.Fori(0, TILES // T4 // 2) as i:
                    for half in range(2):
                        pe.wait_ge(staged, 2 * i + (half + 1))
                        pe.wait_ge(read, 2 * i + (half + 1))
                        pe.sem_inc(go, 1)
                        for k in range(T4):
                            last = nc.tensor.transpose(turn_ps[half][:, k], stage[:, half, k], c.ident[0:D, 0:D])
                        last.then_inc(turned, 1)

            @block.vector
            def _(dve):
                dve.sem_inc(read, 2)
                with dve.Fori(0, TILES // T4 // 2) as i:
                    for half in range(2):
                        dve.wait_ge(turned, 2 * i + (half + 3))
                        rows = h[:, bass.ds(i * (2 * T4) + half * T4, T4)]
                        if add:
                            nc.vector.tensor_tensor(rows, turn_ps[half][:, :, :], rows, ALU.add).then_inc(read, 1)
                        else:
                            nc.vector.tensor_copy(rows, turn_ps[half][:, :, :]).then_inc(read, 1)


EXPERTS = 8
T4 = 4


def norm_project(nc, c, h, x_t, weight, proj, add_back=False):
    with Stage(nc, c) as ctx:
        sb = ctx.sb

        n = 0 if proj is None else proj.shape[2]
        centred, square = sb("centred", [P, TILES, D]), sb("square", [P, TILES, D])
        stage, stage_t = sb("stage", [P, 2, T4, D]), sb("stage_t", [D, 2, T4, P])
        w_sb = sb("w_sb", [D, max(n, 1)])
        turn_ps = [ctx.ps(f"turn_ps{j}", [D, T4, P]) for j in range(2)]
        proj_ps = [ctx.ps(f"proj_ps{j}", [P, T4, max(n, 1)]) for j in range(2)]
        loaded, step, staged, turned, added, staged_t, copied, projected, read, go = (
            ctx.sem(s) for s in
            ("loaded", "step", "staged", "turned", "added", "staged_t", "copied", "projected", "read", "go"))
        norm = Norm(nc, ctx, "norm", TILES, D)
        LOOPS = TILES // T4 // 2
        with nc.Block() as block:

            @block.sync
            def _(sp):
                if n:
                    sp.dma_start(w_sb[:, :], weight).then_inc(loaded, 16)

            @block.vector
            def _(dve):
                done = Done(step)
                norm.centre(dve, done, h[:, :, :], centred[:, :, :], square[:, :, :])
                dve.sem_inc(turned, 2)
                dve.sem_inc(added, 2)
                with dve.Fori(0, LOOPS) as i:
                    for half in range(2):
                        tiles = bass.ds(i * (2 * T4) + half * T4, T4)
                        dve.wait_ge(turned, 2 * i + (half + 1))
                        if add_back:
                            dve.wait_ge(added, 2 * i + (half + 1))
                        nc.vector.tensor_tensor(stage[:, half], centred[:, tiles],
                                                norm.inv[:, tiles].unsqueeze(2).to_broadcast([P, T4, D]), ALU.mult).then_inc(staged, 1)
                        if add_back:
                            dve.wait_ge(staged, 2 * i + (half + 1))
                            nc.vector.tensor_tensor(h[:, tiles], h[:, tiles], stage[:, half], ALU.add).then_inc(added, 1)
                        if n:
                            dve.wait_ge(projected, 2 * i + (half + 1))
                            nc.vector.tensor_copy(proj[:, tiles], proj_ps[half][:, :, :]).then_inc(read, 1)

            @block.tensor
            def _(pe):
                pe.sem_inc(copied, 2)
                pe.sem_inc(read, 2)
                if n:
                    pe.wait_ge(loaded, 16)
                with pe.Fori(0, LOOPS) as i:
                    for half in range(2):
                        pe.wait_ge(staged, 2 * i + (half + 1))
                        pe.wait_ge(copied, 2 * i + (half + 1))
                        pe.sem_inc(go, 1)
                        for k in range(T4):
                            last = nc.tensor.transpose(turn_ps[half][:, k], stage[:, half, k], c.ident[:, :])
                        last.then_inc(turned, 1)
                        if n:
                            pe.wait_ge(staged_t, 2 * i + (half + 1))
                            pe.wait_ge(read, 2 * i + (half + 1))
                            for k in range(T4):
                                last = nc.tensor.matmul(proj_ps[half][:, k], stage_t[:, half, k], w_sb[:, :], start=True, stop=True)
                            last.then_inc(projected, 1)

            @block.scalar
            def _(act):
                norm.root(act)
                with act.Fori(0, LOOPS) as i:
                    for half in range(2):
                        act.wait_ge(turned, 2 * i + (half + 3))
                        if n:
                            nc.scalar.copy(stage_t[:, half], turn_ps[half][:, :, :]).then_inc(staged_t, 1)
                        nc.scalar.copy(x_t[:, bass.ds(i * (2 * T4) + half * T4, T4)], turn_ps[half][:, :, :]).then_inc(copied, 1)


def experts(nc, c, x_t, gates, h, w1, b1, w2, b2):
    E = gates.shape[2]
    width = E * D // 4
    with Stage(nc, c) as ctx:
        sb = ctx.sb

        w1_sb, b1_sb = sb("w1_sb", [D, 4, P]), sb("b1_sb", [P, 4])
        w2_sb, b2_sb = sb("w2_sb", [P, 4, width]), sb("b2_sb", [P, E, D])
        hid = sb("hid", [P, 2, 4, T4, P])
        y, mix = sb("y", [P, 2, E, D]), sb("mix", [P, D])
        hid_ps = [ctx.ps(f"hid_ps{j}", [P, T4, P]) for j in range(4)]
        y_ps = [ctx.ps(f"y_ps{j}", [P, E, D]) for j in range(2)]
        loaded, step, hid_done, hid_read, y_done, y_read, go, add_step = (
            ctx.sem(s) for s in
            ("loaded", "step", "hid_done", "hid_read", "y_done", "y_read", "go", "add_step"))
        LOOPS = TILES // T4 // 2
        with nc.Block() as block:

            @block.sync
            def _(sp):
                load_all(sp, [(w1_sb[:, :, :], w1), (b1_sb[:, :], b1), (w2_sb[:, :, :], w2),
                              (b2_sb[:, :, :], b2.rearrange("(o e) d -> o e d", o=1).to_broadcast([P, E, D]))], loaded)

            @block.tensor
            def _(pe):
                def up(number, first, half):
                    for e in range(4):
                        pe.wait_ge(hid_read, number * 4 + (e + 1))
                        pe.sem_inc(go, 1)
                        nc.tensor.matmul(hid_ps[e][:, :, :], w1_sb[:, e], x_t[:, bass.ds(first, T4)], start=True,
                                         stop=True).then_inc(hid_done, 1)

                pe.sem_inc(hid_read, 4)
                pe.sem_inc(y_read, 2)
                pe.wait_ge(loaded, 16 * 4)
                with pe.Fori(0, LOOPS) as i:
                    for half in range(2):
                        up(2 * i + half, i * (2 * T4) + half * T4, half)
                        pe.wait_ge(hid_read, i * 8 + (half * 4 + 8))
                        for k in range(T4):
                            pe.wait_ge(y_read, i * (2 * T4) + (half * T4 + k + 1))
                            for e in range(4):
                                last = nc.tensor.matmul(y_ps[k % 2][:, :, :].rearrange("p e d -> p (e d)")[:, e * width:(e + 1) * width],
                                                        hid[:, half, e, k], w2_sb[:, e], start=True, stop=True)
                            last.then_inc(y_done, 1)

            @block.scalar
            def _(act):
                act.wait_ge(loaded, 16 * 4)
                with act.Fori(0, LOOPS) as i:
                    for half in range(2):
                        for e in range(4):
                            act.wait_ge(hid_done, i * 8 + (half * 4 + e + 1))
                            nc.scalar.activation(hid[:, half, e], hid_ps[e][:, :, :], ACT.Gelu, bias=b1_sb[:, e:e + 1]).then_inc(hid_read, 1)

            @block.vector
            def _(dve):
                dve.wait_ge(loaded, 16 * 4)
                with dve.Fori(0, LOOPS) as i:
                    done = Done(step, i * (2 * T4 * 3))
                    for half in range(2):
                        for k in range(T4):
                            tile = bass.ds(i * (2 * T4) + (half * T4 + k), 1)
                            dve.wait_ge(y_done, i * (2 * T4) + (half * T4 + k + 1))
                            nc.vector.tensor_tensor(y[:, k % 2], y_ps[k % 2][:, :, :], b2_sb[:, :, :], ALU.add).then_inc(y_read, 1)
                            dve.wait_ge(y_read, i * (2 * T4) + (half * T4 + k + 3))
                            done.add(nc.vector.tensor_tensor(y[:, k % 2], y[:, k % 2], gates[:, tile].squeeze(1).unsqueeze(2).to_broadcast([P, E, D]), ALU.mult))
                            done.wait(dve)
                            done.add(nc.vector.tensor_reduce(mix[:, :], y[:, k % 2].rearrange("p e d -> p d e"), AX.X, ALU.add))
                            done.wait(dve)
                            done.add(nc.vector.tensor_tensor(h[:, tile].squeeze(1), h[:, tile].squeeze(1), mix[:, :], ALU.add))


def top_two(nc, dve, done, score, gates, rank, top, exp_in, exp_out, act_ask, act_told, asked):
    E = score.shape[2]
    for e in range(E):
        mine = score[:, :, e:e + 1]
        done.add(nc.vector.memset(rank[:, :, e:e + 1], 0.0))
        if e:
            done.add(nc.vector.tensor_tensor(rank[:, :, 0:e], score[:, :, 0:e], mine.to_broadcast([P, TILES, e]), ALU.is_ge))
        if e < E - 1:
            done.add(nc.vector.tensor_tensor(rank[:, :, e + 1:E], score[:, :, e + 1:E],
                                             mine.to_broadcast([P, TILES, E - 1 - e]), ALU.is_gt))
        done.wait(dve)
        done.add(nc.vector.tensor_reduce(gates[:, :, e:e + 1], rank[:, :, :], AX.X, ALU.add))
        done.wait(dve)
    done.add(nc.vector.tensor_scalar(rank[:, :, :], gates[:, :, :], 2.0, None, ALU.is_lt))
    done.add(nc.vector.tensor_reduce(top[:, :], score[:, :, :], AX.X, ALU.max))
    done.wait(dve)
    nc.vector.tensor_tensor(exp_in[:, :, :], score[:, :, :], top[:, :].unsqueeze(2).to_broadcast([P, TILES, E]),
                            ALU.subtract).then_inc(act_ask, 1)
    dve.wait_ge(act_told, asked)
    done.add(nc.vector.tensor_tensor(gates[:, :, :], exp_out[:, :, :], rank[:, :, :], ALU.mult))
    done.wait(dve)
    done.add(nc.vector.tensor_reduce(top[:, :], gates[:, :, :], AX.X, ALU.add))
    done.wait(dve)
    done.add(nc.vector.reciprocal(top[:, :], top[:, :]))
    done.wait(dve)
    done.add(nc.vector.tensor_tensor(gates[:, :, :], gates[:, :, :], top[:, :].unsqueeze(2).to_broadcast([P, TILES, E]), ALU.mult))
    done.wait(dve)


GH, GE = 4, 4
GF = GH * GE
ROW = GF + GH
OUT = ROW + GH
LOW = 1e30
ROUND = 1.5 * 2 ** 23
SC = 33


def send_nodes(nc, c, w, proj, start_i, source_rows, start_rows):
    with Stage(nc, c) as ctx:
        sb = ctx.sb

        att = sb("att", [P, 2, GF])
        rows, heads, tmp = sb("rows", [P, TILES, ROW]), sb("heads", [P, TILES, 1 + GH]), sb("tmp", [P, 2, TILES, GF])
        loaded, step, ready, sent_rows = (ctx.sem(s) for s in ("loaded", "step", "ready", "sent_rows"))
        sent = ctx.pool_sem("sent")
        with nc.Block() as block:

            @block.sync
            def _(sp):
                load_all(sp, [(att[:, 0], on_every_partition(w["att_src"], GF)), (att[:, 1], on_every_partition(w["att_dst"], GF))], loaded)
                sp.wait_ge(ready, 1)
                sp.dma_start(source_rows.rearrange("(p t) f -> p t f", p=P), rows[:, :, :]).then_inc(sent_rows, 16)
                sp.wait_ge(sent_rows, 16)

            @block.vector
            def _(dve):
                done = Done(step)
                dve.wait_ge(loaded, 32)
                for k in range(2):
                    done.add(nc.vector.tensor_tensor(tmp[:, k], proj[:, :, :], att[:, k].unsqueeze(1).to_broadcast([P, TILES, GF]), ALU.mult))
                nc.vector.tensor_copy(rows[:, :, 0:GF], proj[:, :, :])
                nc.vector.memset(heads[:, :, 0:1], 1.0)
                done.wait(dve)
                nc.vector.tensor_reduce(rows[:, :, GF:ROW], tmp[:, 0].rearrange("p t (h e) -> p t h e", h=GH), AX.X, ALU.add).then_inc(ready, 1)
                nc.vector.tensor_reduce(heads[:, :, 1:1 + GH], tmp[:, 1].rearrange("p t (h e) -> p t h e", h=GH), AX.X, ALU.add).then_inc(ready, 1)

            @block.gpsimd
            def _(pool):
                pool.wait_ge(ready, 2)
                for t in range(TILES):
                    nc.gpsimd.indirect_dma_start(start_rows, bass.IndirectOffsetOnAxis(ap=start_i[:, t:t + 1], axis=0),
                                                 heads[:, t], None, bounds_check=SLOTS - 1, oob_is_err=False).then_inc(sent, 16)
                pool.wait_ge(sent, 16 * TILES)


def spread_heads(nc, c, start_rows, not_first, minus_low, dst_term, has_none):
    with Stage(nc, c) as ctx:
        sb = ctx.sb

        rows = sb("rows", [P, SCOLS, 1 + GH])
        pair = sb("pair", [P, 2, GH])
        lines, carry = sb("lines", [GH, 2, P]), sb("carry", [GH, P + 1])
        begin = sb("begin", [P, GH])
        turn_ps = ctx.ps("turn_ps", [GH, 2, P])
        back_ps = ctx.ps("back_ps", [P, GH])
        loaded, step, pair_ready, turned, carried, back = (
            ctx.sem(s) for s in ("loaded", "step", "pair_ready", "turned", "carried", "back"))
        with nc.Block() as block:

            @block.sync
            def _(sp):
                sp.dma_start(rows[:, :, :], start_rows.rearrange("(p c) f -> p c f", p=P)).then_inc(loaded, 16)

            @block.vector
            def _(dve):
                def spread(initial):
                    for k in range(GH):
                        last = nc.vector.tensor_tensor_scan(dst_term[:, k], not_first[:, :], rows[:, :, 1 + k],
                                                            initial(k), ALU.mult, ALU.add)
                        done.add(last)

                done = Done(step)
                dve.wait_ge(loaded, 16)
                nc.vector.tensor_scalar(minus_low[:, :], rows[:, :, 0], -LOW, None, ALU.mult)
                done.add(nc.vector.tensor_reduce(has_none[:, :], rows[:, :, 0], AX.X, ALU.max))
                done.add(nc.vector.tensor_scalar(not_first[:, :], rows[:, :, 0], -1.0, 1.0, ALU.mult, ALU.add))
                done.wait(dve)
                done.add(nc.vector.tensor_scalar(has_none[:, :], has_none[:, :], -1.0, 1.0, ALU.mult, ALU.add))
                spread(lambda k: 0.0)
                done.wait(dve)
                nc.vector.tensor_copy(pair[:, 0], dst_term[:, :, SCOLS - 1])
                nc.vector.tensor_copy(pair[:, 1], has_none[:, :].to_broadcast([P, GH])).then_inc(pair_ready, 1)
                dve.wait_ge(turned, 1)
                done.add(nc.vector.tensor_copy(lines[:, :, :], turn_ps[:, :, :]))
                done.add(nc.vector.memset(carry[:, 0:1], 0.0))
                done.wait(dve)
                nc.vector.tensor_tensor_scan(carry[:, 1:P + 1], lines[:, 1], lines[:, 0], 0.0, ALU.mult, ALU.add).then_inc(carried, 1)
                dve.wait_ge(back, 1)
                done.add(nc.vector.tensor_copy(begin[:, :], back_ps[:, :]))
                done.wait(dve)
                spread(lambda k: begin[:, k:k + 1])

            @block.tensor
            def _(pe):
                pe.wait_ge(pair_ready, 1)
                for k in range(2):
                    last = nc.tensor.transpose(turn_ps[:, k], pair[:, k], c.ident[:, :])
                last.then_inc(turned, 1)
                pe.wait_ge(carried, 1)
                nc.tensor.transpose(back_ps[:, :], carry[:, 0:P], c.ident[0:GH, 0:GH]).then_inc(back, 1)


def aggregate(nc, c, sorted_src, source_rows, not_first, minus_low, dst_term, slot_rows, last_rows):
    with Stage(nc, c) as ctx:
        sb = ctx.sb

        ids = sb("ids", [P, SCOLS + 2 * SC], I32)
        id_stage = sb("id_stage", [P, 2, SC], I32)
        got = sb("got", [P, 2, SC, ROW])
        score = sb("score", [P, GH, SC])
        peak = sb("peak", [P, 2, GH, SC + 1])
        ex, weight = sb("ex", [P, 2, GH, SC]), sb("weight", [P, 2, GH, SC])
        message = sb("message", [P, GH, GE, SC])
        rows = sb("rows", [P, 2, SC, OUT])
        ids_loaded, staged, sent, step, ask, told, pool_go, rows_ready = (
            ctx.sem(s) for s in
            ("ids_loaded", "staged", "sent", "step", "ask", "told", "pool_go", "rows_ready"))
        got_in = [ctx.pool_sem(f"got_in{j}") for j in range(2)]
        stored = [ctx.sem(f"stored{j}") for j in range(2)]
        LOOPS = SCOLS // SC // 2
        STEPS = 33
        with nc.Block() as block:

            @block.sync
            def _(sp):
                sp.dma_start(ids[:, 0:SCOLS], sorted_src.rearrange("(p c) o -> p (c o)", p=P)).then_inc(ids_loaded, 16)
                sp.wait_ge(step, 2)
                for half in range(2):
                    sp.dma_start(slot_rows.rearrange("(p c) f -> p c f", p=P)[:, half * SC:(half + 1) * SC],
                                 rows[:, half]).then_inc(stored[half], 16)
                with sp.Fori(0, LOOPS) as i:
                    for half in range(2):
                        sp.wait_ge(rows_ready, 2 * i + (half + 1))
                        sp.wait_ge(stored[half], i * 16 + 16)
                        sp.dma_start(slot_rows.rearrange("(p c) f -> p c f", p=P)[:, bass.ds(i * (2 * SC) + half * SC, SC)],
                                     rows[:, half]).then_inc(stored[half], 16)
                for half in range(2):
                    sp.wait_ge(stored[half], 16 * (LOOPS + 1))

            @block.gpsimd
            def _(pool):
                with pool.Fori(0, LOOPS) as i:
                    for half in range(2):
                        pool.wait_ge(staged, 2 * i + (half + 1))
                        pool.sem_inc(pool_go, 1)
                        for k in range(SC):
                            nc.gpsimd.indirect_dma_start(got[:, half, k], None, source_rows,
                                                         bass.IndirectOffsetOnAxis(ap=id_stage[:, half, k:k + 1], axis=0)).then_inc(got_in[half], 16)

            @block.scalar
            def _(act):
                with act.Fori(0, LOOPS) as i:
                    for half in range(2):
                        act.wait_ge(ask, 2 * i + (half + 1))
                        nc.scalar.activation(weight[:, :, :, :], ex[:, :, :, :], ACT.Exp).then_inc(told, 1)

            @block.vector
            def _(dve):
                start = Done(step)
                start.add(nc.vector.memset(peak[:, 1], -LOW))
                start.add(nc.vector.memset(rows[:, :, :, :], 0.0))
                nc.vector.memset(ids[:, SCOLS:SCOLS + 2 * SC], 0)
                dve.wait_ge(ids_loaded, 16)
                nc.vector.tensor_copy(id_stage[:, 0], ids[:, 0:SC]).then_inc(staged, 1)
                nc.vector.tensor_copy(id_stage[:, 1], ids[:, SC:2 * SC]).then_inc(staged, 1)
                start.wait(dve)
                with dve.Fori(0, LOOPS) as i:
                    for half in range(2):
                        done = Done(step, i * (2 * STEPS) + (half * STEPS + 2))
                        cols = bass.ds(i * (2 * SC) + half * SC, SC)
                        g = got[:, half]
                        dve.wait_ge(got_in[half], i * (16 * SC) + 16 * SC)
                        done.add(nc.vector.tensor_copy(peak[:, half, :, 0:1], peak[:, 1 - half, :, SC:SC + 1]))
                        done.add(nc.vector.tensor_tensor(score[:, :, :], g[:, :, GF:ROW].rearrange("p c h -> p h c"),
                                                         dst_term[:, :, cols], ALU.add))
                        done.wait(dve)
                        done.add(nc.vector.scalar_tensor_tensor(score[:, :, :], score[:, :, :], 0.2, score[:, :, :], ALU.mult, ALU.max))
                        done.wait(dve)
                        for k in range(GH):
                            done.add(nc.vector.tensor_tensor_scan(peak[:, half, k, 1:SC + 1], minus_low[:, cols], score[:, k],
                                                                  peak[:, half, k, 0:1], ALU.add, ALU.max))
                        done.wait(dve)
                        done.add(nc.vector.tensor_tensor(ex[:, 1], peak[:, half, :, 0:SC], peak[:, half, :, 1:SC + 1], ALU.subtract))
                        done.add(nc.vector.tensor_tensor(ex[:, 0], score[:, :, :], peak[:, half, :, 1:SC + 1], ALU.subtract))
                        done.wait(dve)
                        nc.vector.tensor_scalar(ex[:, 1], ex[:, 1], 0.0, None, ALU.min).then_inc(ask, 1)
                        dve.wait_ge(told, 2 * i + (half + 1))
                        done.add(nc.vector.tensor_tensor(weight[:, 1], weight[:, 1], not_first[:, cols].unsqueeze(1).to_broadcast([P, GH, SC]), ALU.mult))
                        done.add(nc.vector.tensor_tensor(message[:, :, :, :], g[:, :, 0:GF].rearrange("p c (h e) -> p h e c", h=GH),
                                                         weight[:, 0].unsqueeze(2).to_broadcast([P, GH, GE, SC]), ALU.mult))
                        dve.wait_ge(stored[half], i * 16 + 16)
                        done.wait(dve)
                        for f in range(ROW):
                            k = f // GE if f < GF else f - GF
                            new = message[:, k, f % GE] if f < GF else weight[:, 0, k]
                            done.add(nc.vector.tensor_tensor_scan(rows[:, half, :, f], weight[:, 1, k], new,
                                                                  rows[:, 1 - half, SC - 1, f:f + 1], ALU.mult, ALU.add))
                        done.add(nc.vector.tensor_copy(rows[:, half, :, ROW:OUT].rearrange("p c h -> p h c"), peak[:, half, :, 1:SC + 1]))
                        done.add(nc.vector.tensor_copy(id_stage[:, half], ids[:, bass.ds(i * (2 * SC) + (half + 2) * SC, SC)]))
                        assert done.n == STEPS, done.n
                        done.wait(dve)
                        dve.sem_inc(staged, 1)
                        dve.sem_inc(rows_ready, 1)
                nc.vector.tensor_copy(last_rows[:, :], rows[:, 1, SC - 1])


def finish_graph(nc, c, w, end_i, start_i, slot_rows, carry_rows, last_rows, has_none, gates):
    with Stage(nc, c) as ctx:
        sb = ctx.sb
        sem = ctx.sem

        part = sb("part", [P, 3, ROW])
        line = sb("line", [ROW, 3, P])
        open_max, open_sum = sb("open_max", [ROW, P + 1]), sb("open_sum", [ROW, P])
        low = sb("low", [ROW, P])
        fac = sb("fac", [ROW, 2, P])
        back = sb("back", [P, 2, ROW])
        none = sb("none", [1, 2, ROW])
        part_ps = ctx.ps("part_ps", [ROW, 3, P])
        back_ps = ctx.ps("back_ps", [P, 2, ROW])
        first_part, last_part = sb("first_part", [P, TILES]), sb("last_part", [P, TILES])
        carry_i = sb("carry_i", [P, TILES], I32)
        mine, before = sb("mine", [P, TILES, OUT]), sb("before", [P, TILES, 2 * ROW])
        peak = sb("peak", [P, TILES, GH])
        ex, factor = sb("ex", [P, 2, TILES, GH]), sb("factor", [P, 2, TILES, GH])
        inv = sb("inv", [P, TILES, GH])
        agg, centred, square = sb("agg", [P, TILES, GF]), sb("centred", [P, TILES, GF]), sb("square", [P, TILES, GF])
        gain = sb("gain", [P, 3, GF])
        score, rank, top, sx = sb("score", [P, TILES, GE]), sb("rank", [P, TILES, GE]), sb("top", [P, TILES]), sb("sx", [P, 2, TILES, GE])
        loaded, step, part_ready, turned, lines_ready, ask, told, turned_back, stored, carry_sent, idx_ready = map(
            sem, ("loaded", "step", "part_ready", "turned", "lines_ready", "ask", "told", "turned_back", "stored",
                  "carry_sent", "idx_ready"))
        mine_in, before_in = ctx.pool_sem("mine_in"), ctx.pool_sem("before_in")
        norm = Norm(nc, ctx, "norm", TILES, GF)

        with nc.Block() as block:

            @block.sync
            def _(sp):
                load_all(sp, [(gain[:, 0], on_every_partition(w["gat_b"], GF)), (gain[:, 1], on_every_partition(w["ln_gamma"], GF)),
                              (gain[:, 2], on_every_partition(w["ln_beta"], GF))], loaded)
                sp.wait_ge(stored, 1)
                sp.dma_start(carry_rows[0:P].rearrange("p (a f) -> p a f", a=2), back[:, :, :]).then_inc(carry_sent, 16)
                sp.dma_start(carry_rows[P:P + 1].rearrange("p (a f) -> p a f", a=2), none[:, :, :]).then_inc(carry_sent, 16)
                sp.wait_ge(carry_sent, 32)

            @block.gpsimd
            def _(pool):
                for t in range(TILES):
                    nc.gpsimd.indirect_dma_start(mine[:, t], None, slot_rows,
                                                 bass.IndirectOffsetOnAxis(ap=end_i[:, t:t + 1], axis=0)).then_inc(mine_in, 16)
                pool.wait_ge(carry_sent, 32)
                pool.wait_ge(idx_ready, 1)
                for t in range(TILES):
                    nc.gpsimd.indirect_dma_start(before[:, t], None, carry_rows,
                                                 bass.IndirectOffsetOnAxis(ap=carry_i[:, t:t + 1], axis=0)).then_inc(before_in, 16)

            @block.tensor
            def _(pe):
                pe.wait_ge(part_ready, 1)
                for k in range(3):
                    last = nc.tensor.transpose(part_ps[:, k], part[:, k], c.ident[:, :])
                last.then_inc(turned, 1)
                pe.wait_ge(lines_ready, 1)
                nc.tensor.transpose(back_ps[:, 0], open_max[:, 1:P + 1], c.ident[0:ROW, 0:ROW])
                nc.tensor.transpose(back_ps[:, 1], open_sum[:, :], c.ident[0:ROW, 0:ROW]).then_inc(turned_back, 1)

            @block.scalar
            def _(act):
                act.wait_ge(ask, 1)
                nc.scalar.activation(fac[:, :, :], fac[:, :, :], ACT.Exp).then_inc(told, 1)
                act.wait_ge(ask, 2)
                nc.scalar.activation(factor[:, :, :, :], ex[:, :, :, :], ACT.Exp).then_inc(told, 1)
                norm.root(act)
                act.wait_ge(ask, 3)
                nc.scalar.activation(sx[:, 1], sx[:, 0], ACT.Exp).then_inc(told, 1)

            @block.vector
            def _(dve):
                v = nc.vector
                done = Done(step)
                done.add(v.tensor_copy(part[:, 0, 0:GF].rearrange("p (h e) -> p h e", h=GH),
                                       last_rows[:, ROW:OUT].unsqueeze(2).to_broadcast([P, GH, GE])))
                v.tensor_copy(part[:, 0, GF:ROW], last_rows[:, ROW:OUT])
                v.tensor_copy(part[:, 1], last_rows[:, 0:ROW])
                v.memset(none[:, 0], -LOW)
                v.memset(none[:, 1], 0.0)
                v.tensor_copy(part[:, 2], has_none[:, :].to_broadcast([P, ROW])).then_inc(part_ready, 1)
                dve.wait_ge(turned, 1)
                done.add(v.tensor_copy(line[:, :, :], part_ps[:, :, :]))
                done.add(v.memset(open_max[:, 0:1], -LOW))
                done.wait(dve)
                done.add(v.tensor_scalar(low[:, :], line[:, 2], -1.0, LOW, ALU.add, ALU.mult))
                done.wait(dve)
                done.add(v.tensor_tensor_scan(open_max[:, 1:P + 1], low[:, :], line[:, 0], -LOW, ALU.add, ALU.max))
                done.wait(dve)
                done.add(v.tensor_tensor(fac[:, 0], open_max[:, 0:P], open_max[:, 1:P + 1], ALU.subtract))
                done.add(v.tensor_tensor(fac[:, 1], line[:, 0], open_max[:, 1:P + 1], ALU.subtract))
                done.wait(dve)
                v.tensor_scalar(fac[:, 0], fac[:, 0], 0.0, None, ALU.min).then_inc(ask, 1)
                dve.wait_ge(told, 1)
                done.add(v.tensor_tensor(fac[:, 0], fac[:, 0], line[:, 2], ALU.mult))
                done.add(v.tensor_tensor(fac[:, 1], fac[:, 1], line[:, 1], ALU.mult))
                done.wait(dve)
                v.tensor_tensor_scan(open_sum[:, :], fac[:, 0], fac[:, 1], 0.0, ALU.mult, ALU.add).then_inc(lines_ready, 1)
                dve.wait_ge(turned_back, 1)
                v.tensor_copy(back[:, :, :], back_ps[:, :, :]).then_inc(stored, 1)
                for out, slots in ((first_part, start_i), (last_part, end_i)):
                    done.add(v.tensor_scalar(out[:, :], slots[:, :], 1.0 / SCOLS, 0.5 / SCOLS - 0.5, ALU.mult, ALU.add))
                done.wait(dve)
                for out in (first_part, last_part):
                    done.add(v.tensor_scalar_add(out[:, :], out[:, :], ROUND))
                done.wait(dve)
                for out in (first_part, last_part):
                    done.add(v.tensor_scalar_add(out[:, :], out[:, :], -ROUND))
                done.wait(dve)
                done.add(v.tensor_tensor(first_part[:, :], first_part[:, :], last_part[:, :], ALU.is_lt))
                done.wait(dve)
                done.add(v.scalar_tensor_tensor(last_part[:, :], last_part[:, :], -float(P + 1), first_part[:, :], ALU.add, ALU.mult))
                done.wait(dve)
                v.tensor_scalar_add(carry_i[:, :], last_part[:, :], float(P)).then_inc(idx_ready, 1)
                dve.wait_ge(mine_in, 16 * TILES)
                dve.wait_ge(before_in, 16 * TILES)
                done.add(v.tensor_tensor(peak[:, :, :], mine[:, :, ROW:OUT], before[:, :, GF:ROW], ALU.max))
                done.wait(dve)
                done.add(v.tensor_tensor(ex[:, 0], mine[:, :, ROW:OUT], peak[:, :, :], ALU.subtract))
                v.tensor_tensor(ex[:, 1], before[:, :, GF:ROW], peak[:, :, :], ALU.subtract).then_inc(ask, 1)
                dve.wait_ge(told, 2)

                def by_head(x):
                    return x.rearrange("p t (h e) -> p t h e", h=GH)

                def wide(x):
                    return x.unsqueeze(3).to_broadcast([P, TILES, GH, GE])

                done.add(v.tensor_tensor(by_head(agg[:, :, :]), by_head(mine[:, :, 0:GF]), wide(factor[:, 0]), ALU.mult))
                done.add(v.tensor_tensor(by_head(centred[:, :, :]), by_head(before[:, :, ROW:ROW + GF]), wide(factor[:, 1]), ALU.mult))
                done.add(v.tensor_tensor(inv[:, :, :], mine[:, :, GF:ROW], factor[:, 0], ALU.mult))
                done.add(v.tensor_tensor(peak[:, :, :], before[:, :, ROW + GF:2 * ROW], factor[:, 1], ALU.mult))
                done.wait(dve)
                done.add(v.tensor_tensor(agg[:, :, :], agg[:, :, :], centred[:, :, :], ALU.add))
                done.add(v.scalar_tensor_tensor(inv[:, :, :], inv[:, :, :], 1e-16, peak[:, :, :], ALU.add, ALU.add))
                done.wait(dve)
                done.add(v.reciprocal(inv[:, :, :], inv[:, :, :]))
                done.wait(dve)
                done.add(v.tensor_tensor(by_head(agg[:, :, :]), by_head(agg[:, :, :]), wide(inv[:, :, :]), ALU.mult))
                dve.wait_ge(loaded, 48)
                done.wait(dve)

                def row(k):
                    return gain[:, k].unsqueeze(1).to_broadcast([P, TILES, GF])

                done.add(v.tensor_tensor(agg[:, :, :], agg[:, :, :], row(0), ALU.add))
                done.wait(dve)
                norm.centre(dve, done, agg[:, :, :], centred[:, :, :], square[:, :, :])
                done.add(v.tensor_tensor(centred[:, :, :], centred[:, :, :], norm.wide(norm.inv), ALU.mult))
                done.wait(dve)
                for k, op in ((1, ALU.mult), (2, ALU.add)):
                    done.add(v.tensor_tensor(centred[:, :, :], centred[:, :, :], row(k), op))
                    done.wait(dve)
                done.add(v.tensor_reduce(score[:, :, :], centred[:, :, :].rearrange("p t (h e) -> p t e h", h=GH), AX.X, ALU.add))
                done.wait(dve)
                done.add(v.tensor_scalar_mul(score[:, :, :], score[:, :, :], 1.0 / GH))
                done.wait(dve)
                top_two(nc, dve, done, score, gates, rank, top, sx[:, 0], sx[:, 1], ask, told, 3)


def route(nc, c, logits, gates):
    E = logits.shape[2]
    with Stage(nc, c) as ctx:
        sb = ctx.sb

        rank, top, sx = sb("rank", [P, TILES, E]), sb("top", [P, TILES]), sb("sx", [P, 2, TILES, E])
        step, ask, told = (ctx.sem(s) for s in ("step", "ask", "told"))
        with nc.Block() as block:

            @block.vector
            def _(dve):
                top_two(nc, dve, Done(step), logits, gates, rank, top, sx[:, 0], sx[:, 1], ask, told, 1)

            @block.scalar
            def _(act):
                act.wait_ge(ask, 1)
                nc.scalar.activation(sx[:, 1], sx[:, 0], ACT.Exp).then_inc(told, 1)


def column_attention(nc, c, w, x_t, out_t):
    KT = SEQ // P
    MASK = -1e10
    with Stage(nc, c) as ctx:
        sb = ctx.sb
        sem = ctx.sem

        wqkv = sb("wqkv", [D, 3, D])
        xb, q, k = sb("xb", [D, SEQ]), sb("q", [D, SEQ]), sb("k", [D, SEQ])
        v = sb("v", [P, KT, D])
        mask = sb("mask", [P, SEQ])
        e = sb("e", [P, KT, SEQ])
        peak, total = sb("peak", [P, KT]), sb("total", [P, KT])
        in_ps = [ctx.ps(f"in_ps{j}", [P, 512]) for j in range(2)]
        s_ps = [ctx.ps(f"s_ps{j}", [P, SEQ]) for j in range(2)]
        o_ps = ctx.ps("o_ps", [D, 2, 512])
        loaded, masked, xb_ready, in_done, in_read, s_done, s_read, v_ready, step, peak_ready, exp_done, o_done, o_read, go = map(
            sem, ("loaded", "masked", "xb_ready", "in_done", "in_read", "s_done", "s_read", "v_ready", "step",
                  "peak_ready", "exp_done", "o_done", "o_read", "go"))

        def width(m):
            return SEQ if m == 0 else (m + 1) * P

        with nc.Block() as block:

            @block.sync
            def _(sp):
                load_all(sp, [(wqkv[:, j], w[n]) for j, n in enumerate(("l1_wq_t", "l1_wk_t", "l1_wv_t"))], loaded)

            @block.gpsimd
            def _(pool):
                nc.gpsimd.memset(mask[:, :], MASK).then_inc(masked, 1)
                pool.wait_ge(masked, 1)
                nc.gpsimd.affine_select(out=mask[:, :], in_=mask[:, :], compare_op=ALU.is_ge, fill=0.0, base=0,
                                        pattern=[[1, SEQ]], channel_multiplier=-1).then_inc(masked, 1)

            @block.scalar
            def _(act):
                act.sem_inc(in_read, 2)
                act.wait_ge(loaded, 48)
                with act.Fori(0, BATCH) as s:
                    act.wait_ge(o_read, s + 1)
                    nc.scalar.copy(xb[:, :].rearrange("d (p t) -> d t p", t=TILES), x_t[:, :, bass.ds(s * (SEQ // TILES), SEQ // TILES)]).then_inc(xb_ready, 1)
                    for j in range(4):
                        act.wait_ge(in_done, s * 5 + (j + 1))
                        nc.scalar.copy((q, k)[j // 2][:, j % 2 * 512:(j % 2 + 1) * 512], in_ps[j % 2][0:D, :]).then_inc(in_read, 1)
                    act.wait_ge(in_done, s * 5 + 5)
                    nc.scalar.copy(v[:, :, :], in_ps[0][:, :].rearrange("p (m d) -> p m d", m=KT)).then_inc(in_read, 1)
                    for m in range(KT):
                        act.wait_ge(peak_ready, s * KT + (m + 1))
                        nc.scalar.activation(e[:, m, 0:width(m)], s_ps[m % 2][:, 0:width(m)], ACT.Exp, scale=D ** -0.5,
                                             bias=peak[:, m:m + 1], accum_out=total[:, m:m + 1]).then_inc(exp_done, 1)
                    act.wait_ge(o_done, s + 1)
                    nc.scalar.copy(out_t[:, bass.ds(s * SEQ, SEQ)].rearrange("d (a n) -> d a n", a=2), o_ps[:, :, :]).then_inc(o_read, 1)

            @block.tensor
            def _(pe):
                pe.sem_inc(o_read, 1)
                pe.sem_inc(s_read, 2)
                pe.wait_ge(loaded, 48)

                def scores(s, m):
                    pe.wait_ge(exp_done, s * KT + (m + 1 - 2 + 2))
                    for a in range(0, width(m), 512):
                        b = min(a + 512, width(m))
                        last = nc.tensor.matmul(s_ps[m % 2][:, a:b], k[:, m * P:(m + 1) * P], q[:, a:b], start=True, stop=True)
                    last.then_inc(s_done, 1)

                def mix(s, m):
                    if m == 0:
                        pe.wait_ge(o_read, s + 1)
                    pe.wait_ge(v_ready, s * KT + (m + 1))
                    for a in range(2):
                        n = min(width(m) - a * 512, 512)
                        if n > 0:
                            last = nc.tensor.matmul(o_ps[:, a, 0:n], v[:, m], e[:, m, a * 512:a * 512 + n],
                                                    start=(m == 0), stop=(m == KT - 1))
                    return last

                pe.sem_inc(exp_done, 2)
                with pe.Fori(0, BATCH) as s:
                    pe.wait_ge(xb_ready, s + 1)
                    for j in range(4):
                        pe.wait_ge(in_read, s * 5 + max(j + 1, 2))
                        pe.sem_inc(go, 1)
                        nc.tensor.matmul(in_ps[j % 2][0:D, :], wqkv[:, j // 2], xb[:, j % 2 * 512:(j % 2 + 1) * 512],
                                         start=True, stop=True).then_inc(in_done, 1)
                    pe.wait_ge(in_read, s * 5 + 6)
                    for m in range(KT):
                        last = nc.tensor.matmul(in_ps[0][:, m * D:(m + 1) * D], xb[:, m * P:(m + 1) * P], wqkv[:, 2], start=True, stop=True)
                    last.then_inc(in_done, 1)
                    scores(s, 0)
                    for m in range(1, KT):
                        scores(s, m)
                        mix(s, m - 1)
                    mix(s, KT - 1).then_inc(o_done, 1)

            @block.vector
            def _(dve):
                def divide(s, m):
                    if m == 0:
                        dve.wait_ge(in_read, s * 5 + 7)
                    dve.wait_ge(exp_done, s * KT + (m + 3))
                    done.add(nc.vector.reciprocal(total[:, m:m + 1], total[:, m:m + 1]))
                    done.wait(dve)
                    nc.vector.tensor_scalar(v[:, m], v[:, m], total[:, m:m + 1], None, ALU.mult).then_inc(v_ready, 1)

                dve.wait_ge(masked, 2)
                with dve.Fori(0, BATCH) as s:
                    done = Done(step, s * (3 * KT))
                    for m in range(KT):
                        n = width(m)
                        lo = m * P
                        dve.wait_ge(s_done, s * KT + (m + 1))
                        cut = slice(0, SEQ) if m == 0 else slice(lo, lo + P)
                        done.add(nc.vector.tensor_tensor(s_ps[m % 2][:, cut], s_ps[m % 2][:, cut], mask[:, 0:cut.stop - cut.start], ALU.add))
                        done.wait(dve)
                        done.add(nc.vector.tensor_reduce(peak[:, m:m + 1], s_ps[m % 2][:, 0:n], AX.X, ALU.max))
                        done.wait(dve)
                        nc.vector.tensor_scalar_mul(peak[:, m:m + 1], peak[:, m:m + 1], -(D ** -0.5)).then_inc(peak_ready, 1)
                        if m:
                            divide(s, m - 1)
                    divide(s, KT - 1)


class Constants:

    def __init__(self, nc, whole):
        def sb(name, shape, dt=F32):
            return whole.enter_context(nc.sbuf_tensor(name, shape, dt))

        self.whole, self.stages, self.used = whole, 0, []
        self.ident, self.ident_b = sb("ident", [P, P]), sb("ident_b", [P, P], BF16)
        self.upper, self.upper_b = sb("upper", [P, P]), sb("upper_b", [P, P], BF16)
        self.zeros, self.ones = sb("zeros", [P, P]), sb("ones", [P, P])
        self.iota_i, self.iota_b = sb("iota_i", [P, P], I32), sb("iota_b", [P, P], BF16)
        self.part_i, self.part_f = sb("part_i", [P, 2], I32), sb("part_f", [P, 2])


def store_nodes(nc, c, h, out):
    with Stage(nc, c) as ctx, nc.Block() as block:
        stored = ctx.sem("stored")

        @block.sync
        def _(sp):
            sp.dma_start(out.rearrange("(p t) d -> p t d", p=P), h[:, :, :]).then_inc(stored, 16)
            sp.wait_ge(stored, 16)


def build_tower(nc, w, out):
    def dram(name, shape, dt=F32):
        return nc.dram_tensor(name, shape, dt).ap()

    sorted_src, start_rows = dram("sorted_src", (SLOTS, 1), I32), dram("start_rows", (SLOTS, 1 + GH))
    source_rows, slot_rows = dram("source_rows", (NODES, ROW)), dram("slot_rows", (SLOTS, OUT))
    carry_rows = dram("carry_rows", (P + 1, 2 * ROW))
    with ExitStack() as whole:
        c = Constants(nc, whole)
        h = whole.enter_context(nc.sbuf_tensor("h", [P, TILES, D], F32))
        start_i = whole.enter_context(nc.sbuf_tensor("start_i", [P, TILES], I32))
        end_i = whole.enter_context(nc.sbuf_tensor("end_i", [P, TILES], I32))
        make_constants(nc, c)
        sort_edges(nc, c, w["edges"], sorted_src, start_rows, start_i, end_i)

        with Stage(nc, c) as s:
            tab_h, tab_x, tab_xt = s.sb("tab_h", [P, 2, D]), s.sb("tab_x", [P, 2, D]), s.sb("tab_xt", [D + 1, VOCAB])
            words, chosen = s.sb("words", [P, NODES]), s.sb("chosen", [P, SEQ])
            chosen_table, plain_table = s.sb("chosen_table", [P, 2, BATCH, D]), s.sb("plain_table", [P, 2, D])
            token_tables(nc, c, w, tab_h, tab_x, tab_xt)
            load_words(nc, c, w, words, chosen)
            word_attention(nc, c, w, tab_h, tab_x, tab_xt, words, chosen, chosen_table, plain_table)
            with Stage(nc, c) as t:
                node_t = t.sb("node_t", [D, NODES])
                look_up(nc, c, words, chosen, chosen_table, plain_table, node_t)
                to_nodes(nc, c, node_t[:, :], h, False)

        with Stage(nc, c) as s:
            x_t = s.sb("x_t", [D, TILES, P])
            gates = s.sb("gates", [P, TILES, GE])
            has_none, last_rows = s.sb("has_none", [P, 1]), s.sb("last_rows", [P, OUT])
            with Stage(nc, c) as t:
                proj = t.sb("proj", [P, TILES, GF])
                norm_project(nc, c, h, x_t, w["gat_w"], proj)
                send_nodes(nc, c, w, proj, start_i, source_rows, start_rows)
            with Stage(nc, c) as t:
                not_first, minus_low = t.sb("not_first", [P, SCOLS]), t.sb("minus_low", [P, SCOLS])
                dst_term = t.sb("dst_term", [P, GH, SCOLS])
                spread_heads(nc, c, start_rows, not_first, minus_low, dst_term, has_none)
                aggregate(nc, c, sorted_src, source_rows, not_first, minus_low, dst_term, slot_rows, last_rows)
            finish_graph(nc, c, w, end_i, start_i, slot_rows, carry_rows, last_rows, has_none, gates)
            experts(nc, c, x_t, gates, h, w["ffn_w1"], w["ffn_b1"], w["ffn_w2"], w["ffn_b2"])

        clear_semaphores(nc, c)
        with Stage(nc, c) as s:
            x_t, out_t = s.sb("x_t", [D, TILES, P]), s.sb("out_t", [D, NODES])
            norm_project(nc, c, h, x_t, None, None)
            column_attention(nc, c, w, x_t, out_t)
            to_nodes(nc, c, out_t[:, :], h, True)
        with Stage(nc, c) as s:
            x_t, gates = s.sb("x_t", [D, TILES, P]), s.sb("gates", [P, TILES, EXPERTS])
            logits = s.sb("logits", [P, TILES, EXPERTS])
            norm_project(nc, c, h, x_t, w["router_t"], logits, add_back=True)
            route(nc, c, logits, gates)
            experts(nc, c, x_t, gates, h, w["moe_w1"], w["moe_b1"], w["moe_w2"], w["moe_b2"])
        store_nodes(nc, c, h, out)


def kernel(**inputs):
    import numpy as np
    import concourse.bacc as bacc
    from concourse.bass_utils import run_bass_kernel_spmd as run

    a = {name: np.asarray(value) for name, value in inputs.items()}

    def with_bias(weight, bias):
        return np.concatenate([weight.T, bias[None]], 0)

    def pair_blocks(w2):
        pairs = w2.reshape(EXPERTS // 2, 2, D, D)
        out = np.zeros((2, D, EXPERTS // 2, 2, D), w2.dtype)
        for j in range(2):
            out[j, :, :, j, :] = pairs[:, j].transpose(1, 0, 2)
        return out.reshape(2 * D, EXPERTS // 2, 2 * D)

    arrays = {
        "tokens": a["x"].reshape(-1),
        "a2a": a["L0_attn_a2a"],
        "emb_t": a["L0_tok_emb_table"].T,
        "tok_w1_t": a["L0_tok_W1"][:, :D].T,
        "tok_b1": a["L0_tok_b1"][:, None],
        "tok_w2_t": with_bias(a["L0_tok_W2"], a["L0_tok_b2"]),
        "tok_gamma": a["L0_tok_gamma"],
        "tok_beta": a["L0_tok_beta"],
        "wq_t": a["L0_attn_wq"].T,
        "wv_t": a["L0_attn_wv"].T,
        "wk_pairs": a["L0_attn_wk"].reshape(HEADS0 // 2, 2 * D).T,
        "fan_t": a["L0_attn_fanout_w"].T,
        "edges": a["L0_ffn_edge_index"],
        "gat_w": a["L0_ffn_W_gat"],
        "att_src": a["L0_ffn_att_src"].reshape(-1),
        "att_dst": a["L0_ffn_att_dst"].reshape(-1),
        "gat_b": a["L0_ffn_b_gat"],
        "ln_gamma": a["L0_ffn_ln_gamma"],
        "ln_beta": a["L0_ffn_ln_beta"],
        "ffn_w1": a["L0_ffn_W1"].transpose(1, 0, 2),
        "ffn_b1": a["L0_ffn_b1"].T,
        "ffn_w2": a["L0_ffn_W2"].transpose(1, 0, 2),
        "ffn_b2": a["L0_ffn_b2"],
        "l1_wq_t": a["L1_attn_Wq"].T,
        "l1_wk_t": a["L1_attn_Wk"].T,
        "l1_wv_t": a["L1_attn_Wv"].T,
        "router_t": a["L1_ffn_router_w"].T,
        "moe_w1": a["L1_ffn_w1"].reshape(EXPERTS // 2, 2, D, D).transpose(2, 0, 1, 3).reshape(D, EXPERTS // 2, 2 * D),
        "moe_b1": a["L1_ffn_b1"].reshape(EXPERTS // 2, 2 * D).T,
        "moe_w2": pair_blocks(a["L1_ffn_w2"]),
        "moe_b2": a["L1_ffn_b2"],
    }
    arrays = {name: np.ascontiguousarray(value) for name, value in arrays.items()}
    nc = bacc.Bacc("TRN2", target_bir_lowering=False, num_devices=1)
    w = {name: nc.dram_tensor("in_" + name, value.shape, mybir.dt.from_np(value.dtype), kind="ExternalInput").ap()
         for name, value in arrays.items()}
    out = nc.dram_tensor("out", (NODES, D), F32, kind="ExternalOutput").ap()
    build_tower(nc, w, out)
    r = run(nc, [{"in_" + name: value for name, value in arrays.items()}], core_ids=[0])
    return r.results[0]["out"].reshape(BATCH, SEQ, D)
```

```python
import concourse.bass as bass
from concourse import mybir
from concourse.alu_op_type import AluOpType as ALU
from contextlib import ExitStack

F32 = mybir.dt.float32
BF16 = mybir.dt.bfloat16
I32 = mybir.dt.int32
U8 = mybir.dt.uint8
ACT = mybir.ActivationFunctionType
AX = mybir.AxisListType

P = 128
BATCH, SEQ, D = 8, 1024, 64
NODES = BATCH * SEQ
TILES = NODES // P
EDGES = 262144
COLS = EDGES // P
GC = 8
GROUPS = COLS // GC
SLOTS = EDGES + NODES
SCOLS = SLOTS // P
DROPPED = 1 << 20


class Stage(ExitStack):

    def __init__(self, nc, c):
        super().__init__()
        self.nc = nc
        c.stages += 1
        self.tag = f"s{c.stages}_"
        self.used, self.whole = c.used, c.whole

    def sb(self, name, shape, dt=F32):
        return self.enter_context(self.nc.sbuf_tensor(self.tag + name, shape, dt))

    def ps(self, name, shape, dt=F32):
        return self.enter_context(self.nc.psum_tensor(self.tag + name, shape, dt))

    def sem(self, name):
        s = self.enter_context(self.nc.semaphore(self.tag + name))
        self.used.append(s)
        return s

    def pool_sem(self, name):
        return self.whole.enter_context(self.nc.semaphore(self.tag + name))


def clear_semaphores(nc, c):
    with nc.Block() as block:

        @block.sync
        def _(sp):
            for s in c.used:
                sp.sem_clear(s)
            c.used.clear()


class Done:

    def __init__(self, sem, base=0):
        self.sem, self.base, self.n = sem, base, 0

    def add(self, instruction, by=1):
        instruction.then_inc(self.sem, by)
        self.n += by
        return self.base + self.n

    def wait(self, engine):
        engine.wait_ge(self.sem, self.base + self.n)


def make_constants(nc, c):
    with Stage(nc, c) as ctx, nc.Block() as block:
        const_step = ctx.sem("const_step")

        @block.gpsimd
        def _(pool):
            done = Done(const_step)
            nc.gpsimd.memset(c.ident[:, :], 0.0)
            nc.gpsimd.memset(c.upper[:, :], 1.0)
            nc.gpsimd.memset(c.zeros[:, :], 0.0)
            nc.gpsimd.memset(c.ones[:, :], 1.0)
            nc.gpsimd.iota(c.iota_i[:, :], [[1, P]], base=0, channel_multiplier=0)
            done.add(nc.gpsimd.iota(c.part_i[:, :], [[P, 2]], base=0, channel_multiplier=1))
            done.wait(pool)
            nc.gpsimd.affine_select(out=c.ident[:, :], in_=c.ident[:, :], compare_op=ALU.not_equal, fill=1.0,
                                    base=0, pattern=[[-1, P]], channel_multiplier=1)
            done.add(nc.gpsimd.affine_select(out=c.upper[:, :], in_=c.upper[:, :], compare_op=ALU.is_gt, fill=0.0,
                                             base=0, pattern=[[1, P]], channel_multiplier=-1))

        @block.vector
        def _(dve):
            dve.wait_ge(const_step, 2)
            nc.vector.tensor_copy(c.ident_b[:, :], c.ident[:, :])
            nc.vector.tensor_copy(c.upper_b[:, :], c.upper[:, :])
            nc.vector.tensor_copy(c.iota_b[:, :], c.iota_i[:, :])
            nc.vector.tensor_copy(c.part_f[:, :], c.part_i[:, :])


class Sender:

    BATCH = 32
    OWN = 16 * TILES // 2

    def __init__(self, nc, ctx, sorted_src):
        self.nc, self.sorted_src = nc, sorted_src
        self.src = ctx.sb("src", [P, COLS], I32)
        self.slots = ctx.sb("slots", [P, GC + COLS])
        self.dropped = ctx.sb("dropped", [P, COLS])
        self.slot_now = ctx.sb("slot_now", [P, 2, self.BATCH], I32)
        self.slot_sum = ctx.sb("slot_sum", [P, self.BATCH])
        self.src_now = ctx.sb("src_now", [P, 2, self.BATCH], I32)
        self.sent = [ctx.pool_sem("sent0"), ctx.pool_sem("sent1")]
        self.copied, self.go = ctx.pool_sem("copied"), ctx.pool_sem("go")
        self.first = 0

    def scatter(self, slots, rows):
        return self.nc.gpsimd.indirect_dma_start(
            self.sorted_src, bass.IndirectOffsetOnAxis(ap=slots, axis=0), rows, None,
            bounds_check=SLOTS - 1, oob_is_err=False)

    def send(self, pool, batches, slots_ready=None):
        n, first = self.BATCH, self.first
        with pool.Fori(0, batches // 2) as i:
            for half in range(2):
                column = i * (2 * n) + (first + half) * n
                if slots_ready is not None:
                    pool.wait_ge(slots_ready, i * (2 * n // GC) + ((first + half + 1) * (n // GC) + 2))
                pool.wait_ge(self.sent[half], i * (16 * n) + (self.OWN + first // 2 * 16 * n))
                self.nc.gpsimd.tensor_tensor(self.slot_sum[:, :], self.slots[:, bass.ds(column + GC, n)],
                                             self.dropped[:, bass.ds(column, n)], ALU.add).then_inc(self.copied, 1)
                self.nc.gpsimd.tensor_copy(self.src_now[:, half], self.src[:, bass.ds(column, n)]).then_inc(self.copied, 1)
                pool.wait_ge(self.copied, i * 6 + (3 * first + 3 * half + 1))
                pool.sem_inc(self.go, 1)
                self.nc.gpsimd.tensor_copy(self.slot_now[:, half], self.slot_sum[:, :]).then_inc(self.copied, 1)
                pool.wait_ge(self.copied, i * 6 + (3 * first + 3 * half + 3))
                pool.sem_inc(self.go, 1)
                for k in range(n):
                    self.scatter(self.slot_now[:, half, k:k + 1], self.src_now[:, half, k:k + 1]).then_inc(self.sent[half], 16)
        self.first += batches

    def share(self, batches):
        return lambda pool: self.send(pool, batches)

    def wait_all(self, pool):
        for sent in self.sent:
            pool.wait_ge(sent, self.OWN + COLS // 2 * 16)


def sort_edges(nc, c, edge_index, sorted_src, start_rows, start_i, end_i, sender, batches):
    with Stage(nc, c) as ctx:
        sb = ctx.sb
        ps = ctx.ps
        sem = ctx.sem

        dst = sb("dst", [P, COLS], I32)
        key_i = sb("key_i", [P, COLS], I32)
        row_key = sb("row_key", [P, COLS + 2 * GC], BF16)
        col_key = sb("col_key", [P, COLS + 2 * GC], BF16)
        row_hot = sb("row_hot", [P, 4, GC, P], BF16)
        col_hot = sb("col_hot", [P, 4, GC, TILES], BF16)
        row_hot_t = sb("row_hot_t", [P, 4, GC, P], BF16)
        before = sb("before", [P, 2, GC, P], BF16)
        next_slot = sb("next_slot", [P, GC, TILES], I32)
        parts = sb("parts", [P, 2, 3, GC, TILES], BF16)
        picked = sb("picked", [P, GC, TILES], F32)
        counts = sb("counts", [P, TILES], F32)
        cum = sb("cum", [P, TILES], F32)
        first = sb("first", [P, TILES], F32)
        first1 = sb("first1", [P, TILES], F32)
        own = sb("own", [P, TILES], I32)
        zero_fill = sb("zero_fill", [P, 5 * SCOLS // 4], F32)

        loaded, filled = sem("loaded"), sem("filled")
        step, hot_ready, hot_free = sem("step"), sem("hot_ready"), sem("hot_free")

        count_psum = Stage(nc, c)
        count_ps, row_ps = count_psum.ps("count_ps", [P, TILES]), count_psum.ps("row_ps", [P, 1])
        counted, summed, prefixed = sem("counted"), sem("summed"), sem("prefixed")

        def build_hot(dve, half, col, build_row=True):
            r = row_key[:, bass.ds(col, GC)].unsqueeze(2).to_broadcast([P, GC, P])
            k = col_key[:, bass.ds(col, GC)].unsqueeze(2).to_broadcast([P, GC, TILES])
            nc.vector.tensor_tensor(row_hot[:, half], r, c.iota_b[:, :].unsqueeze(1).to_broadcast([P, GC, P]), ALU.is_equal)
            nc.vector.tensor_tensor(col_hot[:, half], k, c.iota_b[:, 0:TILES].unsqueeze(1).to_broadcast([P, GC, TILES]),
                                    ALU.is_equal).then_inc(hot_ready, 1)

        with count_psum, nc.Block() as block:

            @block.sync
            def _(sp):
                sp.dma_start(dst[:, :], edge_index[1].rearrange("(p c) -> p c", p=P)).then_inc(loaded, 16)
                sp.dma_start(sender.src[:, :], edge_index[0].rearrange("(p c) -> p c", p=P)).then_inc(loaded, 16)
                sp.wait_ge(filled, 1)
                sp.dma_start(sorted_src.rearrange("(p c) o -> p (c o)", p=P), zero_fill[:, 0:SCOLS].bitcast(I32)).then_inc(filled, 16)
                for q in range(4):
                    n = 5 * SCOLS // 4
                    sp.dma_start(start_rows.rearrange("(p c) o -> p (c o)", p=P)[:, q * n:(q + 1) * n],
                                 zero_fill[:, 0:n]).then_inc(filled, 16)
                sp.wait_ge(filled, 1 + 16 * 5)

            @block.gpsimd
            def _(pool):
                nc.gpsimd.memset(zero_fill[:, :], 0.0).then_inc(filled, 1)
                nc.gpsimd.memset(parts[:, 1], 0.0)
                nc.gpsimd.memset(before[:, 1], 0.0)
                nc.gpsimd.memset(row_hot[:, 3], 0.0)
                nc.gpsimd.memset(row_hot_t[:, 3], 0.0)
                nc.gpsimd.memset(col_hot[:, 3], 0.0)
                nc.gpsimd.iota(own[:, :], [[1, TILES]], base=0, channel_multiplier=TILES)

            @block.vector
            def _(dve):
                done = Done(step)
                dve.wait_ge(loaded, 32)
                done.add(nc.vector.tensor_scalar(key_i[:, :], dst[:, :], 6, None, ALU.logical_shift_right))
                done.wait(dve)
                done.add(nc.vector.tensor_scalar(row_key[:, 0:COLS], key_i[:, :], 255.0, None, ALU.min))
                nc.vector.tensor_scalar(sender.dropped[:, :], key_i[:, :], float(P), float(DROPPED), ALU.is_ge, ALU.mult)
                done.add(nc.vector.tensor_scalar(sender.src[:, :], sender.src[:, :], float(NODES - 1), None, ALU.min))
                done.add(nc.vector.tensor_scalar(dst[:, :], dst[:, :], TILES - 1, None, ALU.bitwise_and))
                nc.vector.memset(row_key[:, COLS:COLS + 2 * GC], 255.0)
                nc.vector.memset(col_key[:, COLS:COLS + 2 * GC], 0.0)
                done.wait(dve)
                done.add(nc.vector.tensor_copy(col_key[:, 0:COLS], dst[:, :]))
                done.wait(dve)
                with dve.Fori(0, GROUPS // 2) as i:
                    for half in range(2):
                        dve.wait_ge(hot_free, 2 * i + (half + 1))
                        build_hot(dve, half, i * (2 * GC) + half * GC)
                dve.wait_ge(counted, 1)
                done.add(nc.vector.tensor_copy(counts[:, :], count_ps[:, :]))
                done.wait(dve)
                done.add(nc.vector.tensor_scalar_add(first[:, :], counts[:, :], 1.0))
                done.wait(dve)
                nc.vector.tensor_tensor_scan(cum[:, :], c.zeros[:, 0:TILES], first[:, :], 0.0, ALU.add, ALU.add).then_inc(summed, 1)
                dve.wait_ge(prefixed, 1)
                dve.wait_ge(summed, 1)
                done.add(nc.vector.tensor_tensor(first[:, :], cum[:, :], first[:, :], ALU.subtract))
                done.wait(dve)
                done.add(nc.vector.tensor_scalar(first[:, :], first[:, :], row_ps[:, 0:1], None, ALU.add))
                done.wait(dve)
                nc.vector.tensor_copy(start_i[:, :], first[:, :])
                nc.vector.tensor_scalar_add(first1[:, :], first[:, :], 1.0)
                nc.vector.tensor_tensor(end_i[:, :], first[:, :], counts[:, :], ALU.add)

            @block.tensor
            def _(pe):
                pe.sem_inc(hot_free, 2)
                nc.tensor.matmul(count_ps[:, :], c.zeros[:, 0:P], c.zeros[:, 0:TILES], start=True, stop=True)
                with pe.Fori(0, GROUPS // 2) as i:
                    for half in range(2):
                        pe.wait_ge(hot_ready, 2 * i + (half + 1))
                        for k in range(GC):
                            last = nc.tensor.matmul(count_ps[:, :], row_hot[:, half, k], col_hot[:, half, k],
                                                    start=False, stop=True, skip_group_check=True)
                        last.then_inc(hot_free, 1)
                nc.tensor.matmul(count_ps[:, :], c.zeros[:, 0:P], c.zeros[:, 0:TILES], start=False, stop=True,
                                 skip_group_check=True).then_inc(counted, 1)
                pe.wait_ge(summed, 1)
                nc.tensor.matmul(row_ps[:, :], c.upper[:, :], cum[:, TILES - 1:TILES], start=True, stop=True).then_inc(prefixed, 1)

        hot_ready2 = sem("hot_ready2")
        turned, turned_sb, same_ready, before_ready = sem("turned"), sem("turned_sb"), sem("same_ready"), sem("before_ready")
        counted2, copied, parts_ready, slots_ps_ready = sem("counted2"), sem("copied"), sem("parts_ready"), sem("slots_ps_ready")
        multiplied, slots_ready = sem("multiplied"), sem("slots_ready")
        turn_ps = ps("turn_ps", [P, GC, P], BF16)
        same_ps = ps("same_ps", [P, GC, P])
        run_ps = ps("run_ps", [P, GC, TILES])
        slots_ps = [ps(f"slots_ps{j}", [P, GC, TILES]) for j in range(2)]

        with nc.Block() as block:

            @block.vector
            def _(dve):
                def build_rows(buf, col):
                    r = row_key[:, bass.ds(col, GC)].unsqueeze(2).to_broadcast([P, GC, P])
                    nc.vector.tensor_tensor(row_hot[:, buf], r, c.iota_b[:, :].unsqueeze(1).to_broadcast([P, GC, P]),
                                            ALU.is_equal).then_inc(hot_ready2, 1)

                def build_cols(buf, col):
                    k = col_key[:, bass.ds(col, GC)].unsqueeze(2).to_broadcast([P, GC, TILES])
                    nc.vector.tensor_tensor(col_hot[:, buf], k, c.iota_b[:, 0:TILES].unsqueeze(1).to_broadcast([P, GC, TILES]),
                                            ALU.is_equal).then_inc(hot_ready2, 1)

                def multiply(buf, half, number):
                    dve.wait_ge(slots_ready, number)
                    dve.wait_ge(slots_ps_ready, number)
                    nc.vector.tensor_tensor(picked[:, :, :], slots_ps[half][:, :, :], col_hot[:, buf], ALU.mult).then_inc(multiplied, 1)

                def gather(col, number):
                    dve.wait_ge(multiplied, number)
                    nc.vector.tensor_reduce(sender.slots[:, bass.ds(col, GC)], picked[:, :, :], AX.X, ALU.add).then_inc(slots_ready, 1)

                dve.sem_inc(slots_ready, 1)
                for u in range(2):
                    build_rows(u, u * GC)
                    build_cols(u, u * GC)
                with dve.Fori(0, GROUPS // 4) as i:
                    for u in range(4):
                        g1 = 4 * i + (u + 1)
                        dve.wait_ge(same_ready, g1)
                        nc.vector.tensor_tensor(before[:, u % 2], same_ps[:, :, :],
                                                c.upper_b[:, :].unsqueeze(1).to_broadcast([P, GC, P]),
                                                ALU.mult).then_inc(before_ready, 1)
                        build_rows((u + 2) % 4, i * (4 * GC) + (u + 2) * GC)
                        multiply((u + 3) % 4, (u + 1) % 2, g1)
                        build_cols((u + 2) % 4, i * (4 * GC) + (u + 2) * GC)
                        gather(i * (4 * GC) + u * GC, g1)
                multiply(3, 1, GROUPS + 1)
                gather(COLS, GROUPS + 1)

            @block.tensor
            def _(pe):
                def turn(buf):
                    for k in range(GC):
                        last = nc.tensor.transpose(turn_ps[:, k], row_hot[:, buf, k], c.ident_b[:, :])
                    last.then_inc(turned, 1)

                def slots(half, buf):
                    for k in range(GC):
                        for byte in range(3):
                            nc.tensor.matmul(slots_ps[half][:, k], row_hot_t[:, buf, k], parts[:, half, byte, k],
                                             start=(byte == 0), stop=False)
                        last = nc.tensor.matmul(slots_ps[half][:, k], before[:, half, k], col_hot[:, buf, k], start=False, stop=True)
                    last.then_inc(slots_ps_ready, 1)

                def count(buf, k, a, b):
                    return nc.tensor.matmul(run_ps[:, a:b], row_hot[:, buf, k],
                                            col_hot[:, buf, k].unsqueeze(1).to_broadcast([P, b - a, TILES]),
                                            start=False, stop=True, skip_group_check=True)

                nc.tensor.matmul(run_ps[:, :, :], c.ident[:, :], first1[:, :].unsqueeze(1).to_broadcast([P, GC, TILES]),
                                 start=True, stop=True)
                pe.wait_ge(hot_ready2, 2)
                turn(0)
                with pe.Fori(0, GROUPS // 4) as i:
                    for u in range(4):
                        g1 = 4 * i + (u + 1)
                        pe.wait_ge(turned_sb, g1)
                        pe.wait_ge(before_ready, g1)
                        for k in range(GC):
                            last = nc.tensor.matmul(same_ps[:, k], row_hot_t[:, u, k], row_hot_t[:, u, k], start=True, stop=True)
                        last.then_inc(same_ready, 1)
                        pe.wait_ge(copied, g1)
                        for k in range(GC):
                            count((u + 3) % 4, k, 0, k + 1)
                        for k in range(GC - 1):
                            last = count(u, k, k + 1, GC)
                        last.then_inc(counted2, 1)
                        pe.wait_ge(hot_ready2, i * 8 + (2 * u + 4))
                        turn((u + 1) % 4)
                        pe.wait_ge(parts_ready, i * 12 + (3 * u + 3))
                        slots((u + 1) % 2, (u + 3) % 4)
                pe.wait_ge(before_ready, GROUPS + 1)
                pe.wait_ge(parts_ready, 3 * GROUPS + 3)
                slots(1, 3)

            @block.scalar
            def _(act):
                act.sem_inc(before_ready, 1)
                act.sem_inc(copied, 1)
                act.sem_inc(parts_ready, 3)
                act.wait_ge(turned, 1)
                nc.scalar.copy(row_hot_t[:, 0], turn_ps[:, :, :]).then_inc(turned_sb, 1)
                with act.Fori(0, GROUPS // 4) as i:
                    for u in range(4):
                        act.wait_ge(counted2, 4 * i + (u + 1))
                        act.wait_ge(parts_ready, i * 12 + (3 * u + 3))
                        nc.scalar.copy(next_slot[:, :, :], run_ps[:, :, :]).then_inc(copied, 1)
                        act.wait_ge(turned, 4 * i + (u + 2))
                        nc.scalar.copy(row_hot_t[:, (u + 1) % 4], turn_ps[:, :, :]).then_inc(turned_sb, 1)
                        act.wait_ge(copied, 4 * i + (u + 2))
                        for byte in range(3):
                            nc.scalar.activation(parts[:, u % 2, byte], next_slot[:, :, :].bitcast(U8)[:, :, byte::4],
                                                 ACT.Copy, scale=float(256 ** byte)).then_inc(parts_ready, 1)

            @block.gpsimd
            def _(pool):
                for t in range(TILES):
                    sender.scatter(start_i[:, t:t + 1], own[:, t:t + 1]).then_inc(sender.sent[t % 2], 16)
                sender.send(pool, batches, slots_ready)


VOCAB, HEADS0, KEYS = 256, 8, 255
EPS = 1e-5


def load_all(engine, pairs, sem):
    for tile, array in pairs:
        engine.dma_start(tile, array).then_inc(sem, 16)


def on_every_partition(array, n):
    return array.rearrange("(o n) -> o n", o=1).to_broadcast([P, n])


class Norm:

    def __init__(self, nc, ctx, name, T, n):
        self.nc, self.T, self.n = nc, T, n
        self.mean = ctx.sb(name + "_mean", [P, T])
        self.var = ctx.sb(name + "_var", [P, T])
        self.std = ctx.sb(name + "_std", [P, T])
        self.inv = ctx.sb(name + "_inv", [P, T])
        self.var_ready = ctx.sem(name + "_var_ready")
        self.std_ready = ctx.sem(name + "_std_ready")

    def wide(self, stat):
        return stat[:, :].unsqueeze(2).to_broadcast([P, self.T, self.n])

    def centre(self, dve, done, x, centred, square):
        v = self.nc.vector
        done.add(v.tensor_reduce(self.mean[:, :], x, AX.X, ALU.add))
        done.wait(dve)
        done.add(v.tensor_scalar_mul(self.mean[:, :], self.mean[:, :], 1.0 / self.n))
        done.wait(dve)
        done.add(v.tensor_tensor(centred, x, self.wide(self.mean), ALU.subtract))
        done.wait(dve)
        done.add(v.tensor_tensor(square, centred, centred, ALU.mult))
        done.wait(dve)
        done.add(v.tensor_reduce(self.var[:, :], square, AX.X, ALU.add))
        done.wait(dve)
        v.tensor_scalar(self.var[:, :], self.var[:, :], 1.0 / self.n, EPS, ALU.mult, ALU.add).then_inc(self.var_ready, 1)
        dve.wait_ge(self.std_ready, 1)
        done.add(v.reciprocal(self.inv[:, :], self.std[:, :]))
        done.wait(dve)

    def root(self, act):
        act.wait_ge(self.var_ready, 1)
        self.nc.scalar.activation(self.std[:, :], self.var[:, :], ACT.Sqrt).then_inc(self.std_ready, 1)


def token_tables(nc, c, w, tab_h, tab_x, tab_xt, meanwhile=None):
    with Stage(nc, c) as ctx:
        sb = ctx.sb
        sem = ctx.sem

        emb_t, w1_t, b1 = sb("emb_t", [D, VOCAB]), sb("w1_t", [D, D]), sb("b1", [D, 1])
        w2_t, gamma, beta = sb("w2_t", [D + 1, D]), sb("gamma", [P, D]), sb("beta", [P, D])
        hid = sb("hid", [D + 1, VOCAB])
        centred, square = sb("centred", [P, 2, D]), sb("square", [P, 2, D])
        hid_ps = ctx.ps("hid_ps", [D, VOCAB])
        out_ps = ctx.ps("out_ps", [P, 2, D])
        xt_ps = ctx.ps("xt_ps", [D, VOCAB])
        loaded, hid_done, act_done, out_done, x_done, xt_done, step = map(
            sem, ("loaded", "hid_done", "act_done", "out_done", "x_done", "xt_done", "step"))
        n1, n2 = Norm(nc, ctx, "n1", 2, D), Norm(nc, ctx, "n2", 2, D)
        with nc.Block() as block:
            if meanwhile:

                @block.gpsimd
                def _(pool):
                    meanwhile(pool)

            @block.sync
            def _(sp):
                load_all(sp, [(emb_t[:, :], w["emb_t"]), (w1_t[:, :], w["tok_w1_t"]), (b1[:, :], w["tok_b1"]),
                              (w2_t[:, :], w["tok_w2_t"]), (gamma[:, :], on_every_partition(w["tok_gamma"], D)),
                              (beta[:, :], on_every_partition(w["tok_beta"], D))], loaded)

            @block.tensor
            def _(pe):
                pe.wait_ge(loaded, 16 * 6)
                nc.tensor.matmul(hid_ps[:, :], w1_t[:, :], emb_t[:, :], start=True, stop=True).then_inc(hid_done, 1)
                pe.wait_ge(act_done, 2)
                for j in range(2):
                    last = nc.tensor.matmul(out_ps[:, j], hid[:, j * P:(j + 1) * P], w2_t[:, :], start=True, stop=True)
                last.then_inc(out_done, 1)
                pe.wait_ge(x_done, 1)
                for j in range(2):
                    last = nc.tensor.transpose(xt_ps[:, j * P:(j + 1) * P], tab_x[:, j], c.ident[:, :])
                last.then_inc(xt_done, 1)

            @block.scalar
            def _(act):
                act.wait_ge(loaded, 16 * 6)
                act.wait_ge(hid_done, 1)
                nc.scalar.activation(hid[0:D, :], hid_ps[:, :], ACT.Relu, bias=b1[:, 0:1]).then_inc(act_done, 1)
                n1.root(act)
                n2.root(act)

            @block.vector
            def _(dve):
                done = Done(step)
                nc.vector.memset(tab_xt[D:D + 1, :], 1.0)
                nc.vector.memset(hid[D:D + 1, :], 1.0).then_inc(act_done, 1)
                dve.wait_ge(loaded, 16 * 6)
                dve.wait_ge(out_done, 1)
                n1.centre(dve, done, out_ps[:, :, :], centred[:, :, :], square[:, :, :])
                done.add(nc.vector.tensor_tensor(centred[:, :, :], centred[:, :, :], n1.wide(n1.inv), ALU.mult))
                done.wait(dve)
                done.add(nc.vector.tensor_tensor(centred[:, :, :], centred[:, :, :],
                                                 gamma[:, :].unsqueeze(1).to_broadcast([P, 2, D]), ALU.mult))
                done.wait(dve)
                done.add(nc.vector.tensor_tensor(tab_h[:, :, :], centred[:, :, :],
                                                 beta[:, :].unsqueeze(1).to_broadcast([P, 2, D]), ALU.add))
                done.wait(dve)
                n2.centre(dve, done, tab_h[:, :, :], centred[:, :, :], square[:, :, :])
                nc.vector.tensor_tensor(tab_x[:, :, :], centred[:, :, :], n2.wide(n2.inv), ALU.mult).then_inc(x_done, 1)
                dve.wait_ge(xt_done, 1)
                nc.vector.tensor_copy(tab_xt[0:D, :], xt_ps[:, :])


def word_attention(nc, c, w, h, tab_h, tab_x, tab_xt, words, chosen, chosen_table, plain_table, meanwhile=None):
    HALF, BLOCKS, PAIRS = 64, VOCAB // 64, HEADS0 // 2
    with Stage(nc, c) as ctx:
        sb = ctx.sb
        ps = ctx.ps
        sem = ctx.sem

        wq_t, wv_t = sb("wq_t", [D + 1, PAIRS, 2, D]), sb("wv_t", [D + 1, PAIRS, 2, D])
        wk, fan_t, fan_b = sb("wk", [P, PAIRS]), sb("fan_t", [D + 1, D]), sb("fan_b", [P, D])
        query = sb("query", [P, PAIRS, VOCAB])
        key = sb("key", [P, PAIRS, VOCAB])
        value = sb("value", [P, BLOCKS, PAIRS, D])
        count = sb("count", [P, BLOCKS, BATCH])
        match, negkey = sb("match", [P, SEQ]), sb("negkey", [P, SEQ])
        block_word_i, block_word = sb("block_word_i", [P, BLOCKS], I32), sb("block_word", [P, BLOCKS])
        weighed = sb("weighed", [P, BLOCKS, PAIRS, BATCH, D])
        twice = sb("twice", [D, 2, D])
        pick = sb("pick", [P, 3 * HALF - 1])
        minus_half = sb("minus_half", [P, 2, HALF])
        key_sum = sb("key_sum", [P, PAIRS, BLOCKS])
        gap = sb("gap", [P, 8, VOCAB])
        e = h[:, :, :].rearrange("p t d -> p (t d)").rearrange("p (b a v) -> p b a v", b=BLOCKS, a=PAIRS)
        den, total = sb("den", [P, BATCH]), sb("total", [P, 2, BATCH, D])
        part = sb("part", [P, BATCH, D])
        gate = sb("gate", [P, 2, BATCH, D])
        mixed_t = sb("mixed_t", [D + 1, 2, BATCH, P])
        base = sb("base", [P, 2, D])
        q_ps, k_ps = [ps(f"q_ps{j}", [P, 2, VOCAB]) for j in range(2)], ps("k_ps", [P, VOCAB])
        v_ps = ps("v_ps", [P, PAIRS, D])
        dist_ps = [ps(f"dist_ps{j}", [P, VOCAB]) for j in range(2)]
        num_ps, den_ps = ps("num_ps", [P, BATCH, D]), ps("den_ps", [P, BATCH])
        loaded, consts, picked, q_done, q_read, k_done, v_done, v_read = map(
            sem, ("loaded", "consts", "picked", "q_done", "q_read", "k_done", "v_done", "v_read"))
        keys_ready, gap_v, gap_s, gap_free, dist_read = map(
            sem, ("keys_ready", "gap_v", "gap_s", "gap_free", "dist_read"))
        weighed_ready, num_done, num_read, gate_in, gate_out, turn_in, turn_out, step, astep = map(
            sem, ("weighed_ready", "num_done", "num_read", "gate_in", "gate_out", "turn_in", "turn_out", "step",
                  "astep"))

        with nc.Block() as block:

            @block.sync
            def _(sp):
                load_all(sp, [(wq_t[:, :, :, :], w["wq_t"].rearrange("i (a h o) -> i a h o", a=PAIRS, h=2)),
                              (wv_t[:, :, :, :], w["wv_t"].rearrange("i (a h o) -> i a h o", a=PAIRS, h=2)),
                              (wk[:, :], w["wk_pairs"]), (fan_t[:, :], w["fan_t"]),
                              (fan_b[:, :], w["fan_t"][D:D + 1, :].to_broadcast([P, D]))], loaded)

            @block.gpsimd
            def _(pool):
                nc.gpsimd.memset(pick[:, :], 0.0)
                nc.gpsimd.iota(block_word_i[:, :], [[HALF, BLOCKS]], base=0, channel_multiplier=1).then_inc(consts, 1)
                meanwhile(pool)

            @block.tensor
            def _(pe):
                pe.wait_ge(loaded, 16 * 5)
                pe.wait_ge(picked, 1)
                for a in range(PAIRS):
                    if a >= 2:
                        pe.wait_ge(q_read, a - 1)
                    nc.tensor.matmul(q_ps[a % 2][:, 0], wq_t[:, a], tab_xt[:, :], start=True, stop=True).then_inc(q_done, 1)
                nc.tensor.matmul(k_ps[:, :], twice[:, :, :], tab_xt[0:D, :], start=True, stop=True).then_inc(k_done, 1)
                for b in range(BLOCKS):
                    if b:
                        pe.wait_ge(v_read, b)
                    for h in range(2):
                        last = nc.tensor.matmul(v_ps[h * HALF:(h + 1) * HALF], tab_xt[:, b * HALF:(b + 1) * HALF],
                                                wv_t[:, :, h], start=True, stop=True)
                    last.then_inc(v_done, 1)
                pe.wait_ge(keys_ready, 1)
                for a in range(PAIRS):
                    for b in range(BLOCKS):
                        for h in range(2):
                            r = slice(h * HALF, (h + 1) * HALF)
                            last = nc.tensor.matmul(k_ps[r, a * BLOCKS + b:a * BLOCKS + b + 1], key[r, a, b * HALF:(b + 1) * HALF],
                                                    c.ones[r, 0:1], start=True, stop=True)
                last.then_inc(k_done, 1)
                pe.sem_inc(gap_free, 8)
                with pe.Fori(0, PAIRS) as a, pe.Fori(0, BLOCKS // 2) as j:
                    i = a * 2 + j
                    for half in range(2):
                        pe.wait_ge(dist_read, 2 * i + (half + 1))
                        nc.tensor.matmul(dist_ps[half][:, :], minus_half[:, :, :], query[:, bass.ds(a, 1)].squeeze(1), start=True, stop=False)
                        for u in range(HALF):
                            if u % 8 < 5:
                                pe.wait_ge(gap_v, i * (2 * 40) + (half * 40 + u // 8 * 5 + u % 8 + 1))
                            else:
                                pe.wait_ge(gap_s, i * (2 * 24) + (half * 24 + u // 8 * 3 + u % 8 - 4))
                            last = nc.tensor.matmul(dist_ps[half][:, :], pick[:, HALF - 1 - u:3 * HALF - 1 - u], gap[:, u % 8],
                                                    start=False, stop=(u == HALF - 1))
                            last.then_inc(gap_free, 1)
                pe.wait_ge(weighed_ready, 1)
                pe.wait_ge(dist_read, 2 + BLOCKS * PAIRS)
                n = 0
                for dh in range(2):
                    for a in range(PAIRS):
                        for h in range(2):
                            if n:
                                pe.wait_ge(num_read, n)
                            r = slice(h * HALF, (h + 1) * HALF)
                            for b in range(BLOCKS):
                                nc.tensor.matmul(num_ps[:, :, :], e[r, b, a, dh * P:(dh + 1) * P], weighed[r, b, a],
                                                 start=(b == 0), stop=(b == BLOCKS - 1))
                            for b in range(BLOCKS):
                                last = nc.tensor.matmul(den_ps[:, :], e[r, b, a, dh * P:(dh + 1) * P], count[r, b],
                                                        start=(b == 0), stop=(b == BLOCKS - 1))
                            last.then_inc(num_done, 1)
                            n += 1
                pe.wait_ge(turn_in, 1)
                for n in range(2 * BATCH // 4):
                    if n >= 2:
                        pe.wait_ge(turn_out, n - 1)
                    for k in range(4):
                        m = 4 * n + k
                        last = nc.tensor.transpose(q_ps[n % 2][0:D, k // 2, (k % 2) * P:(k % 2 + 1) * P], gate[:, m // BATCH, m % BATCH], c.ident[:, :])
                    last.then_inc(q_done, 1)
                pe.wait_ge(turn_out, 2 * BATCH // 4)
                for dh in range(2):
                    pe.wait_ge(num_read, 2 * HEADS0 + dh)
                    for b in range(BATCH):
                        last = nc.tensor.matmul(num_ps[:, b], mixed_t[:, dh, b], fan_t[:, :], start=True, stop=True)
                    last.then_inc(num_done, 1)

            @block.vector
            def _(dve):
                done = Done(step)
                dve.wait_ge(loaded, 16 * 5)
                dve.wait_ge(consts, 1)
                done.add(nc.vector.tensor_copy(block_word[:, :], block_word_i[:, :]))
                nc.vector.memset(mixed_t[D:D + 1, :, :, :], 1.0)
                for h in range(2):
                    nc.vector.memset(minus_half[h * HALF:(h + 1) * HALF, h], -0.5)
                    nc.vector.memset(minus_half[h * HALF:(h + 1) * HALF, 1 - h], 0.0)
                    nc.vector.memset(pick[h * HALF:(h + 1) * HALF, (h + 1) * HALF - 1:(h + 1) * HALF], 1.0)
                    last = nc.vector.tensor_copy(twice[:, h], c.ident[0:D, 0:D])
                last.then_inc(picked, 1)
                done.wait(dve)
                done.add(nc.vector.tensor_scalar_add(block_word[HALF:P, :], block_word[HALF:P, :], float(-HALF)))
                for a in range(PAIRS):
                    dve.wait_ge(q_done, a + 1)
                    nc.vector.tensor_copy(query[:, a], q_ps[a % 2][:, 0]).then_inc(q_read, 1)
                dve.wait_ge(k_done, 1)
                for a in range(PAIRS):
                    last = nc.vector.tensor_scalar(key[:, a], k_ps[:, :], wk[:, a:a + 1], None, ALU.mult)
                last.then_inc(keys_ready, 1)
                for b in range(BLOCKS):
                    dve.wait_ge(v_done, b + 1)
                    nc.vector.tensor_copy(value[:, b], v_ps[:, :, :]).then_inc(v_read, 1)
                dve.wait_ge(keys_ready, 1)
                dve.wait_ge(k_done, 2)
                nc.vector.tensor_scalar_mul(key_sum[:, :, :], k_ps[:, 0:PAIRS * BLOCKS].rearrange("p (a b) -> p a b", a=PAIRS),
                                            -1.0 / D ** 0.5).then_inc(keys_ready, 1)
                with dve.Fori(0, PAIRS) as a, dve.Fori(0, BLOCKS // 2) as j:
                    i = a * 2 + j
                    for half in range(2):
                        for u in range(HALF):
                            if u % 8 < 5:
                                dve.wait_ge(gap_free, i * (2 * HALF) + (half * HALF + u + 1))
                                nc.vector.tensor_scalar(gap[:, u % 8], query[:, bass.ds(a, 1)].squeeze(1),
                                                        key[:, :, :].rearrange("p a u -> p (a u)")[:, bass.ds(i * (2 * HALF) + (half * HALF + u), 1)],
                                                        0.0, ALU.subtract, ALU.max).then_inc(gap_v, 1)
                for b in range(BLOCKS):
                    for s in range(BATCH):
                        done.wait(dve)
                        done.add(nc.vector.scalar_tensor_tensor(
                            match[:, :], words[:, s * SEQ:(s + 1) * SEQ], block_word[:, b:b + 1], chosen[:, :],
                            ALU.is_equal, ALU.mult, accum_out=count[:, b, s:s + 1]))
                done.wait(dve)
                for b in range(BLOCKS):
                    for a in range(PAIRS):
                        last = nc.vector.tensor_tensor(weighed[:, b, a], count[:, b].unsqueeze(2).to_broadcast([P, BATCH, D]),
                                                       value[:, b, a].unsqueeze(1).to_broadcast([P, BATCH, D]), ALU.mult)
                last.then_inc(weighed_ready, 1)
                n = 0
                for dh in range(2):
                    done.add(nc.vector.memset(total[:, dh], 0.0))
                    for a in range(HEADS0):
                        dve.wait_ge(num_done, n + 1)
                        done.add(nc.vector.tensor_scalar_add(den[:, :], den_ps[:, :], 1.0))
                        done.wait(dve)
                        done.add(nc.vector.reciprocal(den[:, :], den[:, :]))
                        done.wait(dve)
                        nc.vector.tensor_tensor(part[:, :, :], num_ps[:, :, :], den[:, :].unsqueeze(2).to_broadcast([P, BATCH, D]),
                                                ALU.mult).then_inc(num_read, 1)
                        dve.wait_ge(num_read, n + 1)
                        done.add(nc.vector.tensor_tensor(total[:, dh], total[:, dh], part[:, :, :], ALU.add))
                        done.wait(dve)
                        n += 1
                nc.vector.sem_inc(gate_in, 1)
                dve.wait_ge(gate_out, 1)
                done.add(nc.vector.tensor_scalar_add(gate[:, :, :, :], gate[:, :, :, :], 1.0))
                done.wait(dve)
                done.add(nc.vector.reciprocal(gate[:, :, :, :], gate[:, :, :, :]))
                done.wait(dve)
                nc.vector.tensor_tensor(gate[:, :, :, :], gate[:, :, :, :], total[:, :, :, :], ALU.mult).then_inc(turn_in, 1)
                for n in range(2 * BATCH // 4):
                    dve.wait_ge(q_done, PAIRS + n + 1)
                    nc.vector.tensor_copy(mixed_t[0:D, n // 2, (n % 2) * 4:(n % 2) * 4 + 4],
                                          q_ps[n % 2][0:D].rearrange("d a (k p) -> d (a k) p", k=2)).then_inc(turn_out, 1)
                done.add(nc.vector.tensor_tensor(base[:, :, :], tab_h[:, :, :], tab_x[:, :, :], ALU.add))
                done.wait(dve)
                nc.vector.tensor_tensor(plain_table[:, :, :], base[:, :, :], fan_b[:, :].unsqueeze(1).to_broadcast([P, 2, D]), ALU.add)
                for dh in range(2):
                    dve.wait_ge(num_done, 2 * HEADS0 + dh + 1)
                    nc.vector.tensor_tensor(chosen_table[:, dh], num_ps[:, :, :], base[:, dh].unsqueeze(1).to_broadcast([P, BATCH, D]),
                                            ALU.add).then_inc(num_read, 1)

            @block.scalar
            def _(act):
                act.wait_ge(keys_ready, 2)
                nc.scalar.mul(negkey[:, :], key[:, :, :].rearrange("p a u -> p (a u)"), -1.0).then_inc(astep, 1)
                act.wait_ge(astep, 1)
                act.sem_inc(dist_read, 2)
                with act.Fori(0, PAIRS) as a, act.Fori(0, BLOCKS // 2) as j:
                    i = a * 2 + j
                    for half in range(2):
                        for u in range(HALF):
                            if u % 8 >= 5:
                                act.wait_ge(gap_free, i * (2 * HALF) + (half * HALF + u + 1))
                                nc.scalar.activation(gap[:, u % 8], query[:, bass.ds(a, 1)].squeeze(1), ACT.Relu,
                                                     bias=negkey[:, bass.ds(i * (2 * HALF) + (half * HALF + u), 1)]).then_inc(gap_s, 1)
                        act.wait_ge(gap_free, i * (2 * HALF) + (8 + (half + 1) * HALF))
                        nc.scalar.activation(e[:, :, :, :].rearrange("p b a v -> p (b a) v")[:, bass.ds(j * (2 * PAIRS) + (a + half * PAIRS), 1)].squeeze(1),
                                             dist_ps[half][:, :], ACT.Exp, scale=-2.0 / D ** 0.5,
                                             bias=key_sum[:, :, :].rearrange("p a b -> p (a b)")[:, bass.ds(2 * i + half, 1)]).then_inc(dist_read, 1)
                act.wait_ge(gate_in, 1)
                nc.scalar.activation(gate[:, :, :, :], total[:, :, :, :], ACT.Exp, scale=-1.702).then_inc(gate_out, 1)


def load_words(nc, c, w, words, chosen, meanwhile=None):
    with Stage(nc, c) as ctx:
        sb = ctx.sb

        words_i = sb("words_i", [P, NODES], I32)
        named_i, named = sb("named_i", [P, 2], I32), sb("named", [P, 2])
        place_i, place = sb("place_i", [P, SEQ], I32), sb("place", [P, SEQ])
        names = sb("names", [P, 2, SEQ], BF16)
        ones_b = sb("ones_b", [P, P], BF16)
        count_ps = ctx.ps("named_ps", [P, 2, SEQ // 2])
        loaded, made, named_loaded, names_ready, counted, step = (
            ctx.sem(n) for n in ("loaded", "made", "named_loaded", "names_ready", "counted", "step"))
        with nc.Block() as block:

            @block.gpsimd
            def _(pool):
                nc.gpsimd.iota(place_i[:, :], [[1, SEQ]], base=0, channel_multiplier=0)
                nc.gpsimd.memset(named_i[:, :], -1).then_inc(made, 1)
                meanwhile(pool)

            @block.sync
            def _(sp):
                sp.dma_start(words_i[:, :], on_every_partition(w["tokens"], NODES)).then_inc(loaded, 16)
                sp.wait_ge(made, 1)
                with nc.allow_non_contiguous_dma(reason="255 words"):
                    sp.dma_start(named_i[:, 0:1], w["a2a"][0:P].rearrange("(p o) -> p o", o=1)).then_inc(named_loaded, 16)
                    sp.dma_start(named_i[0:KEYS - P, 1:2], w["a2a"][P:KEYS].rearrange("(p o) -> p o", o=1)).then_inc(named_loaded, 16)

            @block.vector
            def _(dve):
                done = Done(step)
                nc.vector.memset(ones_b[:, :], 1.0)
                dve.wait_ge(named_loaded, 32)
                nc.vector.tensor_copy(named[:, :], named_i[:, :])
                done.add(nc.vector.tensor_copy(place[:, :], place_i[:, :]))
                done.wait(dve)
                for j in range(2):
                    last = nc.vector.tensor_scalar(names[:, j], place[:, :], named[:, j:j + 1], None, ALU.is_equal)
                last.then_inc(names_ready, 1)
                dve.wait_ge(counted, 1)
                nc.vector.tensor_copy(chosen[:, :].rearrange("p (a n) -> p a n", a=2), count_ps[:, :, :])
                dve.wait_ge(loaded, 16)
                nc.vector.tensor_copy(words[:, :], words_i[:, :])

            @block.tensor
            def _(pe):
                pe.wait_ge(names_ready, 1)
                for q in range(2):
                    for j in range(2):
                        last = nc.tensor.matmul(count_ps[:, q], ones_b[:, :], names[:, j, q * (SEQ // 2):(q + 1) * (SEQ // 2)],
                                                start=(j == 0), stop=(j == 1))
                last.then_inc(counted, 1)


def look_up(nc, c, words, chosen, chosen_table, plain_table, node_t, meanwhile=None):
    HALF = SEQ // 2
    with Stage(nc, c) as ctx:
        sb = ctx.sb

        is_named, not_named = sb("is_named", [P, SEQ]), sb("not_named", [P, SEQ])
        named_word, plain_word = sb("named_word", [P, SEQ]), sb("plain_word", [P, SEQ])
        hot = sb("hot", [P, 2, 2, 2, HALF])
        node_ps = [ctx.ps(f"node_ps{j}", [D, HALF]) for j in range(2)]
        step, hot_ready, hot_used, copied = (
            ctx.sem(n) for n in ("step", "hot_ready", "hot_used", "copied"))
        with nc.Block() as block:
            if meanwhile:

                @block.gpsimd
                def _(pool):
                    meanwhile(pool)

            @block.vector
            def _(dve):
                done = Done(step)
                done.add(nc.vector.tensor_scalar(is_named[:, :], chosen[:, :], 1.0, None, ALU.min))
                done.wait(dve)
                done.add(nc.vector.tensor_scalar(not_named[:, :], is_named[:, :], -1.0, 1.0, ALU.mult, ALU.add))
                done.wait(dve)
                for s in range(BATCH):
                    x = words[:, s * SEQ:(s + 1) * SEQ]
                    if s:
                        dve.wait_ge(hot_ready, 2 * s)
                    for out, mask in ((named_word, is_named), (plain_word, not_named)):
                        done.add(nc.vector.scalar_tensor_tensor(out[:, :], x, 1.0, mask[:, :], ALU.add, ALU.mult))
                    done.wait(dve)
                    for out in (named_word, plain_word):
                        done.add(nc.vector.tensor_scalar_add(out[:, :], out[:, :], -1.0))
                    done.wait(dve)
                    for half in range(2):
                        if s:
                            dve.wait_ge(hot_used, 2 * (s - 1) + half + 1)
                        for kind, out in enumerate((named_word, plain_word)):
                            for j in range(2):
                                last = nc.vector.tensor_scalar(hot[:, half, kind, j], out[:, half * HALF:(half + 1) * HALF],
                                                               c.part_f[:, j:j + 1], None, ALU.is_equal)
                        last.then_inc(hot_ready, 1)

            @block.tensor
            def _(pe):
                for s in range(BATCH):
                    for half in range(2):
                        pe.wait_ge(hot_ready, 2 * s + half + 1)
                        if s:
                            pe.wait_ge(copied, 2 * (s - 1) + half + 1)
                        for j in range(2):
                            nc.tensor.matmul(node_ps[half][:, :], chosen_table[:, j, s], hot[:, half, 0, j], start=(j == 0), stop=False)
                        for j in range(2):
                            last = nc.tensor.matmul(node_ps[half][:, :], plain_table[:, j], hot[:, half, 1, j], start=False, stop=(j == 1))
                        last.then_inc(hot_used, 1)

            @block.scalar
            def _(act):
                for s in range(BATCH):
                    for half in range(2):
                        act.wait_ge(hot_used, 2 * s + half + 1)
                        nc.scalar.copy(node_t[:, s * SEQ + half * HALF:s * SEQ + (half + 1) * HALF], node_ps[half][:, :]).then_inc(copied, 1)


def to_nodes(nc, c, node_t, h, add, meanwhile=None):
    T4 = 4
    with Stage(nc, c) as ctx:
        stage = ctx.sb("stage", [D, 2, T4, P])
        turn_ps = [ctx.ps(f"turn_ps{j}", [P, T4, D]) for j in range(2)]
        staged, turned, read, go = (ctx.sem(n) for n in ("staged", "turned", "read", "go"))
        by_tile = node_t.rearrange("d (p t) -> d t p", t=TILES)
        with nc.Block() as block:
            if meanwhile:

                @block.gpsimd
                def _(pool):
                    meanwhile(pool)

            @block.scalar
            def _(act):
                act.sem_inc(turned, 2)
                with act.Fori(0, TILES // T4 // 2) as i:
                    for half in range(2):
                        act.wait_ge(turned, 2 * i + (half + 1))
                        nc.scalar.copy(stage[:, half], by_tile[:, bass.ds(i * (2 * T4) + half * T4, T4)]).then_inc(staged, 1)

            @block.tensor
            def _(pe):
                with pe.Fori(0, TILES // T4 // 2) as i:
                    for half in range(2):
                        pe.wait_ge(staged, 2 * i + (half + 1))
                        pe.wait_ge(read, 2 * i + (half + 1))
                        pe.sem_inc(go, 1)
                        for k in range(T4):
                            last = nc.tensor.transpose(turn_ps[half][:, k], stage[:, half, k], c.ident[0:D, 0:D])
                        last.then_inc(turned, 1)

            @block.vector
            def _(dve):
                dve.sem_inc(read, 2)
                with dve.Fori(0, TILES // T4 // 2) as i:
                    for half in range(2):
                        dve.wait_ge(turned, 2 * i + (half + 3))
                        rows = h[:, bass.ds(i * (2 * T4) + half * T4, T4)]
                        if add:
                            nc.vector.tensor_tensor(rows, turn_ps[half][:, :, :], rows, ALU.add).then_inc(read, 1)
                        else:
                            nc.vector.tensor_copy(rows, turn_ps[half][:, :, :]).then_inc(read, 1)


EXPERTS = 8
T4 = 4


def norm_project(nc, c, h, x_t, weight, proj, add_back=False, meanwhile=None):
    with Stage(nc, c) as ctx:
        sb = ctx.sb

        n = 0 if proj is None else proj.shape[2]
        centred, square = sb("centred", [P, TILES, D]), sb("square", [P, TILES, D])
        stage, stage_t = sb("stage", [P, 2, T4, D]), sb("stage_t", [D, 2, T4, P])
        w_sb = sb("w_sb", [D, max(n, 1)])
        turn_ps = [ctx.ps(f"turn_ps{j}", [D, T4, P]) for j in range(2)]
        proj_ps = [ctx.ps(f"proj_ps{j}", [P, T4, max(n, 1)]) for j in range(2)]
        loaded, step, staged, turned, added, staged_t, copied, projected, read, go = (
            ctx.sem(s) for s in
            ("loaded", "step", "staged", "turned", "added", "staged_t", "copied", "projected", "read", "go"))
        norm = Norm(nc, ctx, "norm", TILES, D)
        LOOPS = TILES // T4 // 2
        with nc.Block() as block:
            if meanwhile:

                @block.gpsimd
                def _(pool):
                    meanwhile(pool)

            @block.sync
            def _(sp):
                if n:
                    sp.dma_start(w_sb[:, :], weight).then_inc(loaded, 16)

            @block.vector
            def _(dve):
                done = Done(step)
                norm.centre(dve, done, h[:, :, :], centred[:, :, :], square[:, :, :])
                dve.sem_inc(turned, 2)
                dve.sem_inc(added, 2)
                with dve.Fori(0, LOOPS) as i:
                    for half in range(2):
                        tiles = bass.ds(i * (2 * T4) + half * T4, T4)
                        dve.wait_ge(turned, 2 * i + (half + 1))
                        if add_back:
                            dve.wait_ge(added, 2 * i + (half + 1))
                        nc.vector.tensor_tensor(stage[:, half], centred[:, tiles],
                                                norm.inv[:, tiles].unsqueeze(2).to_broadcast([P, T4, D]), ALU.mult).then_inc(staged, 1)
                        if add_back:
                            dve.wait_ge(staged, 2 * i + (half + 1))
                            nc.vector.tensor_tensor(h[:, tiles], h[:, tiles], stage[:, half], ALU.add).then_inc(added, 1)
                        if n:
                            dve.wait_ge(projected, 2 * i + (half + 1))
                            nc.vector.tensor_copy(proj[:, tiles], proj_ps[half][:, :, :]).then_inc(read, 1)

            @block.tensor
            def _(pe):
                pe.sem_inc(copied, 2)
                pe.sem_inc(read, 2)
                if n:
                    pe.wait_ge(loaded, 16)
                with pe.Fori(0, LOOPS) as i:
                    for half in range(2):
                        pe.wait_ge(staged, 2 * i + (half + 1))
                        pe.wait_ge(copied, 2 * i + (half + 1))
                        pe.sem_inc(go, 1)
                        for k in range(T4):
                            last = nc.tensor.transpose(turn_ps[half][:, k], stage[:, half, k], c.ident[:, :])
                        last.then_inc(turned, 1)
                        if n:
                            pe.wait_ge(staged_t, 2 * i + (half + 1))
                            pe.wait_ge(read, 2 * i + (half + 1))
                            for k in range(T4):
                                last = nc.tensor.matmul(proj_ps[half][:, k], stage_t[:, half, k], w_sb[:, :], start=True, stop=True)
                            last.then_inc(projected, 1)

            @block.scalar
            def _(act):
                norm.root(act)
                with act.Fori(0, LOOPS) as i:
                    for half in range(2):
                        act.wait_ge(turned, 2 * i + (half + 3))
                        if n:
                            nc.scalar.copy(stage_t[:, half], turn_ps[half][:, :, :]).then_inc(staged_t, 1)
                        nc.scalar.copy(x_t[:, bass.ds(i * (2 * T4) + half * T4, T4)], turn_ps[half][:, :, :]).then_inc(copied, 1)


def experts(nc, c, x_t, gates, h, w1, b1, w2, b2):
    E = gates.shape[2]
    width = E * D // 4
    with Stage(nc, c) as ctx:
        sb = ctx.sb

        w1_sb, b1_sb = sb("w1_sb", [D, 4, P]), sb("b1_sb", [P, 4])
        w2_sb, b2_sb = sb("w2_sb", [P, 4, width]), sb("b2_sb", [P, E, D])
        hid = sb("hid", [P, 2, 4, T4, P])
        y, mix = sb("y", [P, 2, E, D]), sb("mix", [P, D])
        hid_ps = [ctx.ps(f"hid_ps{j}", [P, T4, P]) for j in range(4)]
        y_ps = [ctx.ps(f"y_ps{j}", [P, E, D]) for j in range(2)]
        loaded, step, hid_done, hid_read, y_done, y_read, go, add_step = (
            ctx.sem(s) for s in
            ("loaded", "step", "hid_done", "hid_read", "y_done", "y_read", "go", "add_step"))
        LOOPS = TILES // T4 // 2
        with nc.Block() as block:

            @block.sync
            def _(sp):
                load_all(sp, [(w1_sb[:, :, :], w1), (b1_sb[:, :], b1), (w2_sb[:, :, :], w2),
                              (b2_sb[:, :, :], b2.rearrange("(o e) d -> o e d", o=1).to_broadcast([P, E, D]))], loaded)

            @block.tensor
            def _(pe):
                def up(number, first, half):
                    for e in range(4):
                        pe.wait_ge(hid_read, number * 4 + (e + 1))
                        pe.sem_inc(go, 1)
                        nc.tensor.matmul(hid_ps[e][:, :, :], w1_sb[:, e], x_t[:, bass.ds(first, T4)], start=True,
                                         stop=True).then_inc(hid_done, 1)

                pe.sem_inc(hid_read, 4)
                pe.sem_inc(y_read, 2)
                pe.wait_ge(loaded, 16 * 4)
                with pe.Fori(0, LOOPS) as i:
                    for half in range(2):
                        up(2 * i + half, i * (2 * T4) + half * T4, half)
                        pe.wait_ge(hid_read, i * 8 + (half * 4 + 8))
                        for k in range(T4):
                            pe.wait_ge(y_read, i * (2 * T4) + (half * T4 + k + 1))
                            for e in range(4):
                                last = nc.tensor.matmul(y_ps[k % 2][:, :, :].rearrange("p e d -> p (e d)")[:, e * width:(e + 1) * width],
                                                        hid[:, half, e, k], w2_sb[:, e], start=True, stop=True)
                            last.then_inc(y_done, 1)

            @block.scalar
            def _(act):
                act.wait_ge(loaded, 16 * 4)
                with act.Fori(0, LOOPS) as i:
                    for half in range(2):
                        for e in range(4):
                            act.wait_ge(hid_done, i * 8 + (half * 4 + e + 1))
                            nc.scalar.activation(hid[:, half, e], hid_ps[e][:, :, :], ACT.Gelu, bias=b1_sb[:, e:e + 1]).then_inc(hid_read, 1)

            @block.vector
            def _(dve):
                dve.wait_ge(loaded, 16 * 4)
                with dve.Fori(0, LOOPS) as i:
                    done = Done(step, i * (2 * T4 * 3))
                    for half in range(2):
                        for k in range(T4):
                            tile = bass.ds(i * (2 * T4) + (half * T4 + k), 1)
                            dve.wait_ge(y_done, i * (2 * T4) + (half * T4 + k + 1))
                            nc.vector.tensor_tensor(y[:, k % 2], y_ps[k % 2][:, :, :], b2_sb[:, :, :], ALU.add).then_inc(y_read, 1)
                            dve.wait_ge(y_read, i * (2 * T4) + (half * T4 + k + 3))
                            done.add(nc.vector.tensor_tensor(y[:, k % 2], y[:, k % 2], gates[:, tile].squeeze(1).unsqueeze(2).to_broadcast([P, E, D]), ALU.mult))
                            done.wait(dve)
                            done.add(nc.vector.tensor_reduce(mix[:, :], y[:, k % 2].rearrange("p e d -> p d e"), AX.X, ALU.add))
                            done.wait(dve)
                            done.add(nc.vector.tensor_tensor(h[:, tile].squeeze(1), h[:, tile].squeeze(1), mix[:, :], ALU.add))


def top_two(nc, dve, done, score, gates, rank, top, exp_in, exp_out, act_ask, act_told, asked):
    E = score.shape[2]
    for e in range(E):
        mine = score[:, :, e:e + 1]
        done.add(nc.vector.memset(rank[:, :, e:e + 1], 0.0))
        if e:
            done.add(nc.vector.tensor_tensor(rank[:, :, 0:e], score[:, :, 0:e], mine.to_broadcast([P, TILES, e]), ALU.is_ge))
        if e < E - 1:
            done.add(nc.vector.tensor_tensor(rank[:, :, e + 1:E], score[:, :, e + 1:E],
                                             mine.to_broadcast([P, TILES, E - 1 - e]), ALU.is_gt))
        done.wait(dve)
        done.add(nc.vector.tensor_reduce(gates[:, :, e:e + 1], rank[:, :, :], AX.X, ALU.add))
        done.wait(dve)
    done.add(nc.vector.tensor_scalar(rank[:, :, :], gates[:, :, :], 2.0, None, ALU.is_lt))
    done.add(nc.vector.tensor_reduce(top[:, :], score[:, :, :], AX.X, ALU.max))
    done.wait(dve)
    nc.vector.tensor_tensor(exp_in[:, :, :], score[:, :, :], top[:, :].unsqueeze(2).to_broadcast([P, TILES, E]),
                            ALU.subtract).then_inc(act_ask, 1)
    dve.wait_ge(act_told, asked)
    done.add(nc.vector.tensor_tensor(gates[:, :, :], exp_out[:, :, :], rank[:, :, :], ALU.mult))
    done.wait(dve)
    done.add(nc.vector.tensor_reduce(top[:, :], gates[:, :, :], AX.X, ALU.add))
    done.wait(dve)
    done.add(nc.vector.reciprocal(top[:, :], top[:, :]))
    done.wait(dve)
    done.add(nc.vector.tensor_tensor(gates[:, :, :], gates[:, :, :], top[:, :].unsqueeze(2).to_broadcast([P, TILES, E]), ALU.mult))
    done.wait(dve)


GH, GE = 4, 4
GF = GH * GE
ROW = GF + GH
OUT = ROW + GH
LOW = 1e30
ROUND = 1.5 * 2 ** 23
SC = 33


def send_nodes(nc, c, w, proj, start_i, source_rows, start_rows, sender):
    with Stage(nc, c) as ctx:
        sb = ctx.sb

        att = sb("att", [P, 2, GF])
        rows, heads, tmp = sb("rows", [P, TILES, ROW]), sb("heads", [P, TILES, 1 + GH]), sb("tmp", [P, 2, TILES, GF])
        loaded, step, ready, sent_rows = (ctx.sem(s) for s in ("loaded", "step", "ready", "sent_rows"))
        sent = ctx.pool_sem("sent")
        with nc.Block() as block:

            @block.sync
            def _(sp):
                load_all(sp, [(att[:, 0], on_every_partition(w["att_src"], GF)), (att[:, 1], on_every_partition(w["att_dst"], GF))], loaded)
                sp.wait_ge(ready, 1)
                sp.dma_start(source_rows.rearrange("(p t) f -> p t f", p=P), rows[:, :, :]).then_inc(sent_rows, 16)
                sp.wait_ge(sent_rows, 16)

            @block.vector
            def _(dve):
                done = Done(step)
                dve.wait_ge(loaded, 32)
                for k in range(2):
                    done.add(nc.vector.tensor_tensor(tmp[:, k], proj[:, :, :], att[:, k].unsqueeze(1).to_broadcast([P, TILES, GF]), ALU.mult))
                nc.vector.tensor_copy(rows[:, :, 0:GF], proj[:, :, :])
                nc.vector.memset(heads[:, :, 0:1], 1.0)
                done.wait(dve)
                nc.vector.tensor_reduce(rows[:, :, GF:ROW], tmp[:, 0].rearrange("p t (h e) -> p t h e", h=GH), AX.X, ALU.add).then_inc(ready, 1)
                nc.vector.tensor_reduce(heads[:, :, 1:1 + GH], tmp[:, 1].rearrange("p t (h e) -> p t h e", h=GH), AX.X, ALU.add).then_inc(ready, 1)

            @block.gpsimd
            def _(pool):
                pool.wait_ge(ready, 2)
                for t in range(TILES):
                    nc.gpsimd.indirect_dma_start(start_rows, bass.IndirectOffsetOnAxis(ap=start_i[:, t:t + 1], axis=0),
                                                 heads[:, t], None, bounds_check=SLOTS - 1, oob_is_err=False).then_inc(sent, 16)
                pool.wait_ge(sent, 16 * TILES)
                sender.wait_all(pool)


def spread_heads(nc, c, start_rows, scratch, not_first, minus_low, dst_term, has_none):
    with Stage(nc, c) as ctx:
        sb = ctx.sb

        rows = scratch[:, 0:SCOLS * (1 + GH)].rearrange("p (c f) -> p c f", f=1 + GH)
        pair = sb("pair", [P, 2, GH])
        lines, carry = sb("lines", [GH, 2, P]), sb("carry", [GH, P + 1])
        begin = sb("begin", [P, GH])
        turn_ps = ctx.ps("turn_ps", [GH, 2, P])
        back_ps = ctx.ps("back_ps", [P, GH])
        loaded, step, pair_ready, turned, carried, back = (
            ctx.sem(s) for s in ("loaded", "step", "pair_ready", "turned", "carried", "back"))
        with nc.Block() as block:

            @block.sync
            def _(sp):
                sp.dma_start(rows[:, :, :], start_rows.rearrange("(p c) f -> p c f", p=P)).then_inc(loaded, 16)

            @block.vector
            def _(dve):
                def spread(initial):
                    for k in range(GH):
                        last = nc.vector.tensor_tensor_scan(dst_term[:, k], not_first[:, :], rows[:, :, 1 + k],
                                                            initial(k), ALU.mult, ALU.add)
                        done.add(last)

                done = Done(step)
                dve.wait_ge(loaded, 16)
                nc.vector.tensor_scalar(minus_low[:, :], rows[:, :, 0], -LOW, None, ALU.mult)
                done.add(nc.vector.tensor_reduce(has_none[:, :], rows[:, :, 0], AX.X, ALU.max))
                done.add(nc.vector.tensor_scalar(not_first[:, :], rows[:, :, 0], -1.0, 1.0, ALU.mult, ALU.add))
                done.wait(dve)
                done.add(nc.vector.tensor_scalar(has_none[:, :], has_none[:, :], -1.0, 1.0, ALU.mult, ALU.add))
                spread(lambda k: 0.0)
                done.wait(dve)
                nc.vector.tensor_copy(pair[:, 0], dst_term[:, :, SCOLS - 1])
                nc.vector.tensor_copy(pair[:, 1], has_none[:, :].to_broadcast([P, GH])).then_inc(pair_ready, 1)
                dve.wait_ge(turned, 1)
                done.add(nc.vector.tensor_copy(lines[:, :, :], turn_ps[:, :, :]))
                done.add(nc.vector.memset(carry[:, 0:1], 0.0))
                done.wait(dve)
                nc.vector.tensor_tensor_scan(carry[:, 1:P + 1], lines[:, 1], lines[:, 0], 0.0, ALU.mult, ALU.add).then_inc(carried, 1)
                dve.wait_ge(back, 1)
                done.add(nc.vector.tensor_copy(begin[:, :], back_ps[:, :]))
                done.wait(dve)
                spread(lambda k: begin[:, k:k + 1])

            @block.tensor
            def _(pe):
                pe.wait_ge(pair_ready, 1)
                for k in range(2):
                    last = nc.tensor.transpose(turn_ps[:, k], pair[:, k], c.ident[:, :])
                last.then_inc(turned, 1)
                pe.wait_ge(carried, 1)
                nc.tensor.transpose(back_ps[:, :], carry[:, 0:P], c.ident[0:GH, 0:GH]).then_inc(back, 1)


def aggregate(nc, c, w, sorted_src, source_rows, not_first, minus_low, dst_term, slot_rows, last_rows, x_t, y):
    with Stage(nc, c) as ctx:
        sb = ctx.sb

        ids = sb("ids", [P, SCOLS + 2 * SC], I32)
        id_stage = sb("id_stage", [P, 2, SC], I32)
        got = sb("got", [P, 2, SC, ROW])
        score = sb("score", [P, GH, SC])
        peak = sb("peak", [P, 2, GH, SC + 1])
        ex, weight = sb("ex", [P, 2, GH, SC]), sb("weight", [P, 2, GH, SC])
        message = sb("message", [P, GH, GE, SC])
        rows = sb("rows", [P, 2, SC, OUT])
        ids_loaded, staged, sent, step, ask, told, pool_go, rows_ready = (
            ctx.sem(s) for s in
            ("ids_loaded", "staged", "sent", "step", "ask", "told", "pool_go", "rows_ready"))
        got_in = [ctx.pool_sem(f"got_in{j}") for j in range(2)]
        stored = [ctx.sem(f"stored{j}") for j in range(2)]
        w1_sb, b1_sb = sb("w1_sb", [D, GE, P]), sb("b1_sb", [P, GE])
        w2_sb, b2_sb = sb("w2_sb", [P, GE, D]), sb("b2_sb", [P, GE, D])
        hid = sb("hid", [P, GE, P])
        hid_ps, y_ps = ctx.ps("hid_ps", [P, GE, P]), ctx.ps("y_ps", [P, GE, D])
        weights_loaded, hid_done, hid_read, y_done, y_read, pe_go = (
            ctx.sem(s) for s in ("weights_loaded", "hid_done", "hid_read", "y_done", "y_read", "pe_go"))
        assert SCOLS // SC == TILES
        LOOPS = SCOLS // SC // 2
        STEPS = 33
        with nc.Block() as block:

            @block.sync
            def _(sp):
                sp.dma_start(ids[:, 0:SCOLS], sorted_src.rearrange("(p c) o -> p (c o)", p=P)).then_inc(ids_loaded, 16)
                load_all(sp, [(w1_sb[:, :, :], w["ffn_w1"]), (b1_sb[:, :], w["ffn_b1"]), (w2_sb[:, :, :], w["ffn_w2"]),
                              (b2_sb[:, :, :], w["ffn_b2"].rearrange("(o e) d -> o e d", o=1).to_broadcast([P, GE, D]))],
                         weights_loaded)
                sp.wait_ge(step, 2)
                for half in range(2):
                    sp.dma_start(slot_rows.rearrange("(p c) f -> p c f", p=P)[:, half * SC:(half + 1) * SC],
                                 rows[:, half]).then_inc(stored[half], 16)
                with sp.Fori(0, LOOPS) as i:
                    for half in range(2):
                        sp.wait_ge(rows_ready, 2 * i + (half + 1))
                        sp.wait_ge(stored[half], i * 16 + 16)
                        sp.dma_start(slot_rows.rearrange("(p c) f -> p c f", p=P)[:, bass.ds(i * (2 * SC) + half * SC, SC)],
                                     rows[:, half]).then_inc(stored[half], 16)
                for half in range(2):
                    sp.wait_ge(stored[half], 16 * (LOOPS + 1))

            @block.gpsimd
            def _(pool):
                with pool.Fori(0, LOOPS) as i:
                    for half in range(2):
                        pool.wait_ge(staged, 2 * i + (half + 1))
                        pool.sem_inc(pool_go, 1)
                        for k in range(SC):
                            nc.gpsimd.indirect_dma_start(got[:, half, k], None, source_rows,
                                                         bass.IndirectOffsetOnAxis(ap=id_stage[:, half, k:k + 1], axis=0)).then_inc(got_in[half], 16)

            @block.scalar
            def _(act):
                with act.Fori(0, LOOPS) as i:
                    for half in range(2):
                        act.wait_ge(ask, 2 * i + (half + 1))
                        nc.scalar.activation(weight[:, :, :, :], ex[:, :, :, :], ACT.Exp).then_inc(told, 1)
                        act.wait_ge(hid_done, 2 * i + (half + 1))
                        if half == 0:
                            act.wait_ge(weights_loaded, 16 * 4)
                        for e in range(GE):
                            nc.scalar.activation(hid[:, e], hid_ps[:, e], ACT.Gelu, bias=b1_sb[:, e:e + 1]).then_inc(hid_read, 1)

            @block.tensor
            def _(pe):
                pe.sem_inc(y_read, 1)
                pe.wait_ge(weights_loaded, 16 * 4)
                with pe.Fori(0, LOOPS) as i:
                    for half in range(2):
                        tile = bass.ds(i * 2 + half, 1)
                        for e in range(GE):
                            last = nc.tensor.matmul(hid_ps[:, e], w1_sb[:, e], x_t[:, tile].squeeze(1), start=True, stop=True)
                        last.then_inc(hid_done, 1)
                        pe.wait_ge(hid_read, i * (2 * GE) + (half + 1) * GE)
                        pe.wait_ge(y_read, 2 * i + (half + 1))
                        pe.sem_inc(pe_go, 1)
                        for e in range(GE):
                            last = nc.tensor.matmul(y_ps[:, e], hid[:, e], w2_sb[:, e], start=True, stop=True)
                        last.then_inc(y_done, 1)

            @block.vector
            def _(dve):
                start = Done(step)
                start.add(nc.vector.memset(peak[:, 1], -LOW))
                start.add(nc.vector.memset(rows[:, :, :, :], 0.0))
                nc.vector.memset(ids[:, SCOLS:SCOLS + 2 * SC], 0)
                dve.wait_ge(ids_loaded, 16)
                nc.vector.tensor_copy(id_stage[:, 0], ids[:, 0:SC]).then_inc(staged, 1)
                nc.vector.tensor_copy(id_stage[:, 1], ids[:, SC:2 * SC]).then_inc(staged, 1)
                start.wait(dve)
                dve.wait_ge(weights_loaded, 16 * 4)
                with dve.Fori(0, LOOPS) as i:
                    for half in range(2):
                        done = Done(step, i * (2 * STEPS) + (half * STEPS + 2))
                        cols = bass.ds(i * (2 * SC) + half * SC, SC)
                        g = got[:, half]
                        dve.wait_ge(got_in[half], i * (16 * SC) + 16 * SC)
                        done.add(nc.vector.tensor_copy(peak[:, half, :, 0:1], peak[:, 1 - half, :, SC:SC + 1]))
                        done.add(nc.vector.tensor_tensor(score[:, :, :], g[:, :, GF:ROW].rearrange("p c h -> p h c"),
                                                         dst_term[:, :, cols], ALU.add))
                        done.wait(dve)
                        done.add(nc.vector.scalar_tensor_tensor(score[:, :, :], score[:, :, :], 0.2, score[:, :, :], ALU.mult, ALU.max))
                        done.wait(dve)
                        for k in range(GH):
                            done.add(nc.vector.tensor_tensor_scan(peak[:, half, k, 1:SC + 1], minus_low[:, cols], score[:, k],
                                                                  peak[:, half, k, 0:1], ALU.add, ALU.max))
                        done.wait(dve)
                        done.add(nc.vector.tensor_tensor(ex[:, 1], peak[:, half, :, 0:SC], peak[:, half, :, 1:SC + 1], ALU.subtract))
                        done.add(nc.vector.tensor_tensor(ex[:, 0], score[:, :, :], peak[:, half, :, 1:SC + 1], ALU.subtract))
                        done.wait(dve)
                        nc.vector.tensor_scalar(ex[:, 1], ex[:, 1], 0.0, None, ALU.min).then_inc(ask, 1)
                        dve.wait_ge(told, 2 * i + (half + 1))
                        done.add(nc.vector.tensor_tensor(weight[:, 1], weight[:, 1], not_first[:, cols].unsqueeze(1).to_broadcast([P, GH, SC]), ALU.mult))
                        done.add(nc.vector.tensor_tensor(message[:, :, :, :], g[:, :, 0:GF].rearrange("p c (h e) -> p h e c", h=GH),
                                                         weight[:, 0].unsqueeze(2).to_broadcast([P, GH, GE, SC]), ALU.mult))
                        dve.wait_ge(stored[half], i * 16 + 16)
                        done.wait(dve)
                        for f in range(ROW):
                            k = f // GE if f < GF else f - GF
                            new = message[:, k, f % GE] if f < GF else weight[:, 0, k]
                            done.add(nc.vector.tensor_tensor_scan(rows[:, half, :, f], weight[:, 1, k], new,
                                                                  rows[:, 1 - half, SC - 1, f:f + 1], ALU.mult, ALU.add))
                        done.add(nc.vector.tensor_copy(rows[:, half, :, ROW:OUT].rearrange("p c h -> p h c"), peak[:, half, :, 1:SC + 1]))
                        done.add(nc.vector.tensor_copy(id_stage[:, half], ids[:, bass.ds(i * (2 * SC) + (half + 2) * SC, SC)]))
                        assert done.n == STEPS, done.n
                        done.wait(dve)
                        dve.sem_inc(staged, 1)
                        dve.sem_inc(rows_ready, 1)
                        dve.wait_ge(y_done, 2 * i + (half + 1))
                        nc.vector.tensor_tensor(y[:, bass.ds(i * 2 + half, 1)].squeeze(1), y_ps[:, :, :], b2_sb[:, :, :],
                                                ALU.add).then_inc(y_read, 1)
                nc.vector.tensor_copy(last_rows[:, :], rows[:, 1, SC - 1])


def finish_graph(nc, c, w, end_i, start_i, slot_rows, carry_rows, last_rows, has_none, gates):
    with Stage(nc, c) as ctx:
        sb = ctx.sb
        sem = ctx.sem

        part = sb("part", [P, 3, ROW])
        line = sb("line", [ROW, 3, P])
        open_max, open_sum = sb("open_max", [ROW, P + 1]), sb("open_sum", [ROW, P])
        low = sb("low", [ROW, P])
        fac = sb("fac", [ROW, 2, P])
        back = sb("back", [P, 2, ROW])
        none = sb("none", [1, 2, ROW])
        part_ps = ctx.ps("part_ps", [ROW, 3, P])
        back_ps = ctx.ps("back_ps", [P, 2, ROW])
        first_part, last_part = sb("first_part", [P, TILES]), sb("last_part", [P, TILES])
        carry_i = sb("carry_i", [P, TILES], I32)
        mine, before = sb("mine", [P, TILES, OUT]), sb("before", [P, TILES, 2 * ROW])
        peak = sb("peak", [P, TILES, GH])
        ex, factor = sb("ex", [P, 2, TILES, GH]), sb("factor", [P, 2, TILES, GH])
        inv = sb("inv", [P, TILES, GH])
        agg, centred, square = sb("agg", [P, TILES, GF]), sb("centred", [P, TILES, GF]), sb("square", [P, TILES, GF])
        gain = sb("gain", [P, 3, GF])
        score, rank, top, sx = sb("score", [P, TILES, GE]), sb("rank", [P, TILES, GE]), sb("top", [P, TILES]), sb("sx", [P, 2, TILES, GE])
        loaded, step, part_ready, turned, lines_ready, ask, told, turned_back, stored, carry_sent, idx_ready = map(
            sem, ("loaded", "step", "part_ready", "turned", "lines_ready", "ask", "told", "turned_back", "stored",
                  "carry_sent", "idx_ready"))
        mine_in, before_in = ctx.pool_sem("mine_in"), ctx.pool_sem("before_in")
        norm = Norm(nc, ctx, "norm", TILES, GF)

        with nc.Block() as block:

            @block.sync
            def _(sp):
                load_all(sp, [(gain[:, 0], on_every_partition(w["gat_b"], GF)), (gain[:, 1], on_every_partition(w["ln_gamma"], GF)),
                              (gain[:, 2], on_every_partition(w["ln_beta"], GF))], loaded)
                sp.wait_ge(stored, 1)
                sp.dma_start(carry_rows[0:P].rearrange("p (a f) -> p a f", a=2), back[:, :, :]).then_inc(carry_sent, 16)
                sp.dma_start(carry_rows[P:P + 1].rearrange("p (a f) -> p a f", a=2), none[:, :, :]).then_inc(carry_sent, 16)
                sp.wait_ge(carry_sent, 32)

            @block.gpsimd
            def _(pool):
                for t in range(TILES):
                    nc.gpsimd.indirect_dma_start(mine[:, t], None, slot_rows,
                                                 bass.IndirectOffsetOnAxis(ap=end_i[:, t:t + 1], axis=0)).then_inc(mine_in, 16)
                pool.wait_ge(carry_sent, 32)
                pool.wait_ge(idx_ready, 1)
                for t in range(TILES):
                    nc.gpsimd.indirect_dma_start(before[:, t], None, carry_rows,
                                                 bass.IndirectOffsetOnAxis(ap=carry_i[:, t:t + 1], axis=0)).then_inc(before_in, 16)

            @block.tensor
            def _(pe):
                pe.wait_ge(part_ready, 1)
                for k in range(3):
                    last = nc.tensor.transpose(part_ps[:, k], part[:, k], c.ident[:, :])
                last.then_inc(turned, 1)
                pe.wait_ge(lines_ready, 1)
                nc.tensor.transpose(back_ps[:, 0], open_max[:, 1:P + 1], c.ident[0:ROW, 0:ROW])
                nc.tensor.transpose(back_ps[:, 1], open_sum[:, :], c.ident[0:ROW, 0:ROW]).then_inc(turned_back, 1)

            @block.scalar
            def _(act):
                act.wait_ge(ask, 1)
                nc.scalar.activation(fac[:, :, :], fac[:, :, :], ACT.Exp).then_inc(told, 1)
                act.wait_ge(ask, 2)
                nc.scalar.activation(factor[:, :, :, :], ex[:, :, :, :], ACT.Exp).then_inc(told, 1)
                norm.root(act)
                act.wait_ge(ask, 3)
                nc.scalar.activation(sx[:, 1], sx[:, 0], ACT.Exp).then_inc(told, 1)

            @block.vector
            def _(dve):
                v = nc.vector
                done = Done(step)
                done.add(v.tensor_copy(part[:, 0, 0:GF].rearrange("p (h e) -> p h e", h=GH),
                                       last_rows[:, ROW:OUT].unsqueeze(2).to_broadcast([P, GH, GE])))
                v.tensor_copy(part[:, 0, GF:ROW], last_rows[:, ROW:OUT])
                v.tensor_copy(part[:, 1], last_rows[:, 0:ROW])
                v.memset(none[:, 0], -LOW)
                v.memset(none[:, 1], 0.0)
                v.tensor_copy(part[:, 2], has_none[:, :].to_broadcast([P, ROW])).then_inc(part_ready, 1)
                dve.wait_ge(turned, 1)
                done.add(v.tensor_copy(line[:, :, :], part_ps[:, :, :]))
                done.add(v.memset(open_max[:, 0:1], -LOW))
                done.wait(dve)
                done.add(v.tensor_scalar(low[:, :], line[:, 2], -1.0, LOW, ALU.add, ALU.mult))
                done.wait(dve)
                done.add(v.tensor_tensor_scan(open_max[:, 1:P + 1], low[:, :], line[:, 0], -LOW, ALU.add, ALU.max))
                done.wait(dve)
                done.add(v.tensor_tensor(fac[:, 0], open_max[:, 0:P], open_max[:, 1:P + 1], ALU.subtract))
                done.add(v.tensor_tensor(fac[:, 1], line[:, 0], open_max[:, 1:P + 1], ALU.subtract))
                done.wait(dve)
                v.tensor_scalar(fac[:, 0], fac[:, 0], 0.0, None, ALU.min).then_inc(ask, 1)
                dve.wait_ge(told, 1)
                done.add(v.tensor_tensor(fac[:, 0], fac[:, 0], line[:, 2], ALU.mult))
                done.add(v.tensor_tensor(fac[:, 1], fac[:, 1], line[:, 1], ALU.mult))
                done.wait(dve)
                v.tensor_tensor_scan(open_sum[:, :], fac[:, 0], fac[:, 1], 0.0, ALU.mult, ALU.add).then_inc(lines_ready, 1)
                dve.wait_ge(turned_back, 1)
                v.tensor_copy(back[:, :, :], back_ps[:, :, :]).then_inc(stored, 1)
                for out, slots in ((first_part, start_i), (last_part, end_i)):
                    done.add(v.tensor_scalar(out[:, :], slots[:, :], 1.0 / SCOLS, 0.5 / SCOLS - 0.5, ALU.mult, ALU.add))
                done.wait(dve)
                for out in (first_part, last_part):
                    done.add(v.tensor_scalar_add(out[:, :], out[:, :], ROUND))
                done.wait(dve)
                for out in (first_part, last_part):
                    done.add(v.tensor_scalar_add(out[:, :], out[:, :], -ROUND))
                done.wait(dve)
                done.add(v.tensor_tensor(first_part[:, :], first_part[:, :], last_part[:, :], ALU.is_lt))
                done.wait(dve)
                done.add(v.scalar_tensor_tensor(last_part[:, :], last_part[:, :], -float(P + 1), first_part[:, :], ALU.add, ALU.mult))
                done.wait(dve)
                v.tensor_scalar_add(carry_i[:, :], last_part[:, :], float(P)).then_inc(idx_ready, 1)
                dve.wait_ge(mine_in, 16 * TILES)
                dve.wait_ge(before_in, 16 * TILES)
                done.add(v.tensor_tensor(peak[:, :, :], mine[:, :, ROW:OUT], before[:, :, GF:ROW], ALU.max))
                done.wait(dve)
                done.add(v.tensor_tensor(ex[:, 0], mine[:, :, ROW:OUT], peak[:, :, :], ALU.subtract))
                v.tensor_tensor(ex[:, 1], before[:, :, GF:ROW], peak[:, :, :], ALU.subtract).then_inc(ask, 1)
                dve.wait_ge(told, 2)

                def by_head(x):
                    return x.rearrange("p t (h e) -> p t h e", h=GH)

                def wide(x):
                    return x.unsqueeze(3).to_broadcast([P, TILES, GH, GE])

                done.add(v.tensor_tensor(by_head(agg[:, :, :]), by_head(mine[:, :, 0:GF]), wide(factor[:, 0]), ALU.mult))
                done.add(v.tensor_tensor(by_head(centred[:, :, :]), by_head(before[:, :, ROW:ROW + GF]), wide(factor[:, 1]), ALU.mult))
                done.add(v.tensor_tensor(inv[:, :, :], mine[:, :, GF:ROW], factor[:, 0], ALU.mult))
                done.add(v.tensor_tensor(peak[:, :, :], before[:, :, ROW + GF:2 * ROW], factor[:, 1], ALU.mult))
                done.wait(dve)
                done.add(v.tensor_tensor(agg[:, :, :], agg[:, :, :], centred[:, :, :], ALU.add))
                done.add(v.scalar_tensor_tensor(inv[:, :, :], inv[:, :, :], 1e-16, peak[:, :, :], ALU.add, ALU.add))
                done.wait(dve)
                done.add(v.reciprocal(inv[:, :, :], inv[:, :, :]))
                done.wait(dve)
                done.add(v.tensor_tensor(by_head(agg[:, :, :]), by_head(agg[:, :, :]), wide(inv[:, :, :]), ALU.mult))
                dve.wait_ge(loaded, 48)
                done.wait(dve)

                def row(k):
                    return gain[:, k].unsqueeze(1).to_broadcast([P, TILES, GF])

                done.add(v.tensor_tensor(agg[:, :, :], agg[:, :, :], row(0), ALU.add))
                done.wait(dve)
                norm.centre(dve, done, agg[:, :, :], centred[:, :, :], square[:, :, :])
                done.add(v.tensor_tensor(centred[:, :, :], centred[:, :, :], norm.wide(norm.inv), ALU.mult))
                done.wait(dve)
                for k, op in ((1, ALU.mult), (2, ALU.add)):
                    done.add(v.tensor_tensor(centred[:, :, :], centred[:, :, :], row(k), op))
                    done.wait(dve)
                done.add(v.tensor_reduce(score[:, :, :], centred[:, :, :].rearrange("p t (h e) -> p t e h", h=GH), AX.X, ALU.add))
                done.wait(dve)
                done.add(v.tensor_scalar_mul(score[:, :, :], score[:, :, :], 1.0 / GH))
                done.wait(dve)
                top_two(nc, dve, done, score, gates, rank, top, sx[:, 0], sx[:, 1], ask, told, 3)


def mix_experts(nc, c, y, gates, h):
    with Stage(nc, c) as ctx:
        mixed = ctx.sb("mixed", [P, TILES, D])
        step = ctx.sem("step")
        with nc.Block() as block:

            @block.vector
            def _(dve):
                done = Done(step)
                done.add(nc.vector.tensor_tensor(y[:, :, :, :], y[:, :, :, :], gates[:, :, :].unsqueeze(3).to_broadcast([P, TILES, GE, D]), ALU.mult))
                done.wait(dve)
                done.add(nc.vector.tensor_reduce(mixed[:, :, :], y[:, :, :, :].rearrange("p t e d -> p t d e"), AX.X, ALU.add))
                done.wait(dve)
                nc.vector.tensor_tensor(h[:, :, :], h[:, :, :], mixed[:, :, :], ALU.add)


def route(nc, c, logits, gates):
    E = logits.shape[2]
    with Stage(nc, c) as ctx:
        sb = ctx.sb

        rank, top, sx = sb("rank", [P, TILES, E]), sb("top", [P, TILES]), sb("sx", [P, 2, TILES, E])
        step, ask, told = (ctx.sem(s) for s in ("step", "ask", "told"))
        with nc.Block() as block:

            @block.vector
            def _(dve):
                top_two(nc, dve, Done(step), logits, gates, rank, top, sx[:, 0], sx[:, 1], ask, told, 1)

            @block.scalar
            def _(act):
                act.wait_ge(ask, 1)
                nc.scalar.activation(sx[:, 1], sx[:, 0], ACT.Exp).then_inc(told, 1)


def column_attention(nc, c, w, x_t, out_t):
    KT = SEQ // P
    MASK = -1e10
    with Stage(nc, c) as ctx:
        sb = ctx.sb
        sem = ctx.sem

        wqkv = sb("wqkv", [D, 3, D])
        xb, q, k = sb("xb", [D, SEQ]), sb("q", [D, SEQ]), sb("k", [D, SEQ])
        v = sb("v", [P, KT, D])
        mask = sb("mask", [P, SEQ])
        e = sb("e", [P, KT, SEQ])
        peak, total = sb("peak", [P, KT]), sb("total", [P, KT])
        in_ps = [ctx.ps(f"in_ps{j}", [P, 512]) for j in range(2)]
        s_ps = [ctx.ps(f"s_ps{j}", [P, SEQ]) for j in range(2)]
        o_ps = ctx.ps("o_ps", [D, 2, 512])
        loaded, masked, xb_ready, in_done, in_read, s_done, s_read, v_ready, step, peak_ready, exp_done, o_done, o_read, go = map(
            sem, ("loaded", "masked", "xb_ready", "in_done", "in_read", "s_done", "s_read", "v_ready", "step",
                  "peak_ready", "exp_done", "o_done", "o_read", "go"))

        def width(m):
            return SEQ if m == 0 else (m + 1) * P

        with nc.Block() as block:

            @block.sync
            def _(sp):
                load_all(sp, [(wqkv[:, j], w[n]) for j, n in enumerate(("l1_wq_t", "l1_wk_t", "l1_wv_t"))], loaded)

            @block.gpsimd
            def _(pool):
                nc.gpsimd.memset(mask[:, :], MASK).then_inc(masked, 1)
                pool.wait_ge(masked, 1)
                nc.gpsimd.affine_select(out=mask[:, :], in_=mask[:, :], compare_op=ALU.is_ge, fill=0.0, base=0,
                                        pattern=[[1, SEQ]], channel_multiplier=-1).then_inc(masked, 1)

            @block.scalar
            def _(act):
                act.sem_inc(in_read, 2)
                act.wait_ge(loaded, 48)
                with act.Fori(0, BATCH) as s:
                    act.wait_ge(o_read, s + 1)
                    nc.scalar.copy(xb[:, :].rearrange("d (p t) -> d t p", t=TILES), x_t[:, :, bass.ds(s * (SEQ // TILES), SEQ // TILES)]).then_inc(xb_ready, 1)
                    for j in range(4):
                        act.wait_ge(in_done, s * 5 + (j + 1))
                        nc.scalar.copy((q, k)[j // 2][:, j % 2 * 512:(j % 2 + 1) * 512], in_ps[j % 2][0:D, :]).then_inc(in_read, 1)
                    act.wait_ge(in_done, s * 5 + 5)
                    nc.scalar.copy(v[:, :, :], in_ps[0][:, :].rearrange("p (m d) -> p m d", m=KT)).then_inc(in_read, 1)
                    for m in range(KT):
                        act.wait_ge(peak_ready, s * KT + (m + 1))
                        nc.scalar.activation(e[:, m, 0:width(m)], s_ps[m % 2][:, 0:width(m)], ACT.Exp, scale=D ** -0.5,
                                             bias=peak[:, m:m + 1], accum_out=total[:, m:m + 1]).then_inc(exp_done, 1)
                    act.wait_ge(o_done, s + 1)
                    nc.scalar.copy(out_t[:, bass.ds(s * SEQ, SEQ)].rearrange("d (a n) -> d a n", a=2), o_ps[:, :, :]).then_inc(o_read, 1)

            @block.tensor
            def _(pe):
                pe.sem_inc(o_read, 1)
                pe.sem_inc(s_read, 2)
                pe.wait_ge(loaded, 48)

                def scores(s, m):
                    pe.wait_ge(exp_done, s * KT + (m + 1 - 2 + 2))
                    for a in range(0, width(m), 512):
                        b = min(a + 512, width(m))
                        last = nc.tensor.matmul(s_ps[m % 2][:, a:b], k[:, m * P:(m + 1) * P], q[:, a:b], start=True, stop=True)
                    last.then_inc(s_done, 1)

                def mix(s, m):
                    if m == 0:
                        pe.wait_ge(o_read, s + 1)
                    pe.wait_ge(v_ready, s * KT + (m + 1))
                    for a in range(2):
                        n = min(width(m) - a * 512, 512)
                        if n > 0:
                            last = nc.tensor.matmul(o_ps[:, a, 0:n], v[:, m], e[:, m, a * 512:a * 512 + n],
                                                    start=(m == 0), stop=(m == KT - 1))
                    return last

                pe.sem_inc(exp_done, 2)
                with pe.Fori(0, BATCH) as s:
                    pe.wait_ge(xb_ready, s + 1)
                    for j in range(4):
                        pe.wait_ge(in_read, s * 5 + max(j + 1, 2))
                        pe.sem_inc(go, 1)
                        nc.tensor.matmul(in_ps[j % 2][0:D, :], wqkv[:, j // 2], xb[:, j % 2 * 512:(j % 2 + 1) * 512],
                                         start=True, stop=True).then_inc(in_done, 1)
                    pe.wait_ge(in_read, s * 5 + 6)
                    for m in range(KT):
                        last = nc.tensor.matmul(in_ps[0][:, m * D:(m + 1) * D], xb[:, m * P:(m + 1) * P], wqkv[:, 2], start=True, stop=True)
                    last.then_inc(in_done, 1)
                    scores(s, 0)
                    for m in range(1, KT):
                        scores(s, m)
                        mix(s, m - 1)
                    mix(s, KT - 1).then_inc(o_done, 1)

            @block.vector
            def _(dve):
                def divide(s, m):
                    if m == 0:
                        dve.wait_ge(in_read, s * 5 + 7)
                    dve.wait_ge(exp_done, s * KT + (m + 3))
                    done.add(nc.vector.reciprocal(total[:, m:m + 1], total[:, m:m + 1]))
                    done.wait(dve)
                    nc.vector.tensor_scalar(v[:, m], v[:, m], total[:, m:m + 1], None, ALU.mult).then_inc(v_ready, 1)

                dve.wait_ge(masked, 2)
                with dve.Fori(0, BATCH) as s:
                    done = Done(step, s * (3 * KT))
                    for m in range(KT):
                        n = width(m)
                        lo = m * P
                        dve.wait_ge(s_done, s * KT + (m + 1))
                        cut = slice(0, SEQ) if m == 0 else slice(lo, lo + P)
                        done.add(nc.vector.tensor_tensor(s_ps[m % 2][:, cut], s_ps[m % 2][:, cut], mask[:, 0:cut.stop - cut.start], ALU.add))
                        done.wait(dve)
                        done.add(nc.vector.tensor_reduce(peak[:, m:m + 1], s_ps[m % 2][:, 0:n], AX.X, ALU.max))
                        done.wait(dve)
                        nc.vector.tensor_scalar_mul(peak[:, m:m + 1], peak[:, m:m + 1], -(D ** -0.5)).then_inc(peak_ready, 1)
                        if m:
                            divide(s, m - 1)
                    divide(s, KT - 1)


class Constants:

    def __init__(self, nc, whole):
        def sb(name, shape, dt=F32):
            return whole.enter_context(nc.sbuf_tensor(name, shape, dt))

        self.whole, self.stages, self.used = whole, 0, []
        self.ident, self.ident_b = sb("ident", [P, P]), sb("ident_b", [P, P], BF16)
        self.upper, self.upper_b = sb("upper", [P, P]), sb("upper_b", [P, P], BF16)
        self.zeros, self.ones = sb("zeros", [P, P]), sb("ones", [P, P])
        self.iota_i, self.iota_b = sb("iota_i", [P, P], I32), sb("iota_b", [P, P], BF16)
        self.part_i, self.part_f = sb("part_i", [P, 2], I32), sb("part_f", [P, 2])


def store_nodes(nc, c, h, out):
    with Stage(nc, c) as ctx, nc.Block() as block:
        stored = ctx.sem("stored")

        @block.sync
        def _(sp):
            sp.dma_start(out.rearrange("(p t) d -> p t d", p=P), h[:, :, :]).then_inc(stored, 16)
            sp.wait_ge(stored, 16)


def token_features(nc, c, w, h, sender):
    with Stage(nc, c) as s:
        tab_h, tab_x, tab_xt = s.sb("tab_h", [P, 2, D]), s.sb("tab_x", [P, 2, D]), s.sb("tab_xt", [D + 1, VOCAB])
        words, chosen = s.sb("words", [P, NODES]), s.sb("chosen", [P, SEQ])
        chosen_table, plain_table = s.sb("chosen_table", [P, 2, BATCH, D]), s.sb("plain_table", [P, 2, D])
        token_tables(nc, c, w, tab_h, tab_x, tab_xt)
        load_words(nc, c, w, words, chosen, meanwhile=sender.share(2))
        word_attention(nc, c, w, h, tab_h, tab_x, tab_xt, words, chosen, chosen_table, plain_table,
                       meanwhile=sender.share(20))
        with Stage(nc, c) as t:
            node_t = t.sb("node_t", [D, NODES])
            look_up(nc, c, words, chosen, chosen_table, plain_table, node_t, meanwhile=sender.share(4))
            to_nodes(nc, c, node_t[:, :], h, False, meanwhile=sender.share(4))


def build_tower(nc, w, out):
    def dram(name, shape, dt=F32):
        return nc.dram_tensor(name, shape, dt).ap()

    sorted_src, start_rows = dram("sorted_src", (SLOTS, 1), I32), dram("start_rows", (SLOTS, 1 + GH))
    source_rows, slot_rows = dram("source_rows", (NODES, ROW)), dram("slot_rows", (SLOTS, OUT))
    carry_rows = dram("carry_rows", (P + 1, 2 * ROW))
    with ExitStack() as whole:
        c = Constants(nc, whole)
        h = whole.enter_context(nc.sbuf_tensor("h", [P, TILES, D], F32))
        start_i = whole.enter_context(nc.sbuf_tensor("start_i", [P, TILES], I32))
        end_i = whole.enter_context(nc.sbuf_tensor("end_i", [P, TILES], I32))
        make_constants(nc, c)
        with Stage(nc, c) as s:
            x_t = s.sb("x_t", [D, TILES, P])
            gates = s.sb("gates", [P, TILES, GE])
            has_none, last_rows = s.sb("has_none", [P, 1]), s.sb("last_rows", [P, OUT])
            with Stage(nc, c) as t:
                sender = Sender(nc, t, sorted_src)
                sort_edges(nc, c, w["edges"], sorted_src, start_rows, start_i, end_i, sender, 28)
                token_features(nc, c, w, h, sender)
                proj = t.sb("proj", [P, TILES, GF])
                norm_project(nc, c, h, x_t, w["gat_w"], proj, meanwhile=sender.share(6))
                send_nodes(nc, c, w, proj, start_i, source_rows, start_rows, sender)
            with Stage(nc, c) as t:
                y = t.sb("y", [P, TILES, GE, D])
                with Stage(nc, c) as u:
                    not_first, minus_low = u.sb("not_first", [P, SCOLS]), u.sb("minus_low", [P, SCOLS])
                    dst_term = u.sb("dst_term", [P, GH, SCOLS])
                    spread_heads(nc, c, start_rows, y[:, :, :, :].rearrange("p t e d -> p (t e d)"), not_first, minus_low, dst_term, has_none)
                    aggregate(nc, c, w, sorted_src, source_rows, not_first, minus_low, dst_term, slot_rows, last_rows, x_t, y)
                finish_graph(nc, c, w, end_i, start_i, slot_rows, carry_rows, last_rows, has_none, gates)
                mix_experts(nc, c, y, gates, h)

        clear_semaphores(nc, c)
        with Stage(nc, c) as s:
            x_t, out_t = s.sb("x_t", [D, TILES, P]), s.sb("out_t", [D, NODES])
            norm_project(nc, c, h, x_t, None, None)
            column_attention(nc, c, w, x_t, out_t)
            to_nodes(nc, c, out_t[:, :], h, True)
        with Stage(nc, c) as s:
            x_t, gates = s.sb("x_t", [D, TILES, P]), s.sb("gates", [P, TILES, EXPERTS])
            logits = s.sb("logits", [P, TILES, EXPERTS])
            norm_project(nc, c, h, x_t, w["router_t"], logits, add_back=True)
            route(nc, c, logits, gates)
            experts(nc, c, x_t, gates, h, w["moe_w1"], w["moe_b1"], w["moe_w2"], w["moe_b2"])
        store_nodes(nc, c, h, out)


def kernel(**inputs):
    import numpy as np
    import concourse.bacc as bacc
    from concourse.bass_utils import run_bass_kernel_spmd as run

    a = {name: np.asarray(value) for name, value in inputs.items()}

    def with_bias(weight, bias):
        return np.concatenate([weight.T, bias[None]], 0)

    def pair_blocks(w2):
        pairs = w2.reshape(EXPERTS // 2, 2, D, D)
        out = np.zeros((2, D, EXPERTS // 2, 2, D), w2.dtype)
        for j in range(2):
            out[j, :, :, j, :] = pairs[:, j].transpose(1, 0, 2)
        return out.reshape(2 * D, EXPERTS // 2, 2 * D)

    arrays = {
        "tokens": a["x"].reshape(-1),
        "a2a": a["L0_attn_a2a"],
        "emb_t": a["L0_tok_emb_table"].T,
        "tok_w1_t": a["L0_tok_W1"][:, :D].T,
        "tok_b1": a["L0_tok_b1"][:, None],
        "tok_w2_t": with_bias(a["L0_tok_W2"], a["L0_tok_b2"]),
        "tok_gamma": a["L0_tok_gamma"],
        "tok_beta": a["L0_tok_beta"],
        "wq_t": a["L0_attn_wq"].T,
        "wv_t": a["L0_attn_wv"].T,
        "wk_pairs": a["L0_attn_wk"].reshape(HEADS0 // 2, 2 * D).T,
        "fan_t": a["L0_attn_fanout_w"].T,
        "edges": a["L0_ffn_edge_index"],
        "gat_w": a["L0_ffn_W_gat"],
        "att_src": a["L0_ffn_att_src"].reshape(-1),
        "att_dst": a["L0_ffn_att_dst"].reshape(-1),
        "gat_b": a["L0_ffn_b_gat"],
        "ln_gamma": a["L0_ffn_ln_gamma"],
        "ln_beta": a["L0_ffn_ln_beta"],
        "ffn_w1": a["L0_ffn_W1"].transpose(1, 0, 2),
        "ffn_b1": a["L0_ffn_b1"].T,
        "ffn_w2": a["L0_ffn_W2"].transpose(1, 0, 2),
        "ffn_b2": a["L0_ffn_b2"],
        "l1_wq_t": a["L1_attn_Wq"].T,
        "l1_wk_t": a["L1_attn_Wk"].T,
        "l1_wv_t": a["L1_attn_Wv"].T,
        "router_t": a["L1_ffn_router_w"].T,
        "moe_w1": a["L1_ffn_w1"].reshape(EXPERTS // 2, 2, D, D).transpose(2, 0, 1, 3).reshape(D, EXPERTS // 2, 2 * D),
        "moe_b1": a["L1_ffn_b1"].reshape(EXPERTS // 2, 2 * D).T,
        "moe_w2": pair_blocks(a["L1_ffn_w2"]),
        "moe_b2": a["L1_ffn_b2"],
    }
    arrays = {name: np.ascontiguousarray(value) for name, value in arrays.items()}
    nc = bacc.Bacc("TRN2", target_bir_lowering=False, num_devices=1)
    w = {name: nc.dram_tensor("in_" + name, value.shape, mybir.dt.from_np(value.dtype), kind="ExternalInput").ap()
         for name, value in arrays.items()}
    out = nc.dram_tensor("out", (NODES, D), F32, kind="ExternalOutput").ap()
    build_tower(nc, w, out)
    r = run(nc, [{"in_" + name: value for name, value in arrays.items()}], core_ids=[0])
    return r.results[0]["out"].reshape(BATCH, SEQ, D)
```

```python
import concourse.bass as bass
from concourse import mybir
from concourse.alu_op_type import AluOpType as ALU
from contextlib import ExitStack

F32 = mybir.dt.float32
BF16 = mybir.dt.bfloat16
I32 = mybir.dt.int32
U8 = mybir.dt.uint8
ACT = mybir.ActivationFunctionType
AX = mybir.AxisListType

P = 128
BATCH, SEQ, D = 8, 1024, 64
NODES = BATCH * SEQ
TILES = NODES // P
EDGES = 262144
COLS = EDGES // P
GC = 8
GROUPS = COLS // GC
SLOTS = EDGES + NODES
SCOLS = SLOTS // P
DROPPED = 1 << 20


class Stage(ExitStack):

    def __init__(self, nc, c):
        super().__init__()
        self.nc = nc
        c.stages += 1
        self.tag = f"s{c.stages}_"
        self.used, self.whole = c.used, c.whole

    def sb(self, name, shape, dt=F32):
        return self.enter_context(self.nc.sbuf_tensor(self.tag + name, shape, dt))

    def ps(self, name, shape, dt=F32):
        return self.enter_context(self.nc.psum_tensor(self.tag + name, shape, dt))

    def sem(self, name):
        s = self.enter_context(self.nc.semaphore(self.tag + name))
        self.used.append(s)
        return s

    def pool_sem(self, name):
        return self.whole.enter_context(self.nc.semaphore(self.tag + name))


def clear_semaphores(nc, c):
    with nc.Block() as block:

        @block.sync
        def _(sp):
            for s in c.used:
                sp.sem_clear(s)
            c.used.clear()


class Done:

    def __init__(self, sem, base=0):
        self.sem, self.base, self.n = sem, base, 0

    def add(self, instruction, by=1):
        instruction.then_inc(self.sem, by)
        self.n += by
        return self.base + self.n

    def wait(self, engine):
        engine.wait_ge(self.sem, self.base + self.n)


def make_constants(nc, c):
    with Stage(nc, c) as ctx, nc.Block() as block:
        const_step = ctx.sem("const_step")

        @block.gpsimd
        def _(pool):
            done = Done(const_step)
            nc.gpsimd.memset(c.ident[:, :], 0.0)
            nc.gpsimd.memset(c.upper[:, :], 1.0)
            nc.gpsimd.memset(c.zeros[:, :], 0.0)
            nc.gpsimd.memset(c.ones[:, :], 1.0)
            nc.gpsimd.iota(c.iota_i[:, :], [[1, P]], base=0, channel_multiplier=0)
            done.add(nc.gpsimd.iota(c.part_i[:, :], [[P, 2]], base=0, channel_multiplier=1))
            done.wait(pool)
            nc.gpsimd.affine_select(out=c.ident[:, :], in_=c.ident[:, :], compare_op=ALU.not_equal, fill=1.0,
                                    base=0, pattern=[[-1, P]], channel_multiplier=1)
            done.add(nc.gpsimd.affine_select(out=c.upper[:, :], in_=c.upper[:, :], compare_op=ALU.is_gt, fill=0.0,
                                             base=0, pattern=[[1, P]], channel_multiplier=-1))

        @block.vector
        def _(dve):
            dve.wait_ge(const_step, 2)
            nc.vector.tensor_copy(c.ident_b[:, :], c.ident[:, :])
            nc.vector.tensor_copy(c.upper_b[:, :], c.upper[:, :])
            nc.vector.tensor_copy(c.iota_b[:, :], c.iota_i[:, :])
            nc.vector.tensor_copy(c.part_f[:, :], c.part_i[:, :])


class Sender:

    BATCH = 32

    def __init__(self, nc, ctx, longer, sorted_src):
        self.nc, self.sorted_src = nc, sorted_src
        self.slot_now = longer.sb("slot_now", [P, 2, self.BATCH], I32)
        self.slot_sum = longer.sb("slot_sum", [P, self.BATCH])
        self.src_now = longer.sb("src_now", [P, 2, self.BATCH], I32)
        self.src = ctx.sb("src", [P, COLS], I32)
        self.slots = ctx.sb("slots", [P, GC + COLS])
        self.dropped = ctx.sb("dropped", [P, COLS])
        self.sent = [ctx.pool_sem("sent0"), ctx.pool_sem("sent1")]
        self.copied, self.go = ctx.pool_sem("copied"), ctx.pool_sem("go")
        self.first = 0

    def scatter(self, slots, rows):
        return self.nc.gpsimd.indirect_dma_start(
            self.sorted_src, bass.IndirectOffsetOnAxis(ap=slots, axis=0), rows, None,
            bounds_check=SLOTS - 1, oob_is_err=False)

    def send(self, pool, batches, slots_ready=None):
        n, first = self.BATCH, self.first

        def batch(i, half, wait):
            if slots_ready is not None:
                pool.wait_ge(slots_ready, i * (2 * n // GC) + ((first + half + 1) * (n // GC) + 2))
            self.stage(pool, first, i, half, wait)
            self.scatter_batch(half)

        if first == 0:
            for half in range(2):
                batch(0, half, False)
        with pool.Fori(1 if first == 0 else 0, batches // 2) as i:
            for half in range(2):
                batch(i, half, True)
        self.first += batches

    def stage(self, pool, first, i, half, wait):
        n = self.BATCH
        column = i * (2 * n) + (first + half) * n
        if wait:
            pool.wait_ge(self.sent[half], i * (16 * n) + first // 2 * 16 * n)
        self.nc.gpsimd.tensor_tensor(self.slot_sum[:, :], self.slots[:, bass.ds(column + GC, n)],
                                     self.dropped[:, bass.ds(column, n)], ALU.add).then_inc(self.copied, 1)
        self.nc.gpsimd.tensor_copy(self.src_now[:, half], self.src[:, bass.ds(column, n)]).then_inc(self.copied, 1)
        pool.wait_ge(self.copied, i * 6 + (3 * first + 3 * half + 1))
        pool.sem_inc(self.go, 1)
        self.nc.gpsimd.tensor_copy(self.slot_now[:, half], self.slot_sum[:, :]).then_inc(self.copied, 1)
        pool.wait_ge(self.copied, i * 6 + (3 * first + 3 * half + 3))
        pool.sem_inc(self.go, 1)

    def scatter_batch(self, half):
        for k in range(self.BATCH):
            self.scatter(self.slot_now[:, half, k:k + 1], self.src_now[:, half, k:k + 1]).then_inc(self.sent[half], 16)

    def stage_last(self, pool):
        assert self.first == COLS // self.BATCH - 2
        for half in range(2):
            self.stage(pool, self.first, 0, half, True)

    def scatter_last(self, pool):
        for half in range(2):
            self.scatter_batch(half)

    def share(self, batches):
        return lambda pool: self.send(pool, batches)

    def wait_all(self, pool):
        for sent in self.sent:
            pool.wait_ge(sent, COLS // 2 * 16)


def sort_edges(nc, c, edge_index, sorted_src, start_rows, start_i, end_i, sender, batches):
    with Stage(nc, c) as ctx:
        sb = ctx.sb
        ps = ctx.ps
        sem = ctx.sem

        dst = sb("dst", [P, COLS], I32)
        key_i = sb("key_i", [P, COLS], I32)
        row_key = sb("row_key", [P, COLS + 2 * GC], BF16)
        col_key = sb("col_key", [P, COLS + 2 * GC], BF16)
        row_hot = sb("row_hot", [P, 4, GC, P], BF16)
        col_hot = sb("col_hot", [P, 4, GC, TILES], BF16)
        row_hot_t = sb("row_hot_t", [P, 4, GC, P], BF16)
        before = sb("before", [P, 2, GC, P], BF16)
        next_slot = sb("next_slot", [P, GC, TILES], I32)
        parts = sb("parts", [P, 2, 3, GC, TILES], BF16)
        picked = sb("picked", [P, GC, TILES], F32)
        counts = sb("counts", [P, TILES], F32)
        cum = sb("cum", [P, TILES], F32)
        first = sb("first", [P, TILES], F32)
        first1 = sb("first1", [P, TILES], F32)
        zero_fill = sb("zero_fill", [P, 5 * SCOLS // 4], F32)

        loaded, filled = sem("loaded"), sem("filled")
        step, hot_ready, hot_free = sem("step"), sem("hot_ready"), sem("hot_free")

        count_psum = Stage(nc, c)
        count_ps, row_ps = count_psum.ps("count_ps", [P, TILES]), count_psum.ps("row_ps", [P, 1])
        keys_ready, apart_ready, squared, act_hot = sem("keys_ready"), sem("apart_ready"), sem("squared"), sem("act_hot")
        counted, summed, prefixed = sem("counted"), sem("summed"), sem("prefixed")

        BY_ACT = (2, 5, 7)
        hot = count_psum.sb("hot", [P, 8, GC, P + TILES], BF16)
        apart = count_psum.sb("apart", [P, 3, GC, P + TILES], BF16)
        square = count_psum.sb("square", [P, 3, GC, P + TILES], BF16)

        def compare(engine, out, col, op, ready):
            r = row_key[:, bass.ds(col, GC)].unsqueeze(2).to_broadcast([P, GC, P])
            k = col_key[:, bass.ds(col, GC)].unsqueeze(2).to_broadcast([P, GC, TILES])
            engine.tensor_tensor(out[:, :, 0:P], r, c.iota_b[:, :].unsqueeze(1).to_broadcast([P, GC, P]), op)
            engine.tensor_tensor(out[:, :, P:P + TILES], k, c.iota_b[:, 0:TILES].unsqueeze(1).to_broadcast([P, GC, TILES]),
                                 op).then_inc(ready, 1)

        with count_psum, nc.Block() as block:

            @block.sync
            def _(sp):
                sp.dma_start(dst[:, :], edge_index[1].rearrange("(p c) -> p c", p=P)).then_inc(loaded, 16)
                sp.dma_start(sender.src[:, :], edge_index[0].rearrange("(p c) -> p c", p=P)).then_inc(loaded, 16)
                sp.wait_ge(filled, 1)
                sp.dma_start(sorted_src.rearrange("(p c) o -> p (c o)", p=P), zero_fill[:, 0:SCOLS].bitcast(I32)).then_inc(filled, 16)
                for q in range(4):
                    n = 5 * SCOLS // 4
                    sp.dma_start(start_rows.rearrange("(p c) o -> p (c o)", p=P)[:, q * n:(q + 1) * n],
                                 zero_fill[:, 0:n]).then_inc(filled, 16)
                sp.wait_ge(filled, 1 + 16 * 5)

            @block.gpsimd
            def _(pool):
                nc.gpsimd.memset(zero_fill[:, :], 0.0).then_inc(filled, 1)
                nc.gpsimd.memset(parts[:, 1], 0.0)
                nc.gpsimd.memset(before[:, 1], 0.0)
                nc.gpsimd.memset(row_hot[:, 3], 0.0)
                nc.gpsimd.memset(row_hot_t[:, 3], 0.0)
                nc.gpsimd.memset(col_hot[:, 3], 0.0)
                pool.wait_ge(keys_ready, 1)
                pool.sem_inc(squared, 3)
                with pool.Fori(0, GROUPS // 8) as i:
                    for j, u in enumerate(BY_ACT):
                        pool.wait_ge(squared, 3 * i + (j + 1))
                        compare(nc.gpsimd, apart[:, j], i * (8 * GC) + u * GC, ALU.subtract, apart_ready)

            @block.scalar
            def _(act):
                with act.Fori(0, GROUPS // 8) as i:
                    for j, u in enumerate(BY_ACT):
                        act.wait_ge(apart_ready, 3 * i + (j + 1))
                        act.wait_ge(act_hot, 3 * i + (j + 1))
                        nc.scalar.activation(square[:, j], apart[:, j], ACT.Square).then_inc(squared, 1)
                        act.wait_ge(squared, 3 * i + (j + 4))
                        act.wait_ge(hot_free, 8 * i + (u + 1))
                        nc.scalar.activation(hot[:, u], square[:, j], ACT.Relu, scale=-1.0, bias=c.ones[:, 0:1]).then_inc(act_hot, 1)

            @block.vector
            def _(dve):
                done = Done(step)
                dve.wait_ge(loaded, 32)
                done.add(nc.vector.tensor_scalar(key_i[:, :], dst[:, :], 6, None, ALU.logical_shift_right))
                done.wait(dve)
                done.add(nc.vector.tensor_scalar(row_key[:, 0:COLS], key_i[:, :], 255.0, None, ALU.min))
                nc.vector.tensor_scalar(sender.dropped[:, :], key_i[:, :], float(P), float(DROPPED), ALU.is_ge, ALU.mult)
                done.add(nc.vector.tensor_scalar(sender.src[:, :], sender.src[:, :], float(NODES - 1), None, ALU.min))
                done.add(nc.vector.tensor_scalar(dst[:, :], dst[:, :], TILES - 1, None, ALU.bitwise_and))
                nc.vector.memset(row_key[:, COLS:COLS + 2 * GC], 255.0)
                nc.vector.memset(col_key[:, COLS:COLS + 2 * GC], 0.0)
                done.wait(dve)
                done.add(nc.vector.tensor_copy(col_key[:, 0:COLS], dst[:, :]))
                done.wait(dve)
                dve.sem_inc(keys_ready, 1)
                with dve.Fori(0, GROUPS // 8) as i:
                    for j, u in enumerate(u for u in range(8) if u not in BY_ACT):
                        dve.wait_ge(hot_free, 8 * i + (u + 1))
                        compare(nc.vector, hot[:, u], i * (8 * GC) + u * GC, ALU.is_equal, hot_ready)
                dve.wait_ge(counted, 1)
                done.add(nc.vector.tensor_copy(counts[:, :], count_ps[:, :]))
                done.wait(dve)
                done.add(nc.vector.tensor_scalar_add(first[:, :], counts[:, :], 1.0))
                done.wait(dve)
                nc.vector.tensor_tensor_scan(cum[:, :], c.zeros[:, 0:TILES], first[:, :], 0.0, ALU.add, ALU.add).then_inc(summed, 1)
                dve.wait_ge(prefixed, 1)
                dve.wait_ge(summed, 1)
                done.add(nc.vector.tensor_tensor(first[:, :], cum[:, :], first[:, :], ALU.subtract))
                done.wait(dve)
                done.add(nc.vector.tensor_scalar(first[:, :], first[:, :], row_ps[:, 0:1], None, ALU.add))
                done.wait(dve)
                nc.vector.tensor_copy(start_i[:, :], first[:, :])
                nc.vector.tensor_scalar_add(first1[:, :], first[:, :], 1.0)
                nc.vector.tensor_tensor(end_i[:, :], first[:, :], counts[:, :], ALU.add)

            @block.tensor
            def _(pe):
                pe.sem_inc(hot_free, 8)
                nc.tensor.matmul(count_ps[:, :], c.zeros[:, 0:P], c.zeros[:, 0:TILES], start=True, stop=True)
                pe.sem_inc(act_hot, 3)
                with pe.Fori(0, GROUPS // 8) as i:
                    for u in range(8):
                        earlier = sum(v < u for v in BY_ACT)
                        if u in BY_ACT:
                            pe.wait_ge(act_hot, 3 * i + (earlier + 4))
                        else:
                            pe.wait_ge(hot_ready, 5 * i + (u - earlier + 1))
                        for k in range(GC):
                            last = nc.tensor.matmul(count_ps[:, :], hot[:, u, k, 0:P], hot[:, u, k, P:P + TILES],
                                                    start=False, stop=True, skip_group_check=True)
                        last.then_inc(hot_free, 1)
                nc.tensor.matmul(count_ps[:, :], c.zeros[:, 0:P], c.zeros[:, 0:TILES], start=False, stop=True,
                                 skip_group_check=True).then_inc(counted, 1)
                pe.wait_ge(summed, 1)
                nc.tensor.matmul(row_ps[:, :], c.upper[:, :], cum[:, TILES - 1:TILES], start=True, stop=True).then_inc(prefixed, 1)

        hot_ready2 = sem("hot_ready2")
        turned, turned_sb, same_ready, before_ready = sem("turned"), sem("turned_sb"), sem("same_ready"), sem("before_ready")
        counted2, copied, parts_ready, slots_ps_ready = sem("counted2"), sem("copied"), sem("parts_ready"), sem("slots_ps_ready")
        multiplied, slots_ready = sem("multiplied"), sem("slots_ready")
        turn_ps = ps("turn_ps", [P, GC, P], BF16)
        same_ps = ps("same_ps", [P, GC, P])
        run_ps = ps("run_ps", [P, GC, TILES])
        slots_ps = [ps(f"slots_ps{j}", [P, GC, TILES]) for j in range(2)]

        with nc.Block() as block:

            @block.vector
            def _(dve):
                def build_rows(buf, col):
                    r = row_key[:, bass.ds(col, GC)].unsqueeze(2).to_broadcast([P, GC, P])
                    nc.vector.tensor_tensor(row_hot[:, buf], r, c.iota_b[:, :].unsqueeze(1).to_broadcast([P, GC, P]),
                                            ALU.is_equal).then_inc(hot_ready2, 1)

                def build_cols(buf, col):
                    k = col_key[:, bass.ds(col, GC)].unsqueeze(2).to_broadcast([P, GC, TILES])
                    nc.vector.tensor_tensor(col_hot[:, buf], k, c.iota_b[:, 0:TILES].unsqueeze(1).to_broadcast([P, GC, TILES]),
                                            ALU.is_equal).then_inc(hot_ready2, 1)

                def multiply(buf, half, number):
                    dve.wait_ge(slots_ready, number)
                    dve.wait_ge(slots_ps_ready, number)
                    nc.vector.tensor_tensor(picked[:, :, :], slots_ps[half][:, :, :], col_hot[:, buf], ALU.mult).then_inc(multiplied, 1)

                def gather(col, number):
                    dve.wait_ge(multiplied, number)
                    nc.vector.tensor_reduce(sender.slots[:, bass.ds(col, GC)], picked[:, :, :], AX.X, ALU.add).then_inc(slots_ready, 1)

                dve.sem_inc(slots_ready, 1)
                for u in range(2):
                    build_rows(u, u * GC)
                    build_cols(u, u * GC)
                with dve.Fori(0, GROUPS // 4) as i:
                    for u in range(4):
                        g1 = 4 * i + (u + 1)
                        dve.wait_ge(same_ready, g1)
                        nc.vector.tensor_tensor(before[:, u % 2], same_ps[:, :, :],
                                                c.upper_b[:, :].unsqueeze(1).to_broadcast([P, GC, P]),
                                                ALU.mult).then_inc(before_ready, 1)
                        build_rows((u + 2) % 4, i * (4 * GC) + (u + 2) * GC)
                        multiply((u + 3) % 4, (u + 1) % 2, g1)
                        build_cols((u + 2) % 4, i * (4 * GC) + (u + 2) * GC)
                        gather(i * (4 * GC) + u * GC, g1)
                multiply(3, 1, GROUPS + 1)
                gather(COLS, GROUPS + 1)

            @block.tensor
            def _(pe):
                def turn(buf):
                    for k in range(GC):
                        last = nc.tensor.transpose(turn_ps[:, k], row_hot[:, buf, k], c.ident_b[:, :])
                    last.then_inc(turned, 1)

                def slots(half, buf):
                    for k in range(GC):
                        for byte in range(3):
                            nc.tensor.matmul(slots_ps[half][:, k], row_hot_t[:, buf, k], parts[:, half, byte, k],
                                             start=(byte == 0), stop=False)
                        last = nc.tensor.matmul(slots_ps[half][:, k], before[:, half, k], col_hot[:, buf, k], start=False, stop=True)
                    last.then_inc(slots_ps_ready, 1)

                def count(buf, k, a, b):
                    return nc.tensor.matmul(run_ps[:, a:b], row_hot[:, buf, k],
                                            col_hot[:, buf, k].unsqueeze(1).to_broadcast([P, b - a, TILES]),
                                            start=False, stop=True, skip_group_check=True)

                nc.tensor.matmul(run_ps[:, :, :], c.ident[:, :], first1[:, :].unsqueeze(1).to_broadcast([P, GC, TILES]),
                                 start=True, stop=True)
                pe.wait_ge(hot_ready2, 2)
                turn(0)
                with pe.Fori(0, GROUPS // 4) as i:
                    for u in range(4):
                        g1 = 4 * i + (u + 1)
                        pe.wait_ge(turned_sb, g1)
                        pe.wait_ge(before_ready, g1)
                        for k in range(GC):
                            last = nc.tensor.matmul(same_ps[:, k], row_hot_t[:, u, k], row_hot_t[:, u, k], start=True, stop=True)
                        last.then_inc(same_ready, 1)
                        pe.wait_ge(copied, g1)
                        for k in range(GC):
                            count((u + 3) % 4, k, 0, k + 1)
                        for k in range(GC - 1):
                            last = count(u, k, k + 1, GC)
                        last.then_inc(counted2, 1)
                        pe.wait_ge(hot_ready2, i * 8 + (2 * u + 4))
                        turn((u + 1) % 4)
                        pe.wait_ge(parts_ready, i * 12 + (3 * u + 3))
                        slots((u + 1) % 2, (u + 3) % 4)
                pe.wait_ge(before_ready, GROUPS + 1)
                pe.wait_ge(parts_ready, 3 * GROUPS + 3)
                slots(1, 3)

            @block.scalar
            def _(act):
                act.sem_inc(before_ready, 1)
                act.sem_inc(copied, 1)
                act.sem_inc(parts_ready, 3)
                act.wait_ge(turned, 1)
                nc.scalar.copy(row_hot_t[:, 0], turn_ps[:, :, :]).then_inc(turned_sb, 1)
                with act.Fori(0, GROUPS // 4) as i:
                    for u in range(4):
                        act.wait_ge(counted2, 4 * i + (u + 1))
                        act.wait_ge(parts_ready, i * 12 + (3 * u + 3))
                        nc.scalar.copy(next_slot[:, :, :], run_ps[:, :, :]).then_inc(copied, 1)
                        act.wait_ge(turned, 4 * i + (u + 2))
                        nc.scalar.copy(row_hot_t[:, (u + 1) % 4], turn_ps[:, :, :]).then_inc(turned_sb, 1)
                        act.wait_ge(copied, 4 * i + (u + 2))
                        for byte in range(3):
                            nc.scalar.activation(parts[:, u % 2, byte], next_slot[:, :, :].bitcast(U8)[:, :, byte::4],
                                                 ACT.Copy, scale=float(256 ** byte)).then_inc(parts_ready, 1)

            @block.gpsimd
            def _(pool):
                sender.send(pool, batches, slots_ready)


VOCAB, HEADS0, KEYS = 256, 8, 255
EPS = 1e-5


def load_all(engine, pairs, sem):
    for tile, array in pairs:
        engine.dma_start(tile, array).then_inc(sem, 16)


def on_every_partition(array, n):
    return array.rearrange("(o n) -> o n", o=1).to_broadcast([P, n])


class Norm:

    def __init__(self, nc, ctx, name, T, n):
        self.nc, self.T, self.n = nc, T, n
        self.mean = ctx.sb(name + "_mean", [P, T])
        self.var = ctx.sb(name + "_var", [P, T])
        self.std = ctx.sb(name + "_std", [P, T])
        self.inv = ctx.sb(name + "_inv", [P, T])
        self.var_ready = ctx.sem(name + "_var_ready")
        self.std_ready = ctx.sem(name + "_std_ready")

    def wide(self, stat):
        return stat[:, :].unsqueeze(2).to_broadcast([P, self.T, self.n])

    def centre(self, dve, done, x, centred, square):
        v = self.nc.vector
        done.add(v.tensor_reduce(self.mean[:, :], x, AX.X, ALU.add))
        done.wait(dve)
        done.add(v.tensor_scalar_mul(self.mean[:, :], self.mean[:, :], 1.0 / self.n))
        done.wait(dve)
        done.add(v.tensor_tensor(centred, x, self.wide(self.mean), ALU.subtract))
        done.wait(dve)
        done.add(v.tensor_tensor(square, centred, centred, ALU.mult))
        done.wait(dve)
        done.add(v.tensor_reduce(self.var[:, :], square, AX.X, ALU.add))
        done.wait(dve)
        v.tensor_scalar(self.var[:, :], self.var[:, :], 1.0 / self.n, EPS, ALU.mult, ALU.add).then_inc(self.var_ready, 1)
        dve.wait_ge(self.std_ready, 1)
        done.add(v.reciprocal(self.inv[:, :], self.std[:, :]))
        done.wait(dve)

    def root(self, act):
        act.wait_ge(self.var_ready, 1)
        self.nc.scalar.activation(self.std[:, :], self.var[:, :], ACT.Sqrt).then_inc(self.std_ready, 1)


def token_tables(nc, c, w, tab_h, tab_x, tab_xt, meanwhile=None):
    with Stage(nc, c) as ctx:
        sb = ctx.sb
        sem = ctx.sem

        emb_t, w1_t, b1 = sb("emb_t", [D, VOCAB]), sb("w1_t", [D, D]), sb("b1", [D, 1])
        w2_t, gamma, beta = sb("w2_t", [D + 1, D]), sb("gamma", [P, D]), sb("beta", [P, D])
        hid = sb("hid", [D + 1, VOCAB])
        centred, square = sb("centred", [P, 2, D]), sb("square", [P, 2, D])
        hid_ps = ctx.ps("hid_ps", [D, VOCAB])
        out_ps = ctx.ps("out_ps", [P, 2, D])
        xt_ps = ctx.ps("xt_ps", [D, VOCAB])
        loaded, hid_done, act_done, out_done, x_done, xt_done, step = map(
            sem, ("loaded", "hid_done", "act_done", "out_done", "x_done", "xt_done", "step"))
        n1, n2 = Norm(nc, ctx, "n1", 2, D), Norm(nc, ctx, "n2", 2, D)
        with nc.Block() as block:
            if meanwhile:

                @block.gpsimd
                def _(pool):
                    meanwhile(pool)

            @block.sync
            def _(sp):
                load_all(sp, [(emb_t[:, :], w["emb_t"]), (w1_t[:, :], w["tok_w1_t"]), (b1[:, :], w["tok_b1"]),
                              (w2_t[:, :], w["tok_w2_t"]), (gamma[:, :], on_every_partition(w["tok_gamma"], D)),
                              (beta[:, :], on_every_partition(w["tok_beta"], D))], loaded)

            @block.tensor
            def _(pe):
                pe.wait_ge(loaded, 16 * 6)
                nc.tensor.matmul(hid_ps[:, :], w1_t[:, :], emb_t[:, :], start=True, stop=True).then_inc(hid_done, 1)
                pe.wait_ge(act_done, 2)
                for j in range(2):
                    last = nc.tensor.matmul(out_ps[:, j], hid[:, j * P:(j + 1) * P], w2_t[:, :], start=True, stop=True)
                last.then_inc(out_done, 1)
                pe.wait_ge(x_done, 1)
                for j in range(2):
                    last = nc.tensor.transpose(xt_ps[:, j * P:(j + 1) * P], tab_x[:, j], c.ident[:, :])
                last.then_inc(xt_done, 1)

            @block.scalar
            def _(act):
                act.wait_ge(loaded, 16 * 6)
                act.wait_ge(hid_done, 1)
                nc.scalar.activation(hid[0:D, :], hid_ps[:, :], ACT.Relu, bias=b1[:, 0:1]).then_inc(act_done, 1)
                n1.root(act)
                n2.root(act)

            @block.vector
            def _(dve):
                done = Done(step)
                nc.vector.memset(tab_xt[D:D + 1, :], 1.0)
                nc.vector.memset(hid[D:D + 1, :], 1.0).then_inc(act_done, 1)
                dve.wait_ge(loaded, 16 * 6)
                dve.wait_ge(out_done, 1)
                n1.centre(dve, done, out_ps[:, :, :], centred[:, :, :], square[:, :, :])
                done.add(nc.vector.tensor_tensor(centred[:, :, :], centred[:, :, :], n1.wide(n1.inv), ALU.mult))
                done.wait(dve)
                done.add(nc.vector.tensor_tensor(centred[:, :, :], centred[:, :, :],
                                                 gamma[:, :].unsqueeze(1).to_broadcast([P, 2, D]), ALU.mult))
                done.wait(dve)
                done.add(nc.vector.tensor_tensor(tab_h[:, :, :], centred[:, :, :],
                                                 beta[:, :].unsqueeze(1).to_broadcast([P, 2, D]), ALU.add))
                done.wait(dve)
                n2.centre(dve, done, tab_h[:, :, :], centred[:, :, :], square[:, :, :])
                nc.vector.tensor_tensor(tab_x[:, :, :], centred[:, :, :], n2.wide(n2.inv), ALU.mult).then_inc(x_done, 1)
                dve.wait_ge(xt_done, 1)
                nc.vector.tensor_copy(tab_xt[0:D, :], xt_ps[:, :])


def word_attention(nc, c, w, h, tab_h, tab_x, tab_xt, words, chosen, chosen_table, plain_table, meanwhile=None):
    HALF, BLOCKS, PAIRS = 64, VOCAB // 64, HEADS0 // 2
    with Stage(nc, c) as ctx:
        sb = ctx.sb
        ps = ctx.ps
        sem = ctx.sem

        wq_t, wv_t = sb("wq_t", [D + 1, PAIRS, 2, D]), sb("wv_t", [D + 1, PAIRS, 2, D])
        wk, fan_t, fan_b = sb("wk", [P, PAIRS]), sb("fan_t", [D + 1, D]), sb("fan_b", [P, D])
        query = sb("query", [P, PAIRS, VOCAB])
        key = sb("key", [P, PAIRS, VOCAB])
        value = sb("value", [P, BLOCKS, PAIRS, D])
        count = sb("count", [P, BLOCKS, BATCH])
        match, negkey = sb("match", [P, SEQ]), sb("negkey", [P, SEQ])
        block_word_i, block_word = sb("block_word_i", [P, BLOCKS], I32), sb("block_word", [P, BLOCKS])
        weighed = sb("weighed", [P, BLOCKS, PAIRS, BATCH, D])
        twice = sb("twice", [D, 2, D])
        pick = sb("pick", [P, 3 * HALF - 1])
        minus_half = sb("minus_half", [P, 2, HALF])
        key_sum = sb("key_sum", [P, PAIRS, BLOCKS])
        gap = sb("gap", [P, 8, VOCAB])
        e = h[:, :, :].rearrange("p t d -> p (t d)").rearrange("p (b a v) -> p b a v", b=BLOCKS, a=PAIRS)
        den, total = sb("den", [P, BATCH]), sb("total", [P, 2, BATCH, D])
        part = sb("part", [P, BATCH, D])
        gate = sb("gate", [P, 2, BATCH, D])
        mixed_t = sb("mixed_t", [D + 1, 2, BATCH, P])
        base = sb("base", [P, 2, D])
        q_ps, k_ps = [ps(f"q_ps{j}", [P, 2, VOCAB]) for j in range(2)], ps("k_ps", [P, VOCAB])
        v_ps = ps("v_ps", [P, PAIRS, D])
        dist_ps = [ps(f"dist_ps{j}", [P, VOCAB]) for j in range(2)]
        num_ps, den_ps = ps("num_ps", [P, BATCH, D]), ps("den_ps", [P, BATCH])
        loaded, consts, picked, q_done, q_read, k_done, v_done, v_read = map(
            sem, ("loaded", "consts", "picked", "q_done", "q_read", "k_done", "v_done", "v_read"))
        keys_ready, gap_v, gap_s, gap_free, dist_read = map(
            sem, ("keys_ready", "gap_v", "gap_s", "gap_free", "dist_read"))
        weighed_ready, num_done, num_read, gate_in, gate_out, turn_in, turn_out, step, astep = map(
            sem, ("weighed_ready", "num_done", "num_read", "gate_in", "gate_out", "turn_in", "turn_out", "step",
                  "astep"))

        with nc.Block() as block:

            @block.sync
            def _(sp):
                load_all(sp, [(wq_t[:, :, :, :], w["wq_t"].rearrange("i (a h o) -> i a h o", a=PAIRS, h=2)),
                              (wv_t[:, :, :, :], w["wv_t"].rearrange("i (a h o) -> i a h o", a=PAIRS, h=2)),
                              (wk[:, :], w["wk_pairs"]), (fan_t[:, :], w["fan_t"]),
                              (fan_b[:, :], w["fan_t"][D:D + 1, :].to_broadcast([P, D]))], loaded)

            @block.gpsimd
            def _(pool):
                nc.gpsimd.memset(pick[:, :], 0.0)
                nc.gpsimd.iota(block_word_i[:, :], [[HALF, BLOCKS]], base=0, channel_multiplier=1).then_inc(consts, 1)
                meanwhile(pool)

            @block.tensor
            def _(pe):
                pe.wait_ge(loaded, 16 * 5)
                pe.wait_ge(picked, 1)
                for a in range(PAIRS):
                    if a >= 2:
                        pe.wait_ge(q_read, a - 1)
                    nc.tensor.matmul(q_ps[a % 2][:, 0], wq_t[:, a], tab_xt[:, :], start=True, stop=True).then_inc(q_done, 1)
                nc.tensor.matmul(k_ps[:, :], twice[:, :, :], tab_xt[0:D, :], start=True, stop=True).then_inc(k_done, 1)
                for b in range(BLOCKS):
                    if b:
                        pe.wait_ge(v_read, b)
                    for h in range(2):
                        last = nc.tensor.matmul(v_ps[h * HALF:(h + 1) * HALF], tab_xt[:, b * HALF:(b + 1) * HALF],
                                                wv_t[:, :, h], start=True, stop=True)
                    last.then_inc(v_done, 1)
                pe.wait_ge(keys_ready, 1)
                for a in range(PAIRS):
                    for b in range(BLOCKS):
                        for h in range(2):
                            r = slice(h * HALF, (h + 1) * HALF)
                            last = nc.tensor.matmul(k_ps[r, a * BLOCKS + b:a * BLOCKS + b + 1], key[r, a, b * HALF:(b + 1) * HALF],
                                                    c.ones[r, 0:1], start=True, stop=True)
                last.then_inc(k_done, 1)
                pe.sem_inc(gap_free, 8)
                with pe.Fori(0, PAIRS) as a, pe.Fori(0, BLOCKS // 2) as j:
                    i = a * 2 + j
                    for half in range(2):
                        pe.wait_ge(dist_read, 2 * i + (half + 1))
                        nc.tensor.matmul(dist_ps[half][:, :], minus_half[:, :, :], query[:, bass.ds(a, 1)].squeeze(1), start=True, stop=False)
                        for u in range(HALF):
                            if u % 8 < 5:
                                pe.wait_ge(gap_v, i * (2 * 40) + (half * 40 + u // 8 * 5 + u % 8 + 1))
                            else:
                                pe.wait_ge(gap_s, i * (2 * 24) + (half * 24 + u // 8 * 3 + u % 8 - 4))
                            last = nc.tensor.matmul(dist_ps[half][:, :], pick[:, HALF - 1 - u:3 * HALF - 1 - u], gap[:, u % 8],
                                                    start=False, stop=(u == HALF - 1))
                            last.then_inc(gap_free, 1)
                pe.wait_ge(weighed_ready, 1)
                pe.wait_ge(dist_read, 2 + BLOCKS * PAIRS)
                n = 0
                for dh in range(2):
                    for a in range(PAIRS):
                        for h in range(2):
                            if n:
                                pe.wait_ge(num_read, n)
                            r = slice(h * HALF, (h + 1) * HALF)
                            for b in range(BLOCKS):
                                nc.tensor.matmul(num_ps[:, :, :], e[r, b, a, dh * P:(dh + 1) * P], weighed[r, b, a],
                                                 start=(b == 0), stop=(b == BLOCKS - 1))
                            for b in range(BLOCKS):
                                last = nc.tensor.matmul(den_ps[:, :], e[r, b, a, dh * P:(dh + 1) * P], count[r, b],
                                                        start=(b == 0), stop=(b == BLOCKS - 1))
                            last.then_inc(num_done, 1)
                            n += 1
                pe.wait_ge(turn_in, 1)
                for n in range(2 * BATCH // 4):
                    if n >= 2:
                        pe.wait_ge(turn_out, n - 1)
                    for k in range(4):
                        m = 4 * n + k
                        last = nc.tensor.transpose(q_ps[n % 2][0:D, k // 2, (k % 2) * P:(k % 2 + 1) * P], gate[:, m // BATCH, m % BATCH], c.ident[:, :])
                    last.then_inc(q_done, 1)
                pe.wait_ge(turn_out, 2 * BATCH // 4)
                for dh in range(2):
                    pe.wait_ge(num_read, 2 * HEADS0 + dh)
                    for b in range(BATCH):
                        last = nc.tensor.matmul(num_ps[:, b], mixed_t[:, dh, b], fan_t[:, :], start=True, stop=True)
                    last.then_inc(num_done, 1)

            @block.vector
            def _(dve):
                done = Done(step)
                dve.wait_ge(loaded, 16 * 5)
                dve.wait_ge(consts, 1)
                done.add(nc.vector.tensor_copy(block_word[:, :], block_word_i[:, :]))
                nc.vector.memset(mixed_t[D:D + 1, :, :, :], 1.0)
                for h in range(2):
                    nc.vector.memset(minus_half[h * HALF:(h + 1) * HALF, h], -0.5)
                    nc.vector.memset(minus_half[h * HALF:(h + 1) * HALF, 1 - h], 0.0)
                    nc.vector.memset(pick[h * HALF:(h + 1) * HALF, (h + 1) * HALF - 1:(h + 1) * HALF], 1.0)
                    last = nc.vector.tensor_copy(twice[:, h], c.ident[0:D, 0:D])
                last.then_inc(picked, 1)
                done.wait(dve)
                done.add(nc.vector.tensor_scalar_add(block_word[HALF:P, :], block_word[HALF:P, :], float(-HALF)))
                for a in range(PAIRS):
                    dve.wait_ge(q_done, a + 1)
                    nc.vector.tensor_copy(query[:, a], q_ps[a % 2][:, 0]).then_inc(q_read, 1)
                dve.wait_ge(k_done, 1)
                for a in range(PAIRS):
                    last = nc.vector.tensor_scalar(key[:, a], k_ps[:, :], wk[:, a:a + 1], None, ALU.mult)
                last.then_inc(keys_ready, 1)
                for b in range(BLOCKS):
                    dve.wait_ge(v_done, b + 1)
                    nc.vector.tensor_copy(value[:, b], v_ps[:, :, :]).then_inc(v_read, 1)
                dve.wait_ge(keys_ready, 1)
                dve.wait_ge(k_done, 2)
                nc.vector.tensor_scalar_mul(key_sum[:, :, :], k_ps[:, 0:PAIRS * BLOCKS].rearrange("p (a b) -> p a b", a=PAIRS),
                                            -1.0 / D ** 0.5).then_inc(keys_ready, 1)
                with dve.Fori(0, PAIRS) as a, dve.Fori(0, BLOCKS // 2) as j:
                    i = a * 2 + j
                    for half in range(2):
                        for u in range(HALF):
                            if u % 8 < 5:
                                dve.wait_ge(gap_free, i * (2 * HALF) + (half * HALF + u + 1))
                                nc.vector.tensor_scalar(gap[:, u % 8], query[:, bass.ds(a, 1)].squeeze(1),
                                                        key[:, :, :].rearrange("p a u -> p (a u)")[:, bass.ds(i * (2 * HALF) + (half * HALF + u), 1)],
                                                        0.0, ALU.subtract, ALU.max).then_inc(gap_v, 1)
                for b in range(BLOCKS):
                    for s in range(BATCH):
                        done.wait(dve)
                        done.add(nc.vector.scalar_tensor_tensor(
                            match[:, :], words[:, s * SEQ:(s + 1) * SEQ], block_word[:, b:b + 1], chosen[:, :],
                            ALU.is_equal, ALU.mult, accum_out=count[:, b, s:s + 1]))
                done.wait(dve)
                for b in range(BLOCKS):
                    for a in range(PAIRS):
                        last = nc.vector.tensor_tensor(weighed[:, b, a], count[:, b].unsqueeze(2).to_broadcast([P, BATCH, D]),
                                                       value[:, b, a].unsqueeze(1).to_broadcast([P, BATCH, D]), ALU.mult)
                last.then_inc(weighed_ready, 1)
                n = 0
                for dh in range(2):
                    done.add(nc.vector.memset(total[:, dh], 0.0))
                    for a in range(HEADS0):
                        dve.wait_ge(num_done, n + 1)
                        done.add(nc.vector.tensor_scalar_add(den[:, :], den_ps[:, :], 1.0))
                        done.wait(dve)
                        done.add(nc.vector.reciprocal(den[:, :], den[:, :]))
                        done.wait(dve)
                        nc.vector.tensor_tensor(part[:, :, :], num_ps[:, :, :], den[:, :].unsqueeze(2).to_broadcast([P, BATCH, D]),
                                                ALU.mult).then_inc(num_read, 1)
                        dve.wait_ge(num_read, n + 1)
                        done.add(nc.vector.tensor_tensor(total[:, dh], total[:, dh], part[:, :, :], ALU.add))
                        done.wait(dve)
                        n += 1
                nc.vector.sem_inc(gate_in, 1)
                dve.wait_ge(gate_out, 1)
                done.add(nc.vector.tensor_scalar_add(gate[:, :, :, :], gate[:, :, :, :], 1.0))
                done.wait(dve)
                done.add(nc.vector.reciprocal(gate[:, :, :, :], gate[:, :, :, :]))
                done.wait(dve)
                nc.vector.tensor_tensor(gate[:, :, :, :], gate[:, :, :, :], total[:, :, :, :], ALU.mult).then_inc(turn_in, 1)
                for n in range(2 * BATCH // 4):
                    dve.wait_ge(q_done, PAIRS + n + 1)
                    nc.vector.tensor_copy(mixed_t[0:D, n // 2, (n % 2) * 4:(n % 2) * 4 + 4],
                                          q_ps[n % 2][0:D].rearrange("d a (k p) -> d (a k) p", k=2)).then_inc(turn_out, 1)
                done.add(nc.vector.tensor_tensor(base[:, :, :], tab_h[:, :, :], tab_x[:, :, :], ALU.add))
                done.wait(dve)
                nc.vector.tensor_tensor(plain_table[:, :, :], base[:, :, :], fan_b[:, :].unsqueeze(1).to_broadcast([P, 2, D]), ALU.add)
                for dh in range(2):
                    dve.wait_ge(num_done, 2 * HEADS0 + dh + 1)
                    nc.vector.tensor_tensor(chosen_table[:, dh], num_ps[:, :, :], base[:, dh].unsqueeze(1).to_broadcast([P, BATCH, D]),
                                            ALU.add).then_inc(num_read, 1)

            @block.scalar
            def _(act):
                act.wait_ge(keys_ready, 2)
                nc.scalar.mul(negkey[:, :], key[:, :, :].rearrange("p a u -> p (a u)"), -1.0).then_inc(astep, 1)
                act.wait_ge(astep, 1)
                act.sem_inc(dist_read, 2)
                with act.Fori(0, PAIRS) as a, act.Fori(0, BLOCKS // 2) as j:
                    i = a * 2 + j
                    for half in range(2):
                        for u in range(HALF):
                            if u % 8 >= 5:
                                act.wait_ge(gap_free, i * (2 * HALF) + (half * HALF + u + 1))
                                nc.scalar.activation(gap[:, u % 8], query[:, bass.ds(a, 1)].squeeze(1), ACT.Relu,
                                                     bias=negkey[:, bass.ds(i * (2 * HALF) + (half * HALF + u), 1)]).then_inc(gap_s, 1)
                        act.wait_ge(gap_free, i * (2 * HALF) + (8 + (half + 1) * HALF))
                        nc.scalar.activation(e[:, :, :, :].rearrange("p b a v -> p (b a) v")[:, bass.ds(j * (2 * PAIRS) + (a + half * PAIRS), 1)].squeeze(1),
                                             dist_ps[half][:, :], ACT.Exp, scale=-2.0 / D ** 0.5,
                                             bias=key_sum[:, :, :].rearrange("p a b -> p (a b)")[:, bass.ds(2 * i + half, 1)]).then_inc(dist_read, 1)
                act.wait_ge(gate_in, 1)
                nc.scalar.activation(gate[:, :, :, :], total[:, :, :, :], ACT.Exp, scale=-1.702).then_inc(gate_out, 1)


def load_words(nc, c, w, words, chosen, meanwhile=None):
    with Stage(nc, c) as ctx:
        sb = ctx.sb

        words_i = sb("words_i", [P, NODES], I32)
        named_i, named = sb("named_i", [P, 2], I32), sb("named", [P, 2])
        place_i, place = sb("place_i", [P, SEQ], I32), sb("place", [P, SEQ])
        names = sb("names", [P, 2, SEQ], BF16)
        ones_b = sb("ones_b", [P, P], BF16)
        count_ps = ctx.ps("named_ps", [P, 2, SEQ // 2])
        loaded, made, named_loaded, names_ready, counted, step = (
            ctx.sem(n) for n in ("loaded", "made", "named_loaded", "names_ready", "counted", "step"))
        with nc.Block() as block:

            @block.gpsimd
            def _(pool):
                nc.gpsimd.iota(place_i[:, :], [[1, SEQ]], base=0, channel_multiplier=0)
                nc.gpsimd.memset(named_i[:, :], -1).then_inc(made, 1)
                meanwhile(pool)

            @block.sync
            def _(sp):
                sp.dma_start(words_i[:, :], on_every_partition(w["tokens"], NODES)).then_inc(loaded, 16)
                sp.wait_ge(made, 1)
                with nc.allow_non_contiguous_dma(reason="255 words"):
                    sp.dma_start(named_i[:, 0:1], w["a2a"][0:P].rearrange("(p o) -> p o", o=1)).then_inc(named_loaded, 16)
                    sp.dma_start(named_i[0:KEYS - P, 1:2], w["a2a"][P:KEYS].rearrange("(p o) -> p o", o=1)).then_inc(named_loaded, 16)

            @block.vector
            def _(dve):
                done = Done(step)
                nc.vector.memset(ones_b[:, :], 1.0)
                dve.wait_ge(named_loaded, 32)
                nc.vector.tensor_copy(named[:, :], named_i[:, :])
                done.add(nc.vector.tensor_copy(place[:, :], place_i[:, :]))
                done.wait(dve)
                for j in range(2):
                    last = nc.vector.tensor_scalar(names[:, j], place[:, :], named[:, j:j + 1], None, ALU.is_equal)
                last.then_inc(names_ready, 1)
                dve.wait_ge(counted, 1)
                nc.vector.tensor_copy(chosen[:, :].rearrange("p (a n) -> p a n", a=2), count_ps[:, :, :])
                dve.wait_ge(loaded, 16)
                nc.vector.tensor_copy(words[:, :], words_i[:, :])

            @block.tensor
            def _(pe):
                pe.wait_ge(names_ready, 1)
                for q in range(2):
                    for j in range(2):
                        last = nc.tensor.matmul(count_ps[:, q], ones_b[:, :], names[:, j, q * (SEQ // 2):(q + 1) * (SEQ // 2)],
                                                start=(j == 0), stop=(j == 1))
                last.then_inc(counted, 1)


def look_up(nc, c, words, chosen, chosen_table, plain_table, node_t, meanwhile=None):
    HALF = SEQ // 2
    with Stage(nc, c) as ctx:
        sb = ctx.sb

        is_named, not_named = sb("is_named", [P, SEQ]), sb("not_named", [P, SEQ])
        named_word, plain_word = sb("named_word", [P, SEQ]), sb("plain_word", [P, SEQ])
        hot = sb("hot", [P, 2, 2, 2, HALF])
        node_ps = [ctx.ps(f"node_ps{j}", [D, HALF]) for j in range(2)]
        step, hot_ready, hot_used, copied = (
            ctx.sem(n) for n in ("step", "hot_ready", "hot_used", "copied"))
        with nc.Block() as block:
            if meanwhile:

                @block.gpsimd
                def _(pool):
                    meanwhile(pool)

            @block.vector
            def _(dve):
                done = Done(step)
                done.add(nc.vector.tensor_scalar(is_named[:, :], chosen[:, :], 1.0, None, ALU.min))
                done.wait(dve)
                done.add(nc.vector.tensor_scalar(not_named[:, :], is_named[:, :], -1.0, 1.0, ALU.mult, ALU.add))
                done.wait(dve)
                for s in range(BATCH):
                    x = words[:, s * SEQ:(s + 1) * SEQ]
                    if s:
                        dve.wait_ge(hot_ready, 2 * s)
                    for out, mask in ((named_word, is_named), (plain_word, not_named)):
                        done.add(nc.vector.scalar_tensor_tensor(out[:, :], x, 1.0, mask[:, :], ALU.add, ALU.mult))
                    done.wait(dve)
                    for out in (named_word, plain_word):
                        done.add(nc.vector.tensor_scalar_add(out[:, :], out[:, :], -1.0))
                    done.wait(dve)
                    for half in range(2):
                        if s:
                            dve.wait_ge(hot_used, 2 * (s - 1) + half + 1)
                        for kind, out in enumerate((named_word, plain_word)):
                            for j in range(2):
                                last = nc.vector.tensor_scalar(hot[:, half, kind, j], out[:, half * HALF:(half + 1) * HALF],
                                                               c.part_f[:, j:j + 1], None, ALU.is_equal)
                        last.then_inc(hot_ready, 1)

            @block.tensor
            def _(pe):
                for s in range(BATCH):
                    for half in range(2):
                        pe.wait_ge(hot_ready, 2 * s + half + 1)
                        if s:
                            pe.wait_ge(copied, 2 * (s - 1) + half + 1)
                        for j in range(2):
                            nc.tensor.matmul(node_ps[half][:, :], chosen_table[:, j, s], hot[:, half, 0, j], start=(j == 0), stop=False)
                        for j in range(2):
                            last = nc.tensor.matmul(node_ps[half][:, :], plain_table[:, j], hot[:, half, 1, j], start=False, stop=(j == 1))
                        last.then_inc(hot_used, 1)

            @block.scalar
            def _(act):
                for s in range(BATCH):
                    for half in range(2):
                        act.wait_ge(hot_used, 2 * s + half + 1)
                        nc.scalar.copy(node_t[:, s * SEQ + half * HALF:s * SEQ + (half + 1) * HALF], node_ps[half][:, :]).then_inc(copied, 1)


def to_nodes(nc, c, node_t, h, add, meanwhile=None):
    T4 = 4
    with Stage(nc, c) as ctx:
        stage = ctx.sb("stage", [D, 2, T4, P])
        turn_ps = [ctx.ps(f"turn_ps{j}", [P, T4, D]) for j in range(2)]
        staged, turned, read, go = (ctx.sem(n) for n in ("staged", "turned", "read", "go"))
        by_tile = node_t.rearrange("d (p t) -> d t p", t=TILES)
        with nc.Block() as block:
            if meanwhile:

                @block.gpsimd
                def _(pool):
                    meanwhile(pool)

            @block.scalar
            def _(act):
                act.sem_inc(turned, 2)
                with act.Fori(0, TILES // T4 // 2) as i:
                    for half in range(2):
                        act.wait_ge(turned, 2 * i + (half + 1))
                        nc.scalar.copy(stage[:, half], by_tile[:, bass.ds(i * (2 * T4) + half * T4, T4)]).then_inc(staged, 1)

            @block.tensor
            def _(pe):
                with pe.Fori(0, TILES // T4 // 2) as i:
                    for half in range(2):
                        pe.wait_ge(staged, 2 * i + (half + 1))
                        pe.wait_ge(read, 2 * i + (half + 1))
                        pe.sem_inc(go, 1)
                        for k in range(T4):
                            last = nc.tensor.transpose(turn_ps[half][:, k], stage[:, half, k], c.ident[0:D, 0:D])
                        last.then_inc(turned, 1)

            @block.vector
            def _(dve):
                dve.sem_inc(read, 2)
                with dve.Fori(0, TILES // T4 // 2) as i:
                    for half in range(2):
                        dve.wait_ge(turned, 2 * i + (half + 3))
                        rows = h[:, bass.ds(i * (2 * T4) + half * T4, T4)]
                        if add:
                            nc.vector.tensor_tensor(rows, turn_ps[half][:, :, :], rows, ALU.add).then_inc(read, 1)
                        else:
                            nc.vector.tensor_copy(rows, turn_ps[half][:, :, :]).then_inc(read, 1)


EXPERTS = 8
T4 = 4


def norm_project(nc, c, h, x_t, weight, proj, add_back=False, meanwhile=None):
    with Stage(nc, c) as ctx:
        sb = ctx.sb

        n = 0 if proj is None else proj.shape[2]
        centred, square = sb("centred", [P, TILES, D]), sb("square", [P, TILES, D])
        stage, stage_t = sb("stage", [P, 2, T4, D]), sb("stage_t", [D, 2, T4, P])
        w_sb = sb("w_sb", [D, max(n, 1)])
        turn_ps = [ctx.ps(f"turn_ps{j}", [D, T4, P]) for j in range(2)]
        proj_ps = [ctx.ps(f"proj_ps{j}", [P, T4, max(n, 1)]) for j in range(2)]
        loaded, step, staged, turned, added, staged_t, copied, projected, read, go = (
            ctx.sem(s) for s in
            ("loaded", "step", "staged", "turned", "added", "staged_t", "copied", "projected", "read", "go"))
        norm = Norm(nc, ctx, "norm", TILES, D)
        LOOPS = TILES // T4 // 4
        with nc.Block() as block:
            if meanwhile:

                @block.gpsimd
                def _(pool):
                    meanwhile(pool)

            @block.sync
            def _(sp):
                if n:
                    sp.dma_start(w_sb[:, :], weight).then_inc(loaded, 16)

            @block.vector
            def _(dve):
                done = Done(step)
                norm.centre(dve, done, h[:, :, :], centred[:, :, :], square[:, :, :])
                dve.sem_inc(turned, 2)
                dve.sem_inc(added, 2)
                def normalise(i, u):
                    tiles = bass.ds(i * (4 * T4) + u * T4, T4)
                    dve.wait_ge(turned, 4 * i + (u + 1))
                    if add_back:
                        dve.wait_ge(added, 4 * i + (u + 1))
                    nc.vector.tensor_tensor(stage[:, u % 2], centred[:, tiles],
                                            norm.inv[:, tiles].unsqueeze(2).to_broadcast([P, T4, D]), ALU.mult).then_inc(staged, 1)
                    if add_back:
                        dve.wait_ge(staged, 4 * i + (u + 1))
                        nc.vector.tensor_tensor(h[:, tiles], h[:, tiles], stage[:, u % 2], ALU.add).then_inc(added, 1)

                def keep(i, u):
                    dve.wait_ge(projected, 4 * i + (u + 1))
                    nc.vector.tensor_copy(proj[:, bass.ds(i * (4 * T4) + u * T4, T4)], proj_ps[u % 2][:, :, :]).then_inc(read, 1)

                with dve.Fori(0, LOOPS) as i:
                    for u in range(5):
                        if u < 4:
                            normalise(i, u)
                        if n and u > 0:
                            keep(i, u - 1)

            @block.tensor
            def _(pe):
                def turn(i, u):
                    pe.wait_ge(staged, 4 * i + (u + 1))
                    pe.wait_ge(copied, 4 * i + (u + 1))
                    pe.sem_inc(go, 1)
                    for k in range(T4):
                        last = nc.tensor.transpose(turn_ps[u % 2][:, k], stage[:, u % 2, k], c.ident[:, :])
                    last.then_inc(turned, 1)

                def project(i, u):
                    pe.wait_ge(staged_t, 4 * i + (u + 1))
                    pe.wait_ge(read, 4 * i + (u + 1))
                    for k in range(T4):
                        last = nc.tensor.matmul(proj_ps[u % 2][:, k], stage_t[:, u % 2, k], w_sb[:, :], start=True, stop=True)
                    last.then_inc(projected, 1)

                pe.sem_inc(copied, 2)
                pe.sem_inc(read, 2)
                if n:
                    pe.wait_ge(loaded, 16)
                with pe.Fori(0, LOOPS) as i:
                    for u in range(5):
                        if u < 4:
                            turn(i, u)
                        if n and u > 0:
                            project(i, u - 1)

            @block.scalar
            def _(act):
                norm.root(act)
                with act.Fori(0, LOOPS) as i:
                    for u in range(4):
                        act.wait_ge(turned, 4 * i + (u + 3))
                        if n:
                            nc.scalar.copy(stage_t[:, u % 2], turn_ps[u % 2][:, :, :]).then_inc(staged_t, 1)
                        nc.scalar.copy(x_t[:, bass.ds(i * (4 * T4) + u * T4, T4)], turn_ps[u % 2][:, :, :]).then_inc(copied, 1)


def experts(nc, c, x_t, gates, h, w1, b1, w2, b2):
    E = gates.shape[2]
    width = E * D // 4
    with Stage(nc, c) as ctx:
        sb = ctx.sb

        w1_sb, b1_sb = sb("w1_sb", [D, 4, P]), sb("b1_sb", [P, 4])
        w2_sb, b2_sb = sb("w2_sb", [P, 4, width]), sb("b2_sb", [P, E, D])
        hid = sb("hid", [P, 2, 4, T4, P])
        y, mix = sb("y", [P, 4, E, D]), sb("mix", [P, 4, D])
        hid_ps = [ctx.ps(f"hid_ps{j}", [P, T4, P]) for j in range(4)]
        y_ps = [ctx.ps(f"y_ps{j}", [P, E, D]) for j in range(2)]
        loaded, hid_done, hid_read, y_done, y_read, go, scaled, summed, stored = (
            ctx.sem(s) for s in
            ("loaded", "hid_done", "hid_read", "y_done", "y_read", "go", "scaled", "summed", "stored"))
        N = 2 * T4
        LOOPS = TILES // T4 // 2
        with nc.Block() as block:

            @block.sync
            def _(sp):
                load_all(sp, [(w1_sb[:, :, :], w1), (b1_sb[:, :], b1), (w2_sb[:, :, :], w2),
                              (b2_sb[:, :, :], b2.rearrange("(o e) d -> o e d", o=1).to_broadcast([P, E, D]))], loaded)

            @block.tensor
            def _(pe):
                def up(number, first, e):
                    pe.wait_ge(hid_read, number * 4 + (e + 1))
                    pe.sem_inc(go, 1)
                    nc.tensor.matmul(hid_ps[e][:, :, :], w1_sb[:, e], x_t[:, bass.ds(first, T4)], start=True,
                                     stop=True).then_inc(hid_done, 1)

                def two_groups(i, last):
                    for half in range(2):
                        for k in range(T4):
                            if not (last and half == 1):
                                up(2 * i + (half + 1), i * (2 * T4) + (half + 1) * T4, k)
                            if k == 0:
                                pe.wait_ge(hid_read, i * 8 + (half * 4 + 8))
                            pe.wait_ge(y_read, i * (2 * T4) + (half * T4 + k + 1))
                            for e in range(4):
                                end = nc.tensor.matmul(y_ps[k % 2][:, :, :].rearrange("p e d -> p (e d)")[:, e * width:(e + 1) * width],
                                                       hid[:, half, e, k], w2_sb[:, e], start=True, stop=True)
                            end.then_inc(y_done, 1)

                assert T4 == 4
                pe.sem_inc(hid_read, 4)
                pe.sem_inc(y_read, 2)
                pe.wait_ge(loaded, 16 * 4)
                for e in range(4):
                    up(0, 0, e)
                with pe.Fori(0, LOOPS - 1) as i:
                    two_groups(i, False)
                two_groups(LOOPS - 1, True)

            @block.scalar
            def _(act):
                act.wait_ge(loaded, 16 * 4)
                with act.Fori(0, LOOPS) as i:
                    for half in range(2):
                        for e in range(4):
                            act.wait_ge(hid_done, i * 8 + (half * 4 + e + 1))
                            nc.scalar.activation(hid[:, half, e], hid_ps[e][:, :, :], ACT.Gelu, bias=b1_sb[:, e:e + 1]).then_inc(hid_read, 1)

            @block.vector
            def _(dve):
                def add_bias(i, k):
                    dve.wait_ge(y_done, i * N + (k + 1))
                    dve.wait_ge(summed, i * N + (k + 1))
                    nc.vector.tensor_tensor(y[:, k % 4], y_ps[k % 2][:, :, :], b2_sb[:, :, :], ALU.add).then_inc(y_read, 1)

                def add_up(i, k):
                    dve.wait_ge(scaled, i * N + (k + 1))
                    dve.wait_ge(stored, i * N + (k + 1))
                    nc.vector.tensor_reduce(mix[:, k % 4], y[:, k % 4].rearrange("p e d -> p d e"), AX.X, ALU.add).then_inc(summed, 1)

                dve.sem_inc(summed, 4)
                dve.wait_ge(loaded, 16 * 4)
                with dve.Fori(0, LOOPS) as i:
                    for k in range(N + 2):
                        if k < N:
                            add_bias(i, k)
                        if k >= 2:
                            add_up(i, k - 2)

            @block.gpsimd
            def _(pool):
                def scale(i, k):
                    pool.wait_ge(y_read, i * N + (k + 3))
                    nc.gpsimd.tensor_tensor(y[:, k % 4], y[:, k % 4], gates[:, bass.ds(i * N + k, 1)].squeeze(1).unsqueeze(2).to_broadcast([P, E, D]),
                                            ALU.mult).then_inc(scaled, 1)

                def store(i, k):
                    tile = bass.ds(i * N + k, 1)
                    pool.wait_ge(summed, i * N + (k + 5))
                    nc.gpsimd.tensor_tensor(h[:, tile].squeeze(1), h[:, tile].squeeze(1), mix[:, k % 4], ALU.add).then_inc(stored, 1)

                pool.sem_inc(stored, 4)
                with pool.Fori(0, LOOPS) as i:
                    for k in range(N + 2):
                        if k < N:
                            scale(i, k)
                        if k >= 2:
                            store(i, k - 2)


def top_two(nc, dve, done, score, gates, rank, top, exp_in, exp_out, act_ask, act_told, asked):
    E = score.shape[2]
    for e in range(E):
        mine = score[:, :, e:e + 1]
        done.add(nc.vector.memset(rank[:, :, e:e + 1], 0.0))
        if e:
            done.add(nc.vector.tensor_tensor(rank[:, :, 0:e], score[:, :, 0:e], mine.to_broadcast([P, TILES, e]), ALU.is_ge))
        if e < E - 1:
            done.add(nc.vector.tensor_tensor(rank[:, :, e + 1:E], score[:, :, e + 1:E],
                                             mine.to_broadcast([P, TILES, E - 1 - e]), ALU.is_gt))
        done.wait(dve)
        done.add(nc.vector.tensor_reduce(gates[:, :, e:e + 1], rank[:, :, :], AX.X, ALU.add))
        done.wait(dve)
    done.add(nc.vector.tensor_scalar(rank[:, :, :], gates[:, :, :], 2.0, None, ALU.is_lt))
    done.add(nc.vector.tensor_reduce(top[:, :], score[:, :, :], AX.X, ALU.max))
    done.wait(dve)
    nc.vector.tensor_tensor(exp_in[:, :, :], score[:, :, :], top[:, :].unsqueeze(2).to_broadcast([P, TILES, E]),
                            ALU.subtract).then_inc(act_ask, 1)
    dve.wait_ge(act_told, asked)
    done.add(nc.vector.tensor_tensor(gates[:, :, :], exp_out[:, :, :], rank[:, :, :], ALU.mult))
    done.wait(dve)
    done.add(nc.vector.tensor_reduce(top[:, :], gates[:, :, :], AX.X, ALU.add))
    done.wait(dve)
    done.add(nc.vector.reciprocal(top[:, :], top[:, :]))
    done.wait(dve)
    done.add(nc.vector.tensor_tensor(gates[:, :, :], gates[:, :, :], top[:, :].unsqueeze(2).to_broadcast([P, TILES, E]), ALU.mult))
    done.wait(dve)


GH, GE = 4, 4
GF = GH * GE
ROW = GF + GH
OUT = ROW + GH
LOW = 1e30
ROUND = 1.5 * 2 ** 23
SC = 33


def send_nodes(nc, c, w, proj, start_i, source_rows, start_rows, sender):
    with Stage(nc, c) as ctx:
        sb = ctx.sb

        att = sb("att", [P, 2, GF])
        rows, heads, tmp = sb("rows", [P, TILES, ROW]), sb("heads", [P, TILES, 1 + GH]), sb("tmp", [P, 2, TILES, GF])
        name = sb("name", [P, TILES], I32)
        loaded, step, ready, sent_rows, named = (ctx.sem(s) for s in ("loaded", "step", "ready", "sent_rows", "named"))
        sent = ctx.pool_sem("sent")
        with nc.Block() as block:

            @block.sync
            def _(sp):
                load_all(sp, [(att[:, 0], on_every_partition(w["att_src"], GF)), (att[:, 1], on_every_partition(w["att_dst"], GF))], loaded)
                sp.wait_ge(ready, 1)
                sp.dma_start(source_rows.rearrange("(p t) f -> p t f", p=P), rows[:, :, :]).then_inc(sent_rows, 16)
                sp.wait_ge(sent_rows, 16)

            @block.vector
            def _(dve):
                done = Done(step)
                dve.wait_ge(loaded, 32)
                for k in range(2):
                    done.add(nc.vector.tensor_tensor(tmp[:, k], proj[:, :, :], att[:, k].unsqueeze(1).to_broadcast([P, TILES, GF]), ALU.mult))
                nc.vector.tensor_copy(rows[:, :, 0:GF], proj[:, :, :])
                dve.wait_ge(named, 1)
                nc.vector.tensor_copy(heads[:, :, 0:1], name[:, :].unsqueeze(2))
                done.wait(dve)
                nc.vector.tensor_reduce(rows[:, :, GF:ROW], tmp[:, 0].rearrange("p t (h e) -> p t h e", h=GH), AX.X, ALU.add).then_inc(ready, 1)
                nc.vector.tensor_reduce(heads[:, :, 1:1 + GH], tmp[:, 1].rearrange("p t (h e) -> p t h e", h=GH), AX.X, ALU.add).then_inc(ready, 1)

            @block.gpsimd
            def _(pool):
                nc.gpsimd.iota(name[:, :], [[1, TILES]], base=1, channel_multiplier=TILES).then_inc(named, 1)
                sender.send(pool, 2)
                pool.wait_ge(ready, 2)
                for t in range(TILES):
                    nc.gpsimd.indirect_dma_start(start_rows, bass.IndirectOffsetOnAxis(ap=start_i[:, t:t + 1], axis=0),
                                                 heads[:, t], None, bounds_check=SLOTS - 1, oob_is_err=False).then_inc(sent, 16)
                sender.stage_last(pool)
                pool.wait_ge(sent, 16 * TILES)


def spread_heads(nc, c, sender, sorted_src, start_rows, ids, scratch, not_first, minus_low, dst_term, has_none):
    with Stage(nc, c) as ctx:
        sb = ctx.sb

        rows = scratch[:, 0:SCOLS * (1 + GH)].rearrange("p (c f) -> p c f", f=1 + GH)
        own = scratch[:, SCOLS * (1 + GH):SCOLS * (2 + GH)].bitcast(I32)
        pair = sb("pair", [P, 2, GH])
        lines, carry = sb("lines", [GH, 2, P]), sb("carry", [GH, P + 1])
        begin = sb("begin", [P, GH])
        turn_ps = ctx.ps("turn_ps", [GH, 2, P])
        back_ps = ctx.ps("back_ps", [P, GH])
        loaded, step, pair_ready, turned, carried, back, list_whole, ids_loaded = (
            ctx.sem(s) for s in ("loaded", "step", "pair_ready", "turned", "carried", "back", "list_whole", "ids_loaded"))
        with nc.Block() as block:

            @block.sync
            def _(sp):
                sp.dma_start(rows[:, :, :], start_rows.rearrange("(p c) f -> p c f", p=P)).then_inc(loaded, 16)
                sp.wait_ge(list_whole, 1)
                sp.dma_start(ids, sorted_src.rearrange("(p c) o -> p (c o)", p=P)).then_inc(ids_loaded, 16)

            @block.gpsimd
            def _(pool):
                sender.scatter_last(pool)
                sender.wait_all(pool)
                pool.sem_inc(list_whole, 1)

            @block.vector
            def _(dve):
                def spread(initial):
                    for k in range(GH):
                        last = nc.vector.tensor_tensor_scan(dst_term[:, k], not_first[:, :], rows[:, :, 1 + k],
                                                            initial(k), ALU.mult, ALU.add)
                        done.add(last)

                done = Done(step)
                dve.wait_ge(loaded, 16)
                nc.vector.tensor_scalar(minus_low[:, :], rows[:, :, 0], 1.0, -LOW, ALU.is_ge, ALU.mult)
                done.add(nc.vector.tensor_scalar(own, rows[:, :, 0], -1.0, 0.0, ALU.add, ALU.max))
                done.add(nc.vector.tensor_reduce(has_none[:, :], rows[:, :, 0], AX.X, ALU.max))
                done.add(nc.vector.tensor_scalar(not_first[:, :], rows[:, :, 0], 1.0, None, ALU.is_lt))
                done.wait(dve)
                done.add(nc.vector.tensor_scalar(has_none[:, :], has_none[:, :], 1.0, None, ALU.is_lt))
                spread(lambda k: 0.0)
                done.wait(dve)
                nc.vector.tensor_copy(pair[:, 0], dst_term[:, :, SCOLS - 1])
                nc.vector.tensor_copy(pair[:, 1], has_none[:, :].to_broadcast([P, GH])).then_inc(pair_ready, 1)
                dve.wait_ge(turned, 1)
                done.add(nc.vector.tensor_copy(lines[:, :, :], turn_ps[:, :, :]))
                done.add(nc.vector.memset(carry[:, 0:1], 0.0))
                done.wait(dve)
                nc.vector.tensor_tensor_scan(carry[:, 1:P + 1], lines[:, 1], lines[:, 0], 0.0, ALU.mult, ALU.add).then_inc(carried, 1)
                dve.wait_ge(back, 1)
                done.add(nc.vector.tensor_copy(begin[:, :], back_ps[:, :]))
                done.wait(dve)
                spread(lambda k: begin[:, k:k + 1])
                dve.wait_ge(ids_loaded, 16)
                nc.vector.tensor_tensor(ids, ids, own, ALU.add)

            @block.tensor
            def _(pe):
                pe.wait_ge(pair_ready, 1)
                for k in range(2):
                    last = nc.tensor.transpose(turn_ps[:, k], pair[:, k], c.ident[:, :])
                last.then_inc(turned, 1)
                pe.wait_ge(carried, 1)
                nc.tensor.transpose(back_ps[:, :], carry[:, 0:P], c.ident[0:GH, 0:GH]).then_inc(back, 1)


def aggregate(nc, c, w, ids, source_rows, not_first, minus_low, dst_term, slot_rows, last_rows, x_t, y):
    with Stage(nc, c) as ctx:
        sb = ctx.sb

        id_stage = sb("id_stage", [P, 2, SC], I32)
        got = sb("got", [P, 2, SC, ROW])
        score = sb("score", [P, GH, SC])
        peak = sb("peak", [P, 2, GH, SC + 1])
        ex, weight = sb("ex", [P, 2, GH, SC]), sb("weight", [P, 2, GH, SC])
        message = sb("message", [P, GH, GE, SC])
        rows = sb("rows", [P, 2, SC, OUT])
        staged, sent, step, ask, told, pool_go, rows_ready = (
            ctx.sem(s) for s in
            ("staged", "sent", "step", "ask", "told", "pool_go", "rows_ready"))
        got_in = [ctx.pool_sem(f"got_in{j}") for j in range(2)]
        stored = [ctx.sem(f"stored{j}") for j in range(2)]
        w1_sb, b1_sb = sb("w1_sb", [D, GE, P]), sb("b1_sb", [P, GE])
        w2_sb, b2_sb = sb("w2_sb", [P, GE, D]), sb("b2_sb", [P, GE, D])
        hid = sb("hid", [P, GE, P])
        hid_ps, y_ps = ctx.ps("hid_ps", [P, GE, P]), ctx.ps("y_ps", [P, GE, D])
        weights_loaded, hid_done, hid_read, y_done, y_read, pe_go = (
            ctx.sem(s) for s in ("weights_loaded", "hid_done", "hid_read", "y_done", "y_read", "pe_go"))
        assert SCOLS // SC == TILES
        LOOPS = SCOLS // SC // 2
        STEPS = 33
        with nc.Block() as block:

            @block.sync
            def _(sp):
                load_all(sp, [(w1_sb[:, :, :], w["ffn_w1"]), (b1_sb[:, :], w["ffn_b1"]), (w2_sb[:, :, :], w["ffn_w2"]),
                              (b2_sb[:, :, :], w["ffn_b2"].rearrange("(o e) d -> o e d", o=1).to_broadcast([P, GE, D]))],
                         weights_loaded)
                sp.wait_ge(step, 2)
                for half in range(2):
                    sp.dma_start(slot_rows.rearrange("(p c) f -> p c f", p=P)[:, half * SC:(half + 1) * SC],
                                 rows[:, half]).then_inc(stored[half], 16)
                with sp.Fori(0, LOOPS) as i:
                    for half in range(2):
                        sp.wait_ge(rows_ready, 2 * i + (half + 1))
                        sp.wait_ge(stored[half], i * 16 + 16)
                        sp.dma_start(slot_rows.rearrange("(p c) f -> p c f", p=P)[:, bass.ds(i * (2 * SC) + half * SC, SC)],
                                     rows[:, half]).then_inc(stored[half], 16)
                for half in range(2):
                    sp.wait_ge(stored[half], 16 * (LOOPS + 1))

            @block.gpsimd
            def _(pool):
                with pool.Fori(0, LOOPS) as i:
                    for half in range(2):
                        pool.wait_ge(staged, 2 * i + (half + 1))
                        pool.sem_inc(pool_go, 1)
                        for k in range(SC):
                            nc.gpsimd.indirect_dma_start(got[:, half, k], None, source_rows,
                                                         bass.IndirectOffsetOnAxis(ap=id_stage[:, half, k:k + 1], axis=0)).then_inc(got_in[half], 16)

            @block.scalar
            def _(act):
                with act.Fori(0, LOOPS) as i:
                    for half in range(2):
                        act.wait_ge(ask, 2 * i + (half + 1))
                        nc.scalar.activation(weight[:, :, :, :], ex[:, :, :, :], ACT.Exp).then_inc(told, 1)
                        act.wait_ge(hid_done, 2 * i + (half + 1))
                        if half == 0:
                            act.wait_ge(weights_loaded, 16 * 4)
                        for e in range(GE):
                            nc.scalar.activation(hid[:, e], hid_ps[:, e], ACT.Gelu, bias=b1_sb[:, e:e + 1]).then_inc(hid_read, 1)

            @block.tensor
            def _(pe):
                pe.sem_inc(y_read, 1)
                pe.wait_ge(weights_loaded, 16 * 4)
                with pe.Fori(0, LOOPS) as i:
                    for half in range(2):
                        tile = bass.ds(i * 2 + half, 1)
                        for e in range(GE):
                            last = nc.tensor.matmul(hid_ps[:, e], w1_sb[:, e], x_t[:, tile].squeeze(1), start=True, stop=True)
                        last.then_inc(hid_done, 1)
                        pe.wait_ge(hid_read, i * (2 * GE) + (half + 1) * GE)
                        pe.wait_ge(y_read, 2 * i + (half + 1))
                        pe.sem_inc(pe_go, 1)
                        for e in range(GE):
                            last = nc.tensor.matmul(y_ps[:, e], hid[:, e], w2_sb[:, e], start=True, stop=True)
                        last.then_inc(y_done, 1)

            @block.vector
            def _(dve):
                start = Done(step)
                start.add(nc.vector.memset(peak[:, 1], -LOW))
                start.add(nc.vector.memset(rows[:, :, :, :], 0.0))
                nc.vector.memset(ids[:, SCOLS:SCOLS + 2 * SC], 0)
                nc.vector.tensor_copy(id_stage[:, 0], ids[:, 0:SC]).then_inc(staged, 1)
                nc.vector.tensor_copy(id_stage[:, 1], ids[:, SC:2 * SC]).then_inc(staged, 1)
                start.wait(dve)
                dve.wait_ge(weights_loaded, 16 * 4)
                with dve.Fori(0, LOOPS) as i:
                    for half in range(2):
                        done = Done(step, i * (2 * STEPS) + (half * STEPS + 2))
                        cols = bass.ds(i * (2 * SC) + half * SC, SC)
                        g = got[:, half]
                        dve.wait_ge(got_in[half], i * (16 * SC) + 16 * SC)
                        done.add(nc.vector.tensor_copy(peak[:, half, :, 0:1], peak[:, 1 - half, :, SC:SC + 1]))
                        done.add(nc.vector.tensor_tensor(score[:, :, :], g[:, :, GF:ROW].rearrange("p c h -> p h c"),
                                                         dst_term[:, :, cols], ALU.add))
                        done.wait(dve)
                        done.add(nc.vector.scalar_tensor_tensor(score[:, :, :], score[:, :, :], 0.2, score[:, :, :], ALU.mult, ALU.max))
                        done.wait(dve)
                        for k in range(GH):
                            done.add(nc.vector.tensor_tensor_scan(peak[:, half, k, 1:SC + 1], minus_low[:, cols], score[:, k],
                                                                  peak[:, half, k, 0:1], ALU.add, ALU.max))
                        done.wait(dve)
                        done.add(nc.vector.tensor_tensor(ex[:, 1], peak[:, half, :, 0:SC], peak[:, half, :, 1:SC + 1], ALU.subtract))
                        done.add(nc.vector.tensor_tensor(ex[:, 0], score[:, :, :], peak[:, half, :, 1:SC + 1], ALU.subtract))
                        done.wait(dve)
                        nc.vector.tensor_scalar(ex[:, 1], ex[:, 1], 0.0, None, ALU.min).then_inc(ask, 1)
                        dve.wait_ge(told, 2 * i + (half + 1))
                        done.add(nc.vector.tensor_tensor(weight[:, 1], weight[:, 1], not_first[:, cols].unsqueeze(1).to_broadcast([P, GH, SC]), ALU.mult))
                        done.add(nc.vector.tensor_tensor(message[:, :, :, :], g[:, :, 0:GF].rearrange("p c (h e) -> p h e c", h=GH),
                                                         weight[:, 0].unsqueeze(2).to_broadcast([P, GH, GE, SC]), ALU.mult))
                        dve.wait_ge(stored[half], i * 16 + 16)
                        done.wait(dve)
                        for f in range(ROW):
                            k = f // GE if f < GF else f - GF
                            new = message[:, k, f % GE] if f < GF else weight[:, 0, k]
                            done.add(nc.vector.tensor_tensor_scan(rows[:, half, :, f], weight[:, 1, k], new,
                                                                  rows[:, 1 - half, SC - 1, f:f + 1], ALU.mult, ALU.add))
                        done.add(nc.vector.tensor_copy(rows[:, half, :, ROW:OUT].rearrange("p c h -> p h c"), peak[:, half, :, 1:SC + 1]))
                        done.add(nc.vector.tensor_copy(id_stage[:, half], ids[:, bass.ds(i * (2 * SC) + (half + 2) * SC, SC)]))
                        assert done.n == STEPS, done.n
                        done.wait(dve)
                        dve.sem_inc(staged, 1)
                        dve.sem_inc(rows_ready, 1)
                        dve.wait_ge(y_done, 2 * i + (half + 1))
                        nc.vector.tensor_tensor(y[:, bass.ds(i * 2 + half, 1)].squeeze(1), y_ps[:, :, :], b2_sb[:, :, :],
                                                ALU.add).then_inc(y_read, 1)
                nc.vector.tensor_copy(last_rows[:, :], rows[:, 1, SC - 1])


def finish_graph(nc, c, w, end_i, start_i, slot_rows, last_rows, has_none, gates):
    with Stage(nc, c) as ctx:
        sb = ctx.sb
        sem = ctx.sem

        N8 = 8
        part = sb("part", [P, 3, ROW])
        line = sb("line", [ROW, 3, P])
        open_max, open_sum = sb("open_max", [ROW, P + 1]), sb("open_sum", [ROW, P])
        low = sb("low", [ROW, P])
        fac = sb("fac", [ROW, 2, P])
        back = sb("back", [P, 2, ROW])
        one_hot, one_hot_t = sb("one_hot", [P, 2, N8, P], BF16), sb("one_hot_t", [P, 2, N8, P])
        hot_ps = [ctx.ps(f"hot_ps{j}", [P, N8, P], BF16) for j in range(2)]
        found_ps = [ctx.ps(f"found_ps{j}", [P, N8, 2 * ROW]) for j in range(2)]
        part_ps = ctx.ps("part_ps", [ROW, 3, P])
        back_ps = ctx.ps("back_ps", [P, 2, ROW])
        first_part, last_part = sb("first_part", [P, TILES]), sb("last_part", [P, TILES])
        carry, empty = sb("carry", [P, TILES], BF16), sb("empty", [P, TILES])
        mine, before = sb("mine", [P, TILES, OUT]), sb("before", [P, TILES, 2 * ROW])
        peak = sb("peak", [P, TILES, GH])
        ex, factor = sb("ex", [P, 2, TILES, GH]), sb("factor", [P, 2, TILES, GH])
        inv = sb("inv", [P, TILES, GH])
        agg, centred, square = sb("agg", [P, TILES, GF]), sb("centred", [P, TILES, GF]), sb("square", [P, TILES, GF])
        gain = sb("gain", [P, 3, GF])
        score, rank, top, sx = sb("score", [P, TILES, GE]), sb("rank", [P, TILES, GE]), sb("top", [P, TILES]), sb("sx", [P, 2, TILES, GE])
        loaded, step, part_ready, turned, lines_ready, ask, told, turned_back, back_ready = map(
            sem, ("loaded", "step", "part_ready", "turned", "lines_ready", "ask", "told", "turned_back", "back_ready"))
        hot_ready, hot_turned, hot_free, hot_t_ready, found, found_read, go = map(
            sem, ("hot_ready", "hot_turned", "hot_free", "hot_t_ready", "found", "found_read", "go"))
        mine_in = ctx.pool_sem("mine_in")
        norm = Norm(nc, ctx, "norm", TILES, GF)

        with nc.Block() as block:

            @block.sync
            def _(sp):
                load_all(sp, [(gain[:, 0], on_every_partition(w["gat_b"], GF)), (gain[:, 1], on_every_partition(w["ln_gamma"], GF)),
                              (gain[:, 2], on_every_partition(w["ln_beta"], GF))], loaded)

            @block.gpsimd
            def _(pool):
                for t in range(TILES):
                    nc.gpsimd.indirect_dma_start(mine[:, t], None, slot_rows,
                                                 bass.IndirectOffsetOnAxis(ap=end_i[:, t:t + 1], axis=0)).then_inc(mine_in, 16)

            @block.tensor
            def _(pe):
                pe.wait_ge(part_ready, 1)
                for k in range(3):
                    last = nc.tensor.transpose(part_ps[:, k], part[:, k], c.ident[:, :])
                last.then_inc(turned, 1)
                pe.wait_ge(lines_ready, 1)
                nc.tensor.transpose(back_ps[:, 0], open_max[:, 1:P + 1], c.ident[0:ROW, 0:ROW])
                nc.tensor.transpose(back_ps[:, 1], open_sum[:, :], c.ident[0:ROW, 0:ROW]).then_inc(turned_back, 1)
                pe.wait_ge(back_ready, 1)
                pe.sem_inc(hot_free, 2)
                with pe.Fori(0, TILES // N8 // 2) as i:
                    for half in range(2):
                        pe.wait_ge(hot_ready, 2 * i + (half + 1))
                        for k in range(N8):
                            last = nc.tensor.transpose(hot_ps[half][:, k], one_hot[:, half, k], c.ident_b[:, :])
                        last.then_inc(hot_turned, 1)
                        pe.wait_ge(hot_t_ready, 2 * i + (half + 1))
                        pe.sem_inc(hot_free, 1)
                        pe.wait_ge(found_read, 2 * i + (half + 1))
                        pe.sem_inc(go, 1)
                        for k in range(N8):
                            last = nc.tensor.matmul(found_ps[half][:, k], one_hot_t[:, half, k],
                                                    back[:, :, :].rearrange("p a f -> p (a f)"), start=True, stop=True)
                        last.then_inc(found, 1)

            @block.scalar
            def _(act):
                act.wait_ge(ask, 1)
                nc.scalar.activation(fac[:, :, :], fac[:, :, :], ACT.Exp).then_inc(told, 1)
                act.sem_inc(found_read, 2)
                with act.Fori(0, TILES // N8 // 2) as i:
                    for half in range(2):
                        act.wait_ge(hot_turned, 2 * i + (half + 1))
                        nc.scalar.copy(one_hot_t[:, half], hot_ps[half][:, :, :]).then_inc(hot_t_ready, 1)
                        act.wait_ge(found, 2 * i + (half + 1))
                        nc.scalar.copy(before[:, bass.ds(i * (2 * N8) + half * N8, N8)], found_ps[half][:, :, :]).then_inc(found_read, 1)
                act.wait_ge(ask, 2)
                nc.scalar.activation(factor[:, :, :, :], ex[:, :, :, :], ACT.Exp).then_inc(told, 1)
                norm.root(act)
                act.wait_ge(ask, 3)
                nc.scalar.activation(sx[:, 1], sx[:, 0], ACT.Exp).then_inc(told, 1)

            @block.vector
            def _(dve):
                v = nc.vector
                done = Done(step)
                done.add(v.tensor_copy(part[:, 0, 0:GF].rearrange("p (h e) -> p h e", h=GH),
                                       last_rows[:, ROW:OUT].unsqueeze(2).to_broadcast([P, GH, GE])))
                v.tensor_copy(part[:, 0, GF:ROW], last_rows[:, ROW:OUT])
                v.tensor_copy(part[:, 1], last_rows[:, 0:ROW])
                v.tensor_copy(part[:, 2], has_none[:, :].to_broadcast([P, ROW])).then_inc(part_ready, 1)
                dve.wait_ge(turned, 1)
                done.add(v.tensor_copy(line[:, :, :], part_ps[:, :, :]))
                done.add(v.memset(open_max[:, 0:1], -LOW))
                done.wait(dve)
                done.add(v.tensor_scalar(low[:, :], line[:, 2], -1.0, LOW, ALU.add, ALU.mult))
                done.wait(dve)
                done.add(v.tensor_tensor_scan(open_max[:, 1:P + 1], low[:, :], line[:, 0], -LOW, ALU.add, ALU.max))
                done.wait(dve)
                done.add(v.tensor_tensor(fac[:, 0], open_max[:, 0:P], open_max[:, 1:P + 1], ALU.subtract))
                done.add(v.tensor_tensor(fac[:, 1], line[:, 0], open_max[:, 1:P + 1], ALU.subtract))
                done.wait(dve)
                v.tensor_scalar(fac[:, 0], fac[:, 0], 0.0, None, ALU.min).then_inc(ask, 1)
                dve.wait_ge(told, 1)
                done.add(v.tensor_tensor(fac[:, 0], fac[:, 0], line[:, 2], ALU.mult))
                done.add(v.tensor_tensor(fac[:, 1], fac[:, 1], line[:, 1], ALU.mult))
                done.wait(dve)
                v.tensor_tensor_scan(open_sum[:, :], fac[:, 0], fac[:, 1], 0.0, ALU.mult, ALU.add).then_inc(lines_ready, 1)
                dve.wait_ge(turned_back, 1)
                v.tensor_copy(back[:, :, :], back_ps[:, :, :]).then_inc(back_ready, 1)
                for out, slots in ((first_part, start_i), (last_part, end_i)):
                    done.add(v.tensor_scalar(out[:, :], slots[:, :], 1.0 / SCOLS, 0.5 / SCOLS - 0.5, ALU.mult, ALU.add))
                done.wait(dve)
                for out in (first_part, last_part):
                    done.add(v.tensor_scalar_add(out[:, :], out[:, :], ROUND))
                done.wait(dve)
                for out in (first_part, last_part):
                    done.add(v.tensor_scalar_add(out[:, :], out[:, :], -ROUND))
                done.wait(dve)
                done.add(v.tensor_tensor(first_part[:, :], first_part[:, :], last_part[:, :], ALU.is_lt))
                done.wait(dve)
                done.add(v.scalar_tensor_tensor(last_part[:, :], last_part[:, :], -float(P + 1), first_part[:, :], ALU.add, ALU.mult))
                done.wait(dve)
                done.add(v.tensor_scalar_add(carry[:, :], last_part[:, :], float(P)))
                done.wait(dve)
                done.add(v.tensor_scalar(empty[:, :], carry[:, :], float(P), -LOW, ALU.is_ge, ALU.mult))
                with dve.Fori(0, TILES // N8 // 2) as i:
                    for half in range(2):
                        dve.wait_ge(hot_free, 2 * i + (half + 1))
                        v.tensor_tensor(one_hot[:, half], carry[:, bass.ds(i * (2 * N8) + half * N8, N8)].unsqueeze(2).to_broadcast([P, N8, P]),
                                        c.iota_b[:, :].unsqueeze(1).to_broadcast([P, N8, P]), ALU.is_equal).then_inc(hot_ready, 1)
                dve.wait_ge(mine_in, 16 * TILES)
                dve.wait_ge(found_read, TILES // N8 + 2)
                done.add(v.tensor_tensor(before[:, :, GF:ROW], before[:, :, GF:ROW], empty[:, :].unsqueeze(2).to_broadcast([P, TILES, ROW - GF]), ALU.add))
                done.wait(dve)
                done.add(v.tensor_tensor(peak[:, :, :], mine[:, :, ROW:OUT], before[:, :, GF:ROW], ALU.max))
                done.wait(dve)
                done.add(v.tensor_tensor(ex[:, 0], mine[:, :, ROW:OUT], peak[:, :, :], ALU.subtract))
                v.tensor_tensor(ex[:, 1], before[:, :, GF:ROW], peak[:, :, :], ALU.subtract).then_inc(ask, 1)
                dve.wait_ge(told, 2)

                def by_head(x):
                    return x.rearrange("p t (h e) -> p t h e", h=GH)

                def wide(x):
                    return x.unsqueeze(3).to_broadcast([P, TILES, GH, GE])

                done.add(v.tensor_tensor(by_head(agg[:, :, :]), by_head(mine[:, :, 0:GF]), wide(factor[:, 0]), ALU.mult))
                done.add(v.tensor_tensor(by_head(centred[:, :, :]), by_head(before[:, :, ROW:ROW + GF]), wide(factor[:, 1]), ALU.mult))
                done.add(v.tensor_tensor(inv[:, :, :], mine[:, :, GF:ROW], factor[:, 0], ALU.mult))
                done.add(v.tensor_tensor(peak[:, :, :], before[:, :, ROW + GF:2 * ROW], factor[:, 1], ALU.mult))
                done.wait(dve)
                done.add(v.tensor_tensor(agg[:, :, :], agg[:, :, :], centred[:, :, :], ALU.add))
                done.add(v.scalar_tensor_tensor(inv[:, :, :], inv[:, :, :], 1e-16, peak[:, :, :], ALU.add, ALU.add))
                done.wait(dve)
                done.add(v.reciprocal(inv[:, :, :], inv[:, :, :]))
                done.wait(dve)
                done.add(v.tensor_tensor(by_head(agg[:, :, :]), by_head(agg[:, :, :]), wide(inv[:, :, :]), ALU.mult))
                dve.wait_ge(loaded, 48)
                done.wait(dve)

                def row(k):
                    return gain[:, k].unsqueeze(1).to_broadcast([P, TILES, GF])

                done.add(v.tensor_tensor(agg[:, :, :], agg[:, :, :], row(0), ALU.add))
                done.wait(dve)
                norm.centre(dve, done, agg[:, :, :], centred[:, :, :], square[:, :, :])
                done.add(v.tensor_tensor(centred[:, :, :], centred[:, :, :], norm.wide(norm.inv), ALU.mult))
                done.wait(dve)
                for k, op in ((1, ALU.mult), (2, ALU.add)):
                    done.add(v.tensor_tensor(centred[:, :, :], centred[:, :, :], row(k), op))
                    done.wait(dve)
                done.add(v.tensor_reduce(score[:, :, :], centred[:, :, :].rearrange("p t (h e) -> p t e h", h=GH), AX.X, ALU.add))
                done.wait(dve)
                done.add(v.tensor_scalar_mul(score[:, :, :], score[:, :, :], 1.0 / GH))
                done.wait(dve)
                top_two(nc, dve, done, score, gates, rank, top, sx[:, 0], sx[:, 1], ask, told, 3)


def mix_experts(nc, c, y, gates, h):
    with Stage(nc, c) as ctx:
        mixed = ctx.sb("mixed", [P, TILES, D])
        scaled, scaled_too, summed = ctx.sem("scaled"), ctx.sem("scaled_too"), ctx.sem("summed")
        gate = gates[:, :, :].unsqueeze(3).to_broadcast([P, TILES, GE, D])
        FIRST, SECOND = slice(0, TILES // 2), slice(TILES // 2, TILES)

        def scale(engine, tiles):
            return engine.tensor_tensor(y[:, tiles], y[:, tiles], gate[:, tiles], ALU.mult)

        with nc.Block() as block:

            @block.vector
            def _(dve):
                def add_up(tiles):
                    nc.vector.tensor_reduce(mixed[:, tiles], y[:, tiles].rearrange("p t e d -> p t d e"), AX.X, ALU.add).then_inc(summed, 1)

                scale(nc.vector, FIRST).then_inc(scaled, 1)
                dve.wait_ge(scaled, 1)
                add_up(FIRST)
                dve.wait_ge(scaled_too, 1)
                add_up(SECOND)
                dve.wait_ge(summed, 2)
                nc.vector.tensor_tensor(h[:, SECOND], h[:, SECOND], mixed[:, SECOND], ALU.add)

            @block.gpsimd
            def _(pool):
                scale(nc.gpsimd, SECOND).then_inc(scaled_too, 1)
                pool.wait_ge(summed, 1)
                nc.gpsimd.tensor_tensor(h[:, FIRST], h[:, FIRST], mixed[:, FIRST], ALU.add)


def route(nc, c, logits, gates):
    E = logits.shape[2]
    with Stage(nc, c) as ctx:
        sb = ctx.sb

        rank, top, sx = sb("rank", [P, TILES, E]), sb("top", [P, TILES]), sb("sx", [P, 2, TILES, E])
        step, ask, told = (ctx.sem(s) for s in ("step", "ask", "told"))
        with nc.Block() as block:

            @block.vector
            def _(dve):
                top_two(nc, dve, Done(step), logits, gates, rank, top, sx[:, 0], sx[:, 1], ask, told, 1)

            @block.scalar
            def _(act):
                act.wait_ge(ask, 1)
                nc.scalar.activation(sx[:, 1], sx[:, 0], ACT.Exp).then_inc(told, 1)


def project_columns(nc, c, w, x_t, q, k, v):
    KT = SEQ // P
    WIDE = SEQ // TILES
    with Stage(nc, c) as ctx:
        wqkv, x = ctx.sb("wqkv", [D, 3, D]), ctx.sb("x", [D, 2, SEQ])
        in_ps = [ctx.ps(f"in_ps{j}", [P, 512]) for j in range(5)]
        loaded, x_ready, in_done, in_read, go = map(ctx.sem, ("loaded", "x_ready", "in_done", "in_read", "go"))
        with nc.Block() as block:

            @block.sync
            def _(sp):
                load_all(sp, [(wqkv[:, j], w[n]) for j, n in enumerate(("l1_wq_t", "l1_wk_t", "l1_wv_t"))], loaded)

            @block.scalar
            def _(act):
                with act.Fori(0, BATCH // 2) as i:
                    for half in range(2):
                        act.wait_ge(in_read, i * 10 + (half * 5 + 1))
                        nc.scalar.copy(x[:, half].rearrange("d (p t) -> d t p", t=TILES),
                                       x_t[:, :, bass.ds(i * (2 * WIDE) + half * WIDE, WIDE)]).then_inc(x_ready, 1)

            @block.tensor
            def _(pe):
                pe.sem_inc(in_read, 6)
                pe.wait_ge(loaded, 48)
                with pe.Fori(0, BATCH // 2) as i:
                    for half in range(2):
                        pe.wait_ge(x_ready, 2 * i + (half + 1))
                        for j in range(4):
                            pe.wait_ge(in_read, i * 10 + (half * 5 + j + 2))
                            pe.sem_inc(go, 1)
                            nc.tensor.matmul(in_ps[j][0:D, :], wqkv[:, j // 2], x[:, half, j % 2 * 512:(j % 2 + 1) * 512],
                                             start=True, stop=True).then_inc(in_done, 1)
                        pe.wait_ge(in_read, i * 10 + (half * 5 + 6))
                        pe.sem_inc(go, 1)
                        for m in range(KT):
                            last = nc.tensor.matmul(in_ps[4][:, m * D:(m + 1) * D], x[:, half, m * P:(m + 1) * P], wqkv[:, 2],
                                                    start=True, stop=True)
                        last.then_inc(in_done, 1)

            @block.vector
            def _(dve):
                with dve.Fori(0, BATCH // 2) as i:
                    for half in range(2):
                        for j in range(4):
                            dve.wait_ge(in_done, i * 10 + (half * 5 + j + 1))
                            nc.vector.tensor_copy((q, k)[j // 2][:, bass.ds(i * (2 * SEQ) + (half * SEQ + j % 2 * 512), 512)],
                                                  in_ps[j][0:D, :]).then_inc(in_read, 1)
                        dve.wait_ge(in_done, i * 10 + (half * 5 + 5))
                        nc.vector.tensor_copy(v[:, bass.ds(i * 2 + half, 1)].squeeze(1),
                                              in_ps[4][:, :].rearrange("p (m d) -> p m d", m=KT)).then_inc(in_read, 1)


def column_attention(nc, c, q, k, v, out_t):
    KT = SEQ // P
    MASK = -1e10
    with Stage(nc, c) as ctx:
        sb = ctx.sb
        sem = ctx.sem

        key = sb("key", [D, KT, P])
        value = sb("value", [P, KT, D])
        mask = sb("mask", [P, SEQ])
        e = sb("e", [P, KT, SEQ])
        peak, total = sb("peak", [P, KT]), sb("total", [P, KT])
        s_ps = [ctx.ps(f"s_ps{j}", [P, SEQ]) for j in range(3)]
        o_ps = ctx.ps("o_ps", [D, 2, 512])
        masked, key_ready, s_done, v_ready, step, peak_ready, exp_done, o_done, o_read, go = map(
            sem, ("masked", "key_ready", "s_done", "v_ready", "step", "peak_ready", "exp_done", "o_done", "o_read", "go"))
        divided = sem("divided")

        def width(m):
            return SEQ if m == 0 else (m + 1) * P

        with nc.Block() as block:

            @block.gpsimd
            def _(pool):
                nc.gpsimd.tensor_copy(key[:, :, :], k[:, 0:SEQ].rearrange("d (m n) -> d m n", m=KT)).then_inc(key_ready, KT)
                nc.gpsimd.memset(mask[:, :], MASK).then_inc(masked, 1)
                pool.wait_ge(masked, 1)
                nc.gpsimd.affine_select(out=mask[:, :], in_=mask[:, :], compare_op=ALU.is_ge, fill=0.0, base=0,
                                        pattern=[[1, SEQ]], channel_multiplier=-1).then_inc(masked, 1)
                with pool.Fori(0, BATCH - 1) as s:
                    for m in range(KT):
                        pool.wait_ge(s_done, s * KT + (m + 1))
                        pool.sem_inc(go, 1)
                        nc.gpsimd.tensor_copy(key[:, m], k[:, bass.ds(s * SEQ + (SEQ + m * P), P)]).then_inc(key_ready, 1)

            @block.scalar
            def _(act):
                def exponentials(s, m):
                    act.wait_ge(peak_ready, s * KT + (m + 1))
                    nc.scalar.activation(e[:, m, 0:width(m)], s_ps[m % 3][:, 0:width(m)], ACT.Exp, scale=D ** -0.5,
                                         bias=peak[:, m:m + 1], accum_out=total[:, m:m + 1]).then_inc(exp_done, 1)

                def sentence(s, last):
                    for m in range(1, KT):
                        exponentials(s, m)
                    if not last:
                        exponentials(s + 1, 0)
                    act.wait_ge(o_done, s + 1)
                    nc.scalar.copy(out_t[:, bass.ds(s * SEQ, SEQ)].rearrange("d (a n) -> d a n", a=2), o_ps[:, :, :]).then_inc(o_read, 1)

                exponentials(0, 0)
                with act.Fori(0, BATCH - 1) as s:
                    sentence(s, False)
                sentence(BATCH - 1, True)

            @block.tensor
            def _(pe):
                pe.sem_inc(o_read, 1)
                pe.sem_inc(exp_done, 2)

                def scores(s, m):
                    pe.wait_ge(key_ready, s * KT + (m + 1))
                    before = {0: 2, 1: 2}.get(m, 3)
                    pe.wait_ge(exp_done, s * KT + (m - before + 3))
                    pe.sem_inc(go, 1)
                    for a in range(0, width(m), 512):
                        b = min(a + 512, width(m))
                        last = nc.tensor.matmul(s_ps[m % 3][:, a:b], key[:, m], q[:, bass.ds(s * SEQ + a, b - a)],
                                                start=True, stop=True)
                    last.then_inc(s_done, 1)

                def mix(s, m):
                    if m == 0:
                        pe.wait_ge(o_read, s + 1)
                    pe.wait_ge(v_ready, s * KT + (m + 1))
                    for a in range(2):
                        n = min(width(m) - a * 512, 512)
                        if n > 0:
                            last = nc.tensor.matmul(o_ps[:, a, 0:n], value[:, m], e[:, m, a * 512:a * 512 + n],
                                                    start=(m == 0), stop=(m == KT - 1))
                    return last

                def sentence(s, last):
                    for m in range(2, KT):
                        scores(s, m)
                        mix(s, m - 2)
                    for m in range(2):
                        if not last:
                            scores(s + 1, m)
                        end = mix(s, KT - 2 + m)
                    end.then_inc(o_done, 1)

                scores(0, 0)
                scores(0, 1)
                with pe.Fori(0, BATCH - 1) as s:
                    sentence(s, False)
                sentence(BATCH - 1, True)

            @block.vector
            def _(dve):
                def maxima(s, m):
                    done = Done(step, s * (2 * KT) + 2 * m)
                    lo = m * P
                    dve.wait_ge(s_done, s * KT + (m + 1))
                    cut = slice(0, SEQ) if m == 0 else slice(lo, lo + P)
                    done.add(nc.vector.tensor_tensor(s_ps[m % 3][:, cut], s_ps[m % 3][:, cut], mask[:, 0:cut.stop - cut.start], ALU.add))
                    done.wait(dve)
                    done.add(nc.vector.tensor_reduce(peak[:, m:m + 1], s_ps[m % 3][:, 0:width(m)], AX.X, ALU.max))
                    done.wait(dve)
                    nc.vector.tensor_scalar_mul(peak[:, m:m + 1], peak[:, m:m + 1], -(D ** -0.5)).then_inc(peak_ready, 1)

                def divide(s, m):
                    dve.wait_ge(exp_done, s * KT + (m + 3))
                    nc.vector.reciprocal(total[:, m:m + 1], total[:, m:m + 1]).then_inc(divided, 1)
                    dve.wait_ge(divided, s * KT + (m + 1))
                    nc.vector.tensor_scalar(value[:, m], v[:, bass.ds(s, 1), m].squeeze(1),
                                            total[:, m:m + 1], None, ALU.mult).then_inc(v_ready, 1)

                def sentence(s, last):
                    for m in range(1, KT):
                        maxima(s, m)
                        divide(s, m - 1)
                    if not last:
                        maxima(s + 1, 0)
                    divide(s, KT - 1)

                dve.wait_ge(masked, 2)
                maxima(0, 0)
                with dve.Fori(0, BATCH - 1) as s:
                    sentence(s, False)
                sentence(BATCH - 1, True)


class Constants:

    def __init__(self, nc, whole):
        def sb(name, shape, dt=F32):
            return whole.enter_context(nc.sbuf_tensor(name, shape, dt))

        self.whole, self.stages, self.used = whole, 0, []
        self.ident, self.ident_b = sb("ident", [P, P]), sb("ident_b", [P, P], BF16)
        self.upper, self.upper_b = sb("upper", [P, P]), sb("upper_b", [P, P], BF16)
        self.zeros, self.ones = sb("zeros", [P, P]), sb("ones", [P, P])
        self.iota_i, self.iota_b = sb("iota_i", [P, P], I32), sb("iota_b", [P, P], BF16)
        self.part_i, self.part_f = sb("part_i", [P, 2], I32), sb("part_f", [P, 2])


def store_nodes(nc, c, h, out):
    with Stage(nc, c) as ctx, nc.Block() as block:
        stored = ctx.sem("stored")

        @block.sync
        def _(sp):
            sp.dma_start(out.rearrange("(p t) d -> p t d", p=P), h[:, :, :]).then_inc(stored, 16)
            sp.wait_ge(stored, 16)


def token_features(nc, c, w, h, sender):
    with Stage(nc, c) as s:
        tab_h, tab_x, tab_xt = s.sb("tab_h", [P, 2, D]), s.sb("tab_x", [P, 2, D]), s.sb("tab_xt", [D + 1, VOCAB])
        words, chosen = s.sb("words", [P, NODES]), s.sb("chosen", [P, SEQ])
        chosen_table, plain_table = s.sb("chosen_table", [P, 2, BATCH, D]), s.sb("plain_table", [P, 2, D])
        token_tables(nc, c, w, tab_h, tab_x, tab_xt)
        load_words(nc, c, w, words, chosen, meanwhile=sender.share(2))
        word_attention(nc, c, w, h, tab_h, tab_x, tab_xt, words, chosen, chosen_table, plain_table,
                       meanwhile=sender.share(20))
        with Stage(nc, c) as t:
            node_t = t.sb("node_t", [D, NODES])
            look_up(nc, c, words, chosen, chosen_table, plain_table, node_t, meanwhile=sender.share(4))
            to_nodes(nc, c, node_t[:, :], h, False, meanwhile=sender.share(2))


def build_tower(nc, w, out):
    def dram(name, shape, dt=F32):
        return nc.dram_tensor(name, shape, dt).ap()

    sorted_src, start_rows = dram("sorted_src", (SLOTS, 1), I32), dram("start_rows", (SLOTS, 1 + GH))
    source_rows, slot_rows = dram("source_rows", (NODES, ROW)), dram("slot_rows", (SLOTS, OUT))
    with ExitStack() as whole:
        c = Constants(nc, whole)
        h = whole.enter_context(nc.sbuf_tensor("h", [P, TILES, D], F32))
        start_i = whole.enter_context(nc.sbuf_tensor("start_i", [P, TILES], I32))
        end_i = whole.enter_context(nc.sbuf_tensor("end_i", [P, TILES], I32))
        make_constants(nc, c)
        with Stage(nc, c) as s:
            x_t = s.sb("x_t", [D, TILES, P])
            gates = s.sb("gates", [P, TILES, GE])
            has_none, last_rows = s.sb("has_none", [P, 1]), s.sb("last_rows", [P, OUT])
            with Stage(nc, c) as t:
                sender = Sender(nc, t, s, sorted_src)
                sort_edges(nc, c, w["edges"], sorted_src, start_rows, start_i, end_i, sender, 30)
                token_features(nc, c, w, h, sender)
                proj = t.sb("proj", [P, TILES, GF])
                norm_project(nc, c, h, x_t, w["gat_w"], proj, meanwhile=sender.share(2))
                send_nodes(nc, c, w, proj, start_i, source_rows, start_rows, sender)
            with Stage(nc, c) as t:
                y = t.sb("y", [P, TILES, GE, D])
                with Stage(nc, c) as u:
                    not_first, minus_low = u.sb("not_first", [P, SCOLS]), u.sb("minus_low", [P, SCOLS])
                    dst_term = u.sb("dst_term", [P, GH, SCOLS])
                    ids = u.sb("ids", [P, SCOLS + 2 * SC], I32)
                    spread_heads(nc, c, sender, sorted_src, start_rows, ids[:, 0:SCOLS],
                                 y[:, :, :, :].rearrange("p t e d -> p (t e d)"), not_first, minus_low, dst_term, has_none)
                    aggregate(nc, c, w, ids, source_rows, not_first, minus_low, dst_term, slot_rows, last_rows, x_t, y)
                finish_graph(nc, c, w, end_i, start_i, slot_rows, last_rows, has_none, gates)
                mix_experts(nc, c, y, gates, h)

        clear_semaphores(nc, c)
        with Stage(nc, c) as s:
            x_t, out_t = s.sb("x_t", [D, TILES, P]), s.sb("out_t", [D, NODES])
            norm_project(nc, c, h, x_t, None, None)
            with Stage(nc, c) as t:
                q, k = t.sb("q", [D, NODES]), t.sb("k", [D, NODES])
                v = t.sb("v", [P, BATCH, SEQ // P, D])
                project_columns(nc, c, w, x_t, q, k, v)
                column_attention(nc, c, q, k, v, out_t)
            to_nodes(nc, c, out_t[:, :], h, True)
        with Stage(nc, c) as s:
            x_t, gates = s.sb("x_t", [D, TILES, P]), s.sb("gates", [P, TILES, EXPERTS])
            logits = s.sb("logits", [P, TILES, EXPERTS])
            norm_project(nc, c, h, x_t, w["router_t"], logits, add_back=True)
            route(nc, c, logits, gates)
            experts(nc, c, x_t, gates, h, w["moe_w1"], w["moe_b1"], w["moe_w2"], w["moe_b2"])
        store_nodes(nc, c, h, out)


def kernel(**inputs):
    import numpy as np
    import concourse.bacc as bacc
    from concourse.bass_utils import run_bass_kernel_spmd as run

    a = {name: np.asarray(value) for name, value in inputs.items()}

    def with_bias(weight, bias):
        return np.concatenate([weight.T, bias[None]], 0)

    def pair_blocks(w2):
        pairs = w2.reshape(EXPERTS // 2, 2, D, D)
        out = np.zeros((2, D, EXPERTS // 2, 2, D), w2.dtype)
        for j in range(2):
            out[j, :, :, j, :] = pairs[:, j].transpose(1, 0, 2)
        return out.reshape(2 * D, EXPERTS // 2, 2 * D)

    arrays = {
        "tokens": a["x"].reshape(-1),
        "a2a": a["L0_attn_a2a"],
        "emb_t": a["L0_tok_emb_table"].T,
        "tok_w1_t": a["L0_tok_W1"][:, :D].T,
        "tok_b1": a["L0_tok_b1"][:, None],
        "tok_w2_t": with_bias(a["L0_tok_W2"], a["L0_tok_b2"]),
        "tok_gamma": a["L0_tok_gamma"],
        "tok_beta": a["L0_tok_beta"],
        "wq_t": a["L0_attn_wq"].T,
        "wv_t": a["L0_attn_wv"].T,
        "wk_pairs": a["L0_attn_wk"].reshape(HEADS0 // 2, 2 * D).T,
        "fan_t": a["L0_attn_fanout_w"].T,
        "edges": a["L0_ffn_edge_index"],
        "gat_w": a["L0_ffn_W_gat"],
        "att_src": a["L0_ffn_att_src"].reshape(-1),
        "att_dst": a["L0_ffn_att_dst"].reshape(-1),
        "gat_b": a["L0_ffn_b_gat"],
        "ln_gamma": a["L0_ffn_ln_gamma"],
        "ln_beta": a["L0_ffn_ln_beta"],
        "ffn_w1": a["L0_ffn_W1"].transpose(1, 0, 2),
        "ffn_b1": a["L0_ffn_b1"].T,
        "ffn_w2": a["L0_ffn_W2"].transpose(1, 0, 2),
        "ffn_b2": a["L0_ffn_b2"],
        "l1_wq_t": a["L1_attn_Wq"].T,
        "l1_wk_t": a["L1_attn_Wk"].T,
        "l1_wv_t": a["L1_attn_Wv"].T,
        "router_t": a["L1_ffn_router_w"].T,
        "moe_w1": a["L1_ffn_w1"].reshape(EXPERTS // 2, 2, D, D).transpose(2, 0, 1, 3).reshape(D, EXPERTS // 2, 2 * D),
        "moe_b1": a["L1_ffn_b1"].reshape(EXPERTS // 2, 2 * D).T,
        "moe_w2": pair_blocks(a["L1_ffn_w2"]),
        "moe_b2": a["L1_ffn_b2"],
    }
    arrays = {name: np.ascontiguousarray(value) for name, value in arrays.items()}
    nc = bacc.Bacc("TRN2", target_bir_lowering=False, num_devices=1)
    w = {name: nc.dram_tensor("in_" + name, value.shape, mybir.dt.from_np(value.dtype), kind="ExternalInput").ap()
         for name, value in arrays.items()}
    out = nc.dram_tensor("out", (NODES, D), F32, kind="ExternalOutput").ap()
    build_tower(nc, w, out)
    r = run(nc, [{"in_" + name: value for name, value in arrays.items()}], core_ids=[0])
    return r.results[0]["out"].reshape(BATCH, SEQ, D)
```
